# Optimizing a Trainium2 kernel written in Bass

```python
import numpy as np
import jax
import jax.numpy as jnp

def _softmax(x, axis=-1):
    return jax.nn.softmax(x, axis=axis)

def _gelu(x):
    return jax.nn.gelu(x, approximate=True)

def _silu(x):
    return jax.nn.silu(x)

def _sigmoid(x):
    return jax.nn.sigmoid(x)

def _layernorm(x, axis=-1, eps=1e-05):
    m = jnp.mean(x, axis=axis, keepdims=True)
    v = jnp.var(x, axis=axis, keepdims=True)
    return (x - m) / jnp.sqrt(v + eps)

def _scatter_add(tgt, idx, src, axis=0):
    return tgt.at[idx].add(src)

def _segment_sum(src, seg, n):
    return jax.ops.segment_sum(src, seg, n)
kernel_name = 'mk_gnn_ffn_d2_gnn_r8_1d9f0d'

def setup_inputs(seed: int=0):
    np.random.seed(seed)
    _w = jnp.asarray

    def _rec_inputs():
        import jax
        import jax.numpy as jnp
        _gk = jax.random.key(seed)
        x = -0.0003713 + 1 * jax.random.normal(jax.random.fold_in(_gk, 1), (6250, 256), jnp.float32)
        src = jax.random.randint(jax.random.fold_in(_gk, 2), (100000,), 0, 6250, jnp.int32)
        dst = jax.random.randint(jax.random.fold_in(_gk, 3), (100000,), 0, 6250, jnp.int32)
        _o = jnp.argsort(dst, stable=True)
        src = src[_o]
        dst = dst[_o]
        return (x, src, dst)
    x, src, dst = _rec_inputs()

    def _L0_gnn_setup():
        import jax, jax.numpy as jnp
        import numpy as np
        N_NODES = 6250

        def _gcn_conv(x, edge_index, W, b):
            n = x.shape[0]
            loop = jnp.arange(n, dtype=edge_index.dtype)
            src = jnp.concatenate([edge_index[0], loop])
            dst = jnp.concatenate([edge_index[1], loop])
            h = x @ W
            deg = jax.ops.segment_sum(jnp.ones_like(dst, dtype=h.dtype), dst, num_segments=n)
            dinv = jnp.where(deg > 0, jax.lax.rsqrt(deg), 0.0)
            norm = dinv[src] * dinv[dst]
            msg = h[src] * norm[:, None]
            out = jax.ops.segment_sum(msg, dst, num_segments=n)
            return out + b
        key = jax.random.key(seed)
        k1, k2, k3, k4 = jax.random.split(key, 4)
        in_c, hid = (256, 128)
        x = jax.random.normal(k1, (N_NODES, in_c), dtype=jnp.float32)
        edge_index = jax.random.randint(k2, (2, 100000), 0, N_NODES, dtype=jnp.int32)
        W_conv = jax.random.normal(k3, (in_c, hid), dtype=jnp.float32) * (1.0 / np.sqrt(in_c))
        b_conv = jnp.zeros((hid,), dtype=jnp.float32)
        limit = np.sqrt(6.0 / (hid + in_c))
        W_lin = jax.random.uniform(k4, (hid, in_c), dtype=jnp.float32, minval=-limit, maxval=limit)
        b_lin = jnp.zeros((in_c,), dtype=jnp.float32)
        return {'x': x, 'edge_index': edge_index, 'W_conv': W_conv, 'b_conv': b_conv, 'W_lin': W_lin, 'b_lin': b_lin}
    _L0_gnn_all = _L0_gnn_setup()
    _L0_gnn_in = {k: v for k, v in _L0_gnn_all.items() if k in ('W_conv', 'b_conv', 'W_lin', 'b_lin')}
    del _L0_gnn_all

    def _L0_ffn_setup():
        import jax, jax.numpy as jnp
        import numpy as np
        B, K, D = (512, 16, 256)
        E = 32
        H = int(D * 0.25)
        key = jax.random.key(seed)
        ks = jax.random.split(key, 7)
        d_rs = D ** (-0.5)
        h_rs = H ** (-0.5)
        x = jax.random.normal(ks[0], (B, K, D), dtype=jnp.float32)
        router_w = jax.random.uniform(ks[1], (E, D), jnp.float32, -d_rs, d_rs)
        router_b = jax.random.uniform(ks[2], (E,), jnp.float32, -d_rs, d_rs)
        W1 = jax.random.uniform(ks[3], (E, D, H), jnp.float32, -h_rs, h_rs)
        b1 = jax.random.uniform(ks[4], (E, H), jnp.float32, -h_rs, h_rs)
        W2 = jax.random.uniform(ks[5], (E, H, D), jnp.float32, -d_rs, d_rs)
        b2 = jax.random.uniform(ks[6], (E, D), jnp.float32, -d_rs, d_rs)
        return {'x': x, 'router_w': router_w, 'router_b': router_b, 'W1': W1, 'b1': b1, 'W2': W2, 'b2': b2}
    _L0_ffn_all = _L0_ffn_setup()
    _L0_ffn_in = {k: v for k, v in _L0_ffn_all.items() if k in ('router_w', 'router_b', 'W1', 'b1', 'W2', 'b2')}
    del _L0_ffn_all

    def _L1_gnn_setup():
        import jax, jax.numpy as jnp
        import numpy as np
        N_NODES = 6250
        D = 256
        L = 2
        N_EDGES = 100000
        NEG_SLOPE = 0.2

        def _gat_conv(h, W_l, al, ar, b, src, dst, n):
            hp = h @ W_l
            el = hp @ al
            er = hp @ ar
            e = jax.nn.leaky_relu(el[src] + er[dst], NEG_SLOPE)
            emax = jax.ops.segment_max(e, dst, num_segments=n)
            ex = jnp.exp(e - emax[dst])
            denom = jax.ops.segment_sum(ex, dst, num_segments=n)
            alpha = ex / denom[dst]
            out = jax.ops.segment_sum(hp[src] * alpha[:, None], dst, num_segments=n)
            return out + b
        key = jax.random.key(seed)
        ks = jax.random.split(key, 8)
        x = jax.random.normal(ks[0], (N_NODES, D), dtype=jnp.float32)
        W = jax.random.normal(ks[1], (L, D, D), dtype=jnp.float32) * (1.0 / np.sqrt(D))
        attn_l = jax.random.normal(ks[2], (L, D), dtype=jnp.float32) * (1.0 / np.sqrt(D))
        attn_r = jax.random.normal(ks[3], (L, D), dtype=jnp.float32) * (1.0 / np.sqrt(D))
        bias = jnp.zeros((L, D), dtype=jnp.float32)
        src = jax.random.randint(ks[4], (N_EDGES,), 0, N_NODES, dtype=jnp.int32)
        dst = jax.random.randint(ks[5], (N_EDGES,), 0, N_NODES, dtype=jnp.int32)
        return {'x': x, 'W': W, 'attn_l': attn_l, 'attn_r': attn_r, 'bias': bias, 'src': src, 'dst': dst}
    _L1_gnn_all = _L1_gnn_setup()
    _L1_gnn_in = {k: v for k, v in _L1_gnn_all.items() if k in ('W', 'attn_l', 'attn_r', 'bias')}
    del _L1_gnn_all

    def _L1_ffn_setup():
        import jax, jax.numpy as jnp
        import numpy as np
        B, N, D = (16, 512, 256)
        NUM_EXPERTS, TOP_K, HEADS = (4, 2, 4)
        N_EDGES = 131072
        LN_EPS = 1e-05

        def _layernorm(x, g, b):
            mu = x.mean(-1, keepdims=True)
            var = ((x - mu) ** 2).mean(-1, keepdims=True)
            return (x - mu) * jax.lax.rsqrt(var + LN_EPS) * g + b

        def _forward(x, edge_index, W_gat, att_src, att_dst, b_gat, ln_gamma, ln_beta, W1, b1, W2, b2):
            Bc, Nc, Dc = x.shape
            M = Bc * Nc
            x_flat = x.reshape(M, Dc)
            h = (x_flat @ W_gat).reshape(M, HEADS, NUM_EXPERTS)
            loops = jnp.arange(M, dtype=edge_index.dtype)
            src = jnp.concatenate([edge_index[0], loops])
            dst = jnp.concatenate([edge_index[1], loops])
            a_src = (h * att_src).sum(-1)
            a_dst = (h * att_dst).sum(-1)
            e = jax.nn.leaky_relu(a_src[src] + a_dst[dst], negative_slope=0.2)
            e_max = jax.ops.segment_max(e, dst, num_segments=M)
            ee = jnp.exp(e - e_max[dst])
            denom = jax.ops.segment_sum(ee, dst, num_segments=M)
            alpha = ee / (denom[dst] + 1e-16)
            msg = h[src] * alpha[:, :, None]
            agg = jax.ops.segment_sum(msg, dst, num_segments=M).reshape(M, HEADS * NUM_EXPERTS) + b_gat
            scores = _layernorm(agg, ln_gamma, ln_beta).reshape(M, HEADS, NUM_EXPERTS).mean(1)
            scores = scores.reshape(Bc, Nc, NUM_EXPERTS)
            topk_s, topk_i = jax.lax.top_k(scores, TOP_K)
            w = jax.nn.softmax(topk_s, axis=-1)
            out = jnp.zeros_like(x)
            for ei in range(NUM_EXPERTS):
                g = jnp.where(topk_i == ei, w, 0.0).sum(-1)
                hh = jax.nn.gelu(x @ W1[ei] + b1[ei], approximate=False)
                out = out + g[..., None] * (hh @ W2[ei] + b2[ei])
            return out
        key = jax.random.key(seed)
        ks = jax.random.split(key, 8)
        s = 0.05
        return {'x': jax.random.normal(ks[0], (B, N, D), jnp.float32), 'W_gat': jax.random.normal(ks[1], (D, HEADS * NUM_EXPERTS), jnp.float32) * s, 'att_src': jax.random.normal(ks[2], (HEADS, NUM_EXPERTS), jnp.float32) * s, 'att_dst': jax.random.normal(ks[3], (HEADS, NUM_EXPERTS), jnp.float32) * s, 'b_gat': jnp.zeros((HEADS * NUM_EXPERTS,), jnp.float32), 'ln_gamma': jnp.ones((HEADS * NUM_EXPERTS,), jnp.float32), 'ln_beta': jnp.zeros((HEADS * NUM_EXPERTS,), jnp.float32), 'W1': jax.random.normal(ks[4], (NUM_EXPERTS, D, 2 * D), jnp.float32) * s, 'b1': jnp.zeros((NUM_EXPERTS, 2 * D), jnp.float32), 'W2': jax.random.normal(ks[5], (NUM_EXPERTS, 2 * D, D), jnp.float32) * s, 'b2': jnp.zeros((NUM_EXPERTS, D), jnp.float32), 'edge_index': jax.random.randint(ks[6], (2, N_EDGES), 0, B * N, jnp.int32)}
    _L1_ffn_all = _L1_ffn_setup()
    _L1_ffn_in = {k: v for k, v in _L1_ffn_all.items() if k in ('W_gat', 'att_src', 'att_dst', 'b_gat', 'ln_gamma', 'ln_beta', 'W1', 'b1', 'W2', 'b2', 'edge_index')}
    del _L1_ffn_all
    return {'x': x, 'src': src, 'dst': dst, 'L0_gnn_W_conv': _L0_gnn_in['W_conv'], 'L0_gnn_b_conv': _L0_gnn_in['b_conv'], 'L0_gnn_W_lin': _L0_gnn_in['W_lin'], 'L0_gnn_b_lin': _L0_gnn_in['b_lin'], 'L0_ffn_router_w': _L0_ffn_in['router_w'], 'L0_ffn_router_b': _L0_ffn_in['router_b'], 'L0_ffn_W1': _L0_ffn_in['W1'], 'L0_ffn_b1': _L0_ffn_in['b1'], 'L0_ffn_W2': _L0_ffn_in['W2'], 'L0_ffn_b2': _L0_ffn_in['b2'], 'L1_gnn_W': _L1_gnn_in['W'], 'L1_gnn_attn_l': _L1_gnn_in['attn_l'], 'L1_gnn_attn_r': _L1_gnn_in['attn_r'], 'L1_gnn_bias': _L1_gnn_in['bias'], 'L1_ffn_W_gat': _L1_ffn_in['W_gat'], 'L1_ffn_att_src': _L1_ffn_in['att_src'], 'L1_ffn_att_dst': _L1_ffn_in['att_dst'], 'L1_ffn_b_gat': _L1_ffn_in['b_gat'], 'L1_ffn_ln_gamma': _L1_ffn_in['ln_gamma'], 'L1_ffn_ln_beta': _L1_ffn_in['ln_beta'], 'L1_ffn_W1': _L1_ffn_in['W1'], 'L1_ffn_b1': _L1_ffn_in['b1'], 'L1_ffn_W2': _L1_ffn_in['W2'], 'L1_ffn_b2': _L1_ffn_in['b2'], 'L1_ffn_edge_index': _L1_ffn_in['edge_index']}

def reference(x, src, dst, L0_gnn_W_conv, L0_gnn_b_conv, L0_gnn_W_lin, L0_gnn_b_lin, L0_ffn_router_w, L0_ffn_router_b, L0_ffn_W1, L0_ffn_b1, L0_ffn_W2, L0_ffn_b2, L1_gnn_W, L1_gnn_attn_l, L1_gnn_attn_r, L1_gnn_bias, L1_ffn_W_gat, L1_ffn_att_src, L1_ffn_att_dst, L1_ffn_b_gat, L1_ffn_ln_gamma, L1_ffn_ln_beta, L1_ffn_W1, L1_ffn_b1, L1_ffn_W2, L1_ffn_b2, L1_ffn_edge_index):
    import jax
    import jax.numpy as jnp

    def _L0_gnn_ref(x, edge_index, W_conv, b_conv, W_lin, b_lin):
        import jax, jax.numpy as jnp
        import numpy as np
        N_NODES = 6250

        def _gcn_conv(x, edge_index, W, b):
            n = x.shape[0]
            loop = jnp.arange(n, dtype=edge_index.dtype)
            src = jnp.concatenate([edge_index[0], loop])
            dst = jnp.concatenate([edge_index[1], loop])
            h = x @ W
            deg = jax.ops.segment_sum(jnp.ones_like(dst, dtype=h.dtype), dst, num_segments=n)
            dinv = jnp.where(deg > 0, jax.lax.rsqrt(deg), 0.0)
            norm = dinv[src] * dinv[dst]
            msg = h[src] * norm[:, None]
            out = jax.ops.segment_sum(msg, dst, num_segments=n)
            return out + b
        h = _gcn_conv(x, edge_index, W_conv, b_conv)
        return h @ W_lin + b_lin

    def _L0_ffn_ref(x, router_w, router_b, W1, b1, W2, b2):
        import jax, jax.numpy as jnp
        import numpy as np
        B, K, D = (512, 16, 256)
        E = 32
        H = int(D * 0.25)
        xf = x.reshape(-1, D)
        logits = xf @ router_w.T + router_b
        idx = jnp.argmax(logits, axis=-1)
        w1t = jnp.take(W1, idx, axis=0)
        h = jnp.einsum('nd,ndh->nh', xf, w1t) + jnp.take(b1, idx, axis=0)
        h = jax.nn.relu(h)
        w2t = jnp.take(W2, idx, axis=0)
        out = jnp.einsum('nh,nhd->nd', h, w2t) + jnp.take(b2, idx, axis=0)
        out = jax.nn.relu(out)
        return out.reshape(x.shape)

    def _L1_gnn_ref(x, W, attn_l, attn_r, bias, src, dst):
        import jax, jax.numpy as jnp
        import numpy as np
        N_NODES = 6250
        D = 256
        L = 2
        N_EDGES = 100000
        NEG_SLOPE = 0.2

        def _gat_conv(h, W_l, al, ar, b, src, dst, n):
            hp = h @ W_l
            el = hp @ al
            er = hp @ ar
            e = jax.nn.leaky_relu(el[src] + er[dst], NEG_SLOPE)
            emax = jax.ops.segment_max(e, dst, num_segments=n)
            ex = jnp.exp(e - emax[dst])
            denom = jax.ops.segment_sum(ex, dst, num_segments=n)
            alpha = ex / denom[dst]
            out = jax.ops.segment_sum(hp[src] * alpha[:, None], dst, num_segments=n)
            return out + b
        n = x.shape[0]
        loops = jnp.arange(n, dtype=src.dtype)
        src_sl = jnp.concatenate([src, loops])
        dst_sl = jnp.concatenate([dst, loops])
        h = x
        n_layers = W.shape[0]
        for i in range(n_layers):
            h = _gat_conv(h, W[i], attn_l[i], attn_r[i], bias[i], src_sl, dst_sl, n)
            if i < n_layers - 1:
                h = jax.nn.relu(h)
        return h

    def _L1_ffn_ref(x, W_gat, att_src, att_dst, b_gat, ln_gamma, ln_beta, W1, b1, W2, b2, edge_index):
        import jax, jax.numpy as jnp
        import numpy as np
        B, N, D = (16, 512, 256)
        NUM_EXPERTS, TOP_K, HEADS = (4, 2, 4)
        N_EDGES = 131072
        LN_EPS = 1e-05

        def _layernorm(x, g, b):
            mu = x.mean(-1, keepdims=True)
            var = ((x - mu) ** 2).mean(-1, keepdims=True)
            return (x - mu) * jax.lax.rsqrt(var + LN_EPS) * g + b

        def _forward(x, edge_index, W_gat, att_src, att_dst, b_gat, ln_gamma, ln_beta, W1, b1, W2, b2):
            Bc, Nc, Dc = x.shape
            M = Bc * Nc
            x_flat = x.reshape(M, Dc)
            h = (x_flat @ W_gat).reshape(M, HEADS, NUM_EXPERTS)
            loops = jnp.arange(M, dtype=edge_index.dtype)
            src = jnp.concatenate([edge_index[0], loops])
            dst = jnp.concatenate([edge_index[1], loops])
            a_src = (h * att_src).sum(-1)
            a_dst = (h * att_dst).sum(-1)
            e = jax.nn.leaky_relu(a_src[src] + a_dst[dst], negative_slope=0.2)
            e_max = jax.ops.segment_max(e, dst, num_segments=M)
            ee = jnp.exp(e - e_max[dst])
            denom = jax.ops.segment_sum(ee, dst, num_segments=M)
            alpha = ee / (denom[dst] + 1e-16)
            msg = h[src] * alpha[:, :, None]
            agg = jax.ops.segment_sum(msg, dst, num_segments=M).reshape(M, HEADS * NUM_EXPERTS) + b_gat
            scores = _layernorm(agg, ln_gamma, ln_beta).reshape(M, HEADS, NUM_EXPERTS).mean(1)
            scores = scores.reshape(Bc, Nc, NUM_EXPERTS)
            topk_s, topk_i = jax.lax.top_k(scores, TOP_K)
            w = jax.nn.softmax(topk_s, axis=-1)
            out = jnp.zeros_like(x)
            for ei in range(NUM_EXPERTS):
                g = jnp.where(topk_i == ei, w, 0.0).sum(-1)
                hh = jax.nn.gelu(x @ W1[ei] + b1[ei], approximate=False)
                out = out + g[..., None] * (hh @ W2[ei] + b2[ei])
            return out
        return _forward(x, edge_index, W_gat, att_src, att_dst, b_gat, ln_gamma, ln_beta, W1, b1, W2, b2)
    edge_index = jnp.stack([src, dst])
    x = x + _L0_gnn_ref(_layernorm(x, axis=-1), edge_index, L0_gnn_W_conv, L0_gnn_b_conv, L0_gnn_W_lin, L0_gnn_b_lin)
    x = x + _L0_ffn_ref(_layernorm(x, axis=-1)[None], L0_ffn_router_w, L0_ffn_router_b, L0_ffn_W1, L0_ffn_b1, L0_ffn_W2, L0_ffn_b2)[0]
    x = x + _L1_gnn_ref(_layernorm(x, axis=-1), L1_gnn_W, L1_gnn_attn_l, L1_gnn_attn_r, L1_gnn_bias, src, dst)
    x = x + _L1_ffn_ref(_layernorm(x, axis=-1)[None], L1_ffn_W_gat, L1_ffn_att_src, L1_ffn_att_dst, L1_ffn_b_gat, L1_ffn_ln_gamma, L1_ffn_ln_beta, L1_ffn_W1, L1_ffn_b1, L1_ffn_W2, L1_ffn_b2, L1_ffn_edge_index)[0]
    return x

_drawn_inputs = setup_inputs


def setup_inputs(seed=0):
    import zlib

    import numpy as np

    out = dict(_drawn_inputs(seed))
    spreads = {'L0_gnn_b_conv': (0.0, 0.1),
     'L0_gnn_b_lin': (0.0, 0.1),
     'L1_gnn_bias': (0.0, 0.1),
     'L1_ffn_b_gat': (0.0, 0.1),
     'L1_ffn_ln_gamma': (1.0, 0.2),
     'L1_ffn_ln_beta': (0.0, 0.1),
     'L1_ffn_b1': (0.0, 0.1),
     'L1_ffn_b2': (0.0, 0.1)}
    factors = {'L0_ffn_b1': 3.382, 'L1_gnn_attn_r': 3.808, 'L1_ffn_att_dst': 4.117}
    for name, (base, spread) in spreads.items():
        noise = np.random.default_rng([zlib.crc32(name.encode()), seed]).standard_normal(out[name].shape)
        drawn = base * np.exp(spread * noise) if base else spread * noise
        out[name] = jnp.asarray(drawn.astype(out[name].dtype))
    for name, factor in factors.items():
        out[name] = (out[name] * factor).astype(out[name].dtype)
    return out
```

```python
import numpy as np
from contextlib import ExitStack

import concourse.bass as bass
import concourse.mybir as mybir

P = 128
N_NODES = 6250
D = 256
NT = -(-N_NODES // P)
NPAD = NT * P
G = 7
NG = NT // G
HID = 128
EXPERTS, EH = 32, 64
FH = EXPERTS * EH
FT = FH // P
HEADS, NE = 4, 4
MH = 2 * D
E1, E2 = 100000, 131072
B = 32
SB = 13
MASK = (1 << SB) - 1
KEY1 = 0x40000000
KEY2 = KEY1 | 1 << (2 * SB)
LAST = 0x4FFFFFFF
SORT_BITS = 18
F = (1 << SORT_BITS) // P
C1 = B * -(-(E1 + NPAD) // (B * P))
C2 = B * -(-(E2 + NPAD) // (B * P))
FILL1 = C1 * P - E1 - NPAD
CH = C1 + C2
EP1 = 125
EF1, EF2 = E1 // EP1, E2 // P
WIN = NPAD + P
LOW = -1e30
EPS = 1e-5
GH = 16
POOL_GROUPS = 26
assert C1 * P + E2 + NPAD <= 1 << SORT_BITS and CH <= F and FILL1 % 2 == 0 and NT % G == 0
assert EF1 + EF2 + 2 * NT + 2 <= F and C1 // B % 2 == 0 and C2 // B % 2 == 0

F32 = mybir.dt.float32
BF16 = mybir.dt.bfloat16
I32 = mybir.dt.int32
I16 = mybir.dt.int16
U32 = mybir.dt.uint32
ALU = mybir.AluOpType
ACT = mybir.ActivationFunctionType
AX = mybir.AxisListType.X
EDVE = mybir.EngineType.DVE


class Memory:

    def __init__(self, nc, stack, stage):
        self.nc, self.stack, self.stage = nc, stack, stage
        self.sems = []
        if stage != "g":
            stack.callback(self.give_back)

    def sbuf(self, name, shape, dt=F32):
        return self.stack.enter_context(self.nc.sbuf_tensor(f"{self.stage}_{name}", shape, dt))

    def sem(self, name):
        s = self.nc.alloc_semaphore(name=f"{self.stage}_{name}")
        self.sems.append(s)
        return s

    def give_back(self):
        if not self.sems:
            return
        self.nc.clear_and_free_semaphores(self.sems)
        self.nc.all_engine_barrier()


def wait_alone(pool, g, sem, value):
    pool.wait_ge(sem, value)
    g.carried = g.carried % 8 + 1
    pool.tensor_tensor(g.carrier[:, g.carried:g.carried + 1], g.carrier[:, 0:1], g.carrier[:, 0:1], ALU.mult)


def sort_plan():
    fb = F.bit_length() - 1
    plan = []
    for k in range(1, SORT_BITS + 1):
        if k > fb:
            plan.append(("sign", k))
            plan.append(("flip",))
            for j in range(k - 1, fb - 1, -1):
                plan.append(("swap", None, j - fb, P))
            plan.append(("flip",))
        elif k == fb:
            plan.append(("sign", k))
        for j in range(min(k, fb) - 1, -1, -1):
            plan.append(("swap", k if k < fb else None, j, F))
    return plan


def swap_views(x, k, j, width):
    d = 1 << j
    if k is None:
        v = x.rearrange("p (a h d) -> p a h d", h=2, d=d)
        return [(v[:, :, 0, :], v[:, :, 1, :], True)]
    m = 1 << (k - j - 1)
    v = x.rearrange("p (a u m h d) -> p a u m h d", u=2, m=m, h=2, d=d)
    return [(v[:, :, u, :, 0, :], v[:, :, u, :, 1, :], u == 0) for u in (0, 1)]


def sort_edges(nc, io, g):
    with ExitStack() as stack:
        m = Memory(nc, stack, "sort")
        e1s, e1d = m.sbuf("e1s", [EP1, EF1], I32), m.sbuf("e1d", [EP1, EF1], I32)
        e2s, e2d = m.sbuf("e2s", [P, EF2], I32), m.sbuf("e2d", [P, EF2], I32)
        node = m.sbuf("node", [P, NT], I32)
        keys = [m.sbuf("keys_a", [P, F]), m.sbuf("keys_b", [P, F])]
        part = m.sbuf("part", [P, 1], I32)
        head = m.sbuf("head", [P, 1], I32)
        heads = m.sbuf("heads", [P, HEADS * NE + HEADS], I32)
        bits = m.sbuf("bits", [P, 9], I32)
        sign = m.sbuf("sign", [P, 9])
        flipsign = m.sbuf("flipsign", [P, 9])
        lo, hi = m.sbuf("lo", [EP1, EF1], I32), m.sbuf("hi", [EP1, EF1], I32)
        digit = m.sbuf("digit", [EP1, 2, 2, GH])
        oh_lo, oh_hi = m.sbuf("oh_lo", [EP1, 2, GH, P], BF16), m.sbuf("oh_hi", [EP1, 2, GH, NT], BF16)
        digit2 = m.sbuf("digit2", [EP1, 2, 2, GH])
        oh_lo2, oh_hi2 = m.sbuf("oh_lo2", [EP1, 2, GH, P], BF16), m.sbuf("oh_hi2", [EP1, 2, GH, NT], BF16)
        iotab = m.sbuf("iotab", [P, P], BF16)
        onehots2, counted2 = m.sem("onehots2"), m.sem("counted2")
        zero = m.sbuf("zero", [P, P], BF16)
        degree = m.sbuf("degree", [P, 3, NT])
        edges_in = m.sem("edges_in")
        made = m.sem("made")
        split = m.sem("split")
        step = m.sem("sort_step")
        flipped = m.sem("flipped")
        copied = m.sem("copied")
        onehots = m.sem("onehots")
        digits = m.sem("digits")
        counted = m.sem("counted")
        stored = m.sem("keys_stored")
        degree_sum, degree_done = m.sem("degree_sum"), m.sem("degree_done")
        plan = sort_plan()
        n_groups = EF1 // GH
        dve_groups = n_groups - POOL_GROUPS
        done = {}
        end = {}

        with nc.Block() as block:
            @block.gpsimd
            def _(pool):
                pool.memset(g.carrier[:, :], 1.0).then_inc(made, 1)
                pool.iota(node[:, :], [[1, NT]], base=0, channel_multiplier=NT).then_inc(made, 1)
                pool.iota(part[:, :], [[0, 1]], base=0, channel_multiplier=1).then_inc(made, 1)
                pool.iota(g.iota[:, :], [[1, P]], base=0, channel_multiplier=0, allow_small_or_imprecise_dtypes=True).then_inc(made, 1)
                pool.iota(g.pcol[:, :], [[P, 2]], base=0, channel_multiplier=1, allow_small_or_imprecise_dtypes=True).then_inc(made, 1)
                pool.memset(g.ones[:, :], 1.0).then_inc(made, 1)
                pool.memset(zero[:, :], 0.0).then_inc(made, 1)
                pool.memset(g.ident[:, :], 0.0).then_inc(made, 1)
                pool.memset(g.group[:, :], 1.0).then_inc(made, 1)
                pool.iota(heads[:, 0:HEADS * NE], [[1, HEADS], [0, NE]], base=0, channel_multiplier=0).then_inc(made, 1)
                pool.iota(heads[:, HEADS * NE:], [[1, HEADS]], base=0, channel_multiplier=0).then_inc(made, 1)
                pool.wait_ge(made, 11)
                pool.affine_select(out=g.ident[:, :], in_=g.ident[:, :], compare_op=ALU.not_equal, fill=1.0, base=0,
                                   pattern=[[-1, P]], channel_multiplier=1).then_inc(made, 1)
                pool.affine_select(out=g.group[:, :], in_=g.group[:, :], compare_op=ALU.is_ge, fill=0.0, base=0,
                                   pattern=[[-HEADS, B]], channel_multiplier=1).then_inc(made, 1)
                pool.wait_ge(made, 13)
                pool.affine_select(out=g.group[:, :], in_=g.group[:, :], compare_op=ALU.is_ge, fill=0.0, base=HEADS - 1,
                                   pattern=[[HEADS, B]], channel_multiplier=-1).then_inc(made, 1)
                pool.wait_ge(split, 2)
                with pool.Fori(0, POOL_GROUPS // 2) as it:
                    for s in (0, 1):
                        i = it * 2 + s
                        wait_alone(pool, g, counted, i + 2)
                        cols = bass.ds(i * GH, GH)
                        pool.tensor_copy(digit[:, s, 0, :], lo[:, cols]).then_inc(digits, 1)
                        pool.tensor_copy(digit[:, s, 1, :], hi[:, cols]).then_inc(digits, 1)
                        wait_alone(pool, g, digits, i * 2 + 2)
                        for q in range(GH):
                            pool.tensor_scalar(oh_lo[:, s, q, :], g.iota[0:EP1, :], digit[:, s, 0, q:q + 1], None, ALU.is_equal)
                            last = pool.tensor_scalar(oh_hi[:, s, q, :], g.iota[0:EP1, 0:NT], digit[:, s, 1, q:q + 1], None, ALU.is_equal)
                        last.then_inc(onehots, 1)

            @block.vector
            def _(dve):
                n = [0]

                def did(ins):
                    n[0] += 1
                    ins.then_inc(step, 1)

                def after():
                    dve.wait_ge(step, n[0])

                k0 = keys[0][:, :].bitcast(I32)
                did(dve.memset(k0, LAST))
                dve.wait_ge(edges_in, 4 * 16)
                dve.tensor_scalar(lo[:, :], e1d[:, :], P - 1, None, ALU.bitwise_and).then_inc(split, 1)
                dve.tensor_scalar(hi[:, :], e1d[:, :], 7, None, ALU.logical_shift_right).then_inc(split, 1)
                dve.wait_ge(made, 11)
                did(dve.tensor_copy(iotab[:, :], g.iota[:, :]))
                after()
                c = 0
                spans = []
                for s, d, rows, w, key in ((e1s, e1d, EP1, EF1, KEY1), (e2s, e2d, P, EF2, KEY2)):
                    did(dve.scalar_tensor_tensor(out=k0[0:rows, c:c + w], in0=d[:, :], scalar=SB, in1=s[:, :],
                                                 op0=ALU.logical_shift_left, op1=ALU.bitwise_or))
                    spans.append((rows, c, w, key))
                    c += w
                dve.wait_ge(made, 3)
                for key in (KEY1, KEY2):
                    did(dve.scalar_tensor_tensor(out=k0[:, c:c + NT], in0=node[:, :], scalar=SB, in1=node[:, :],
                                                 op0=ALU.logical_shift_left, op1=ALU.bitwise_or))
                    spans.append((P, c, NT, key))
                    c += NT
                did(dve.memset(k0[0:FILL1 // 2, c:c + 2], KEY1 | ((1 << 2 * SB) - 1)))
                after()
                for rows, c, w, key in spans:
                    did(dve.tensor_scalar(k0[0:rows, c:c + w], k0[0:rows, c:c + w], key, None, ALU.bitwise_or))
                for b in range(9):
                    did(dve.tensor_scalar(bits[:, b:b + 1], part[:, :], b, 1, ALU.logical_shift_right, ALU.bitwise_and))
                after()
                dve.wait_ge(made, 11)
                did(dve.tensor_scalar(head[:, :], part[:, :], HEADS - 1, None, ALU.bitwise_and))
                after()
                did(dve.tensor_tensor(g.select_router[:, :], heads[:, :], head[:, :].broadcast_to([P, HEADS * NE + HEADS]), ALU.is_equal))
                did(dve.tensor_scalar(sign[:, :], bits[:, :], -2.0, 1.0, ALU.mult, ALU.add))
                after()
                did(dve.tensor_tensor(flipsign[:, 1:9], sign[:, 0:8], sign[:, 1:9], ALU.mult))
                did(dve.tensor_copy(flipsign[:, 0:1], sign[:, 0:1]))
                after()
                at, flips = 0, 0
                fb = F.bit_length() - 1
                for i, s in enumerate(plan):
                    x, y = keys[at], keys[1 - at]
                    if s[0] == "swap":
                        _, k, j, width = s
                        for (xl, xh, up), (yl, yh, _) in zip(swap_views(x[:, :], k, j, width), swap_views(y[:, :], k, j, width)):
                            did(dve.tensor_tensor(yl, xl, xh, ALU.min if up else ALU.max))
                            did(dve.tensor_tensor(yh, xl, xh, ALU.max if up else ALU.min))
                    elif s[0] == "sign":
                        b = s[1] - fb
                        did(dve.tensor_scalar(y[:, :], x[:, :], flipsign[:, b:b + 1], None, ALU.mult))
                    else:
                        flips += 1
                        for q in (0, 1):
                            dve.wait_ge(flipped, 4 * (flips - 1) + q + 1)
                            did(dve.tensor_copy(y[:, q * 512:(q + 1) * 512], g.bank[q][:, :]))
                        dve.wait_ge(copied, 2 * flips)
                    after()
                    done[i] = n[0]
                    at = 1 - at
                end.update(at=at, total=n[0])
                with dve.Fori(0, dve_groups // 2) as it:
                    for t in (0, 1):
                        i = it * 2 + t
                        dve.wait_ge(counted2, i + 1)
                        cols = bass.ds((POOL_GROUPS + i) * GH, GH)
                        dve.tensor_copy(digit2[:, t, 0, :], lo[:, cols])
                        dve.tensor_copy(digit2[:, t, 1, :], hi[:, cols])
                        dve.drain()
                        for q in range(GH):
                            dve.tensor_scalar(oh_lo2[:, t, q, :], iotab[0:EP1, :], digit2[:, t, 0, q:q + 1], None, ALU.is_equal)
                            last = dve.tensor_scalar(oh_hi2[:, t, q, :], iotab[0:EP1, 0:NT], digit2[:, t, 1, q:q + 1], None, ALU.is_equal)
                        last.then_inc(onehots2, 1)
                dve.wait_ge(degree_sum, 1)
                dve.tensor_scalar(degree[:, 0, :], g.bank[7][:, 0:NT], 1.0, None, ALU.add).then_inc(degree_done, 1)
                dve.wait_ge(degree_done, 2)
                newton(dve, degree[:, 0, :], degree[:, 1, :], g.dinv[:, :], degree[:, 2, :])

            @block.tensor
            def _(pe):
                pe.wait_ge(made, 12)
                hist = g.bank[7][:, 0:NT]
                nc.tensor.matmul(hist, zero[:, :], zero[:, 0:NT], start=True, stop=False).then_inc(counted, 3)
                pe.nop().then_inc(counted2, 2)
                todo = [POOL_GROUPS // 2]

                def count_some(most):
                    now = min(most, todo[0])
                    if not now:
                        return
                    first = POOL_GROUPS // 2 - todo[0]
                    todo[0] -= now
                    with pe.Fori(first, first + now) as it:
                        for s in (0, 1):
                            i = it * 2 + s
                            pe.wait_ge(onehots, i + 1)
                            for q in range(GH):
                                last = nc.tensor.matmul(hist, oh_lo[:, s, q, :], oh_hi[:, s, q, :], start=False, stop=False)
                            last.then_inc(counted, 1)

                count_some(POOL_GROUPS // 4)
                flips = 0
                at = 0
                for i, s in enumerate(plan):
                    if s[0] == "flip":
                        pe.wait_ge(step, done[i - 1])
                        if flips:
                            pe.wait_ge(copied, 2 * flips)
                        for q in range(4):
                            for r in range(4):
                                c = (4 * q + r) * P
                                last = nc.tensor.transpose(g.bank[q][:, r * P:(r + 1) * P], keys[at][:, c:c + P], g.ident[:, :])
                            last.then_inc(flipped, 1)
                        flips += 1
                        if flips % 2 == 0:
                            count_some(1)
                    at = 1 - at
                count_some(n_groups)
                with pe.Fori(0, dve_groups // 2) as it:
                    for t in (0, 1):
                        i = it * 2 + t
                        pe.wait_ge(onehots2, i + 1)
                        for q in range(GH):
                            last = nc.tensor.matmul(hist, oh_lo2[:, t, q, :], oh_hi2[:, t, q, :], start=False, stop=False)
                        last.then_inc(counted2, 1)
                nc.tensor.matmul(hist, zero[:, :], zero[:, 0:NT], start=False, stop=True).then_inc(degree_sum, 1)

            @block.scalar
            def _(act):
                flips = 0
                at = 0
                for i, s in enumerate(plan):
                    if s[0] == "flip":
                        for q in (2, 3):
                            act.wait_ge(flipped, 4 * flips + q + 1)
                            act.activation(keys[1 - at][:, q * 512:(q + 1) * 512], g.bank[q][:, :], ACT.Copy).then_inc(copied, 1)
                        flips += 1
                    at = 1 - at
                act.wait_ge(degree_done, 1)
                act.activation(degree[:, 1, :], degree[:, 0, :], ACT.Sqrt).then_inc(degree_done, 1)

            @block.sync
            def _(sp):
                sp.dma_start(e1s[:, :], io["src"].rearrange("(p f) -> p f", p=EP1)).then_inc(edges_in, 16)
                sp.dma_start(e1d[:, :], io["dst"].rearrange("(p f) -> p f", p=EP1)).then_inc(edges_in, 16)
                sp.dma_start(e2s[:, :], io["edges"][0].rearrange("(p f) -> p f", p=P)).then_inc(edges_in, 16)
                sp.dma_start(e2d[:, :], io["edges"][1].rearrange("(p f) -> p f", p=P)).then_inc(edges_in, 16)
                sp.wait_ge(step, end["total"])
                sp.dma_start(io["keys"].rearrange("(p f) -> p f", p=P), keys[end["at"]][:, :].bitcast(I32)).then_inc(stored, 16)
                sp.wait_ge(stored, 16)


def index_edges(nc, io, g):
    with ExitStack() as stack:
        m = Memory(nc, stack, "index")
        rows = m.sbuf("nat", [P, F], I32)
        col = m.sbuf("col", [P, F], I32)
        tmp = m.sbuf("tmp", [P, F], I32)
        nodef = m.sbuf("nodef", [P, F])
        ends = m.sbuf("ends", [1, 2, F], I32)
        endf = m.sbuf("endf", [1, 2, F])
        crow = m.sbuf("crow", [B, CH // B, P], I32)
        base = m.sbuf("base", [B, CH // B, 1], I32)
        basef = m.sbuf("basef", [B, CH // B, 1])
        crowf = m.sbuf("crowf", [B, CH // B, P])
        placeb = m.sbuf("placeb", [B, CH // B, P], BF16)
        cont = m.sbuf("cont", [1, F])
        loaded, turned, s, stored = m.sem("loaded"), m.sem("turned"), m.sem("step"), m.sem("stored")
        spread, taken = m.sem("spread"), m.sem("taken")
        at = {}
        with nc.Block() as block:
            @block.vector
            def _(dve):
                n = [0]

                def did(ins):
                    n[0] += 1
                    ins.then_inc(s, 1)
                    dve.wait_ge(s, n[0])

                dve.wait_ge(loaded, 64)
                for q in range(4):
                    dve.wait_ge(turned, q + 1)
                    out = col[:, :].bitcast(F32).rearrange("e (p r) -> e r p", r=F // P)[:, 4 * q:4 * q + 4, :]
                    ins = dve.tensor_copy(out, g.bank[q][:, :].rearrange("e (r p) -> e r p", r=4))
                    ins.then_inc(taken, 1)
                dve.wait_ge(taken, 4)
                did(dve.tensor_scalar(tmp[:, :], col[:, :], MASK, None, ALU.bitwise_and))
                did(dve.tensor_scalar(g.src[:, :], tmp[:, 0:CH], float(N_NODES - 1), None, ALU.min))
                did(dve.tensor_scalar(tmp[:, :], col[:, :], SB, MASK, ALU.logical_shift_right, ALU.bitwise_and))
                did(dve.tensor_copy(nodef[:, :], tmp[:, :]))
                did(dve.tensor_scalar(ends[:, :, :], ends[:, :, :], SB, MASK, ALU.logical_shift_right, ALU.bitwise_and))
                did(dve.tensor_copy(endf[:, :, :], ends[:, :, :]))
                did(dve.memset(cont[:, 0:1], 0.0))
                did(dve.tensor_tensor(cont[:, 1:F], endf[:, 0, 1:F], endf[:, 1, 0:F - 1], ALU.is_equal))
                did(dve.memset(g.cont_low[:, 0:1], LOW))
                did(dve.tensor_tensor(endf[:, 0, 1:F], endf[:, 1, 1:F], endf[:, 1, 0:F - 1], ALU.not_equal))
                did(dve.tensor_scalar(g.same_low[:, 1:CH], endf[:, 0, 1:CH], LOW, None, ALU.mult))
                did(dve.memset(g.same_low[:, 0:1], LOW))
                did(dve.tensor_scalar(g.cont_low[:, 1:CH], cont[:, 1:CH], -LOW, LOW, ALU.mult, ALU.add))
                did(dve.tensor_scalar(g.base[:, :], ends[:, 0, 0:CH], float(NPAD), None, ALU.min))
                did(dve.tensor_copy(endf[:, 0, 0:CH], g.base[:, :]))
                did(dve.tensor_scalar(ends[:, 0, :], ends[:, 0, :], float(NPAD), None, ALU.min))
                did(dve.tensor_scalar(ends[:, 0, :], ends[:, 0, :], 7, None, ALU.logical_shift_right))
                did(dve.tensor_copy(g.tile[:, :], ends[:, 0, 0:CH]))
                at.update(flags=n[0])
                did(dve.tensor_scalar(crow[:, :, :], crow[:, :, :], SB, MASK, ALU.logical_shift_right, ALU.bitwise_and))
                did(dve.tensor_scalar(base[:, :, :], crow[:, :, 0:1], float(NPAD), None, ALU.min))
                did(dve.tensor_scalar(base[:, :, :], base[:, :, :], 7, 7, ALU.logical_shift_right, ALU.logical_shift_left))
                did(dve.tensor_copy(basef[:, :, :], base[:, :, :]))
                did(dve.tensor_copy(crowf[:, :, :], crow[:, :, :]))
                did(dve.tensor_tensor(placeb[:, :, :], crowf[:, :, :], basef[:, :, :].broadcast_to([B, CH // B, P]), ALU.subtract))
                at.update(place=n[0])
                for q in range(4):
                    w = min(512, CH - q * 512)
                    dve.wait_ge(spread, q + 1)
                    dve.tensor_tensor(g.rel[:, q * 512:q * 512 + w], nodef[:, q * 512:q * 512 + w], g.bank[q][:, 0:w], ALU.subtract).then_inc(taken, 1)
                for q in range(-(-C1 // 512)):
                    w = min(512, C1 - q * 512)
                    dve.wait_ge(spread, q + 5)
                    dve.tensor_copy(g.keep[:, q * 512:q * 512 + w], g.bank[q][:, 0:w]).then_inc(taken, 1)

            @block.sync
            def _(sp):
                sp.dma_start(rows[:, :], io["keys"].rearrange("(p f) -> p f", p=P)).then_inc(loaded, 16)
                chunks = io["keys"].rearrange("(c e) -> c e", e=P)
                with nc.allow_non_contiguous_dma(reason="one key of each chunk"):
                    sp.dma_start(ends[:, 0, :], chunks[:, 0:1].rearrange("c e -> e c")).then_inc(loaded, 16)
                    sp.dma_start(ends[:, 1, :], chunks[:, P - 1:P].rearrange("c e -> e c")).then_inc(loaded, 16)
                sp.dma_start(crow[:, :, :], chunks[0:CH, :].rearrange("(b j) e -> j b e", j=B)).then_inc(loaded, 16)
                sp.wait_ge(s, at["place"])
                sp.dma_start(io["place"].rearrange("(b j e) -> j b e", j=B, e=P), placeb[:, :, :]).then_inc(stored, 16)
                sp.wait_ge(stored, 16)

            @block.tensor
            def _(pe):
                pe.wait_ge(loaded, 64)
                natf = rows[:, :].bitcast(F32)
                for q in range(4):
                    for r in range(4):
                        c = (4 * q + r) * P
                        last = nc.tensor.transpose(g.bank[q][:, r * P:(r + 1) * P], natf[:, c:c + P], g.ident[:, :])
                    last.then_inc(turned, 1)
                pe.wait_ge(s, at["flags"])
                for q in range(4):
                    pe.wait_ge(taken, 4 + q)
                    nc.tensor.matmul(g.bank[q][:, :], g.ones[0:1, :], endf[0:1, 0, q * 512:(q + 1) * 512], start=True, stop=True).then_inc(spread, 1)
                for q in range(-(-C1 // 512)):
                    pe.wait_ge(taken, 8 + q)
                    nc.tensor.matmul(g.bank[q][:, :], g.ones[0:1, :], cont[0:1, q * 512:(q + 1) * 512], start=True, stop=True).then_inc(spread, 1)


def running_lows(nc, io, g, c0, n_chunks, H):
    nb, HP = n_chunks // B, B * H
    with ExitStack() as stack:
        m = Memory(nc, stack, f"low{g.lows}")
        g.lows += 1
        krow = m.sbuf("krow", [HP, nb, P], I32)
        krowf = m.sbuf("krowf", [HP, nb, P])
        other = m.sbuf("other", [HP, nb, P])
        key_in, s = m.sem("key_in"), m.sem("step")
        with nc.Block() as block:
            @block.sync
            def _(sp):
                keys_of = io["keys"][c0 * P:(c0 + n_chunks) * P].rearrange("(b j e) -> j b e", j=B, e=P)
                for h in range(H):
                    sp.dma_start(krow[h:HP:H, :, :], keys_of).then_inc(key_in, 16)

            @block.vector
            def _(dve):
                n = [0]

                def did(ins):
                    n[0] += 1
                    ins.then_inc(s, 1)
                    dve.wait_ge(s, n[0])

                did(dve.memset(g.low[:, :, :], LOW))
                did(dve.memset(g.low_back[:, :, :], LOW))
                dve.wait_ge(key_in, 16 * H)
                did(dve.tensor_scalar(krow[:, :, :], krow[:, :, :], SB, MASK, ALU.logical_shift_right, ALU.bitwise_and))
                did(dve.tensor_copy(krowf[:, :, :], krow[:, :, :]))
                did(dve.tensor_tensor(other[:, :, 1:P], krowf[:, :, 1:P], krowf[:, :, 0:P - 1], ALU.not_equal))
                did(dve.tensor_scalar(g.low[:, :, 1:P], other[:, :, 1:P], LOW, None, ALU.mult))
                did(dve.tensor_scalar(g.low_back[:, :, 1:P][:, :, ::-1], other[:, :, 1:P], LOW, None, ALU.mult))
                did(dve.tensor_tensor(other[:, :, :], krowf[:, :, :], krowf[:, :, 0:1].broadcast_to([HP, nb, P]), ALU.not_equal))
                did(dve.tensor_scalar(g.low0[:, :, :], other[:, :, :], LOW, None, ALU.mult))


def gather_pass(nc, io, g, kind, table, c0, n_chunks):
    soft = kind != "gcn"
    H = HEADS if kind == "router" else 1
    HP = B * H
    W = table.shape[1]
    blocks = {"gcn": 1, "gat": 3, "router": 1}[kind]
    OUT = HEADS * NE + HEADS if kind == "router" else P
    score = {"gat": D, "router": HEADS * NE}.get(kind)
    nb = n_chunks // B
    with ExitStack() as stack:
        m = Memory(nc, stack, kind + str(g.passes))
        g.passes += 1
        rows = m.sbuf("rows", [P, 2, B, W])
        index = m.sbuf("index", [P, 2, B], I32)
        rel = m.sbuf("rel_now", [P, B])
        keep = m.sbuf("keep_now", [P, B])
        onehot = m.sbuf("onehot", [P, 4, P])
        first = m.sbuf("first", [P, 8, blocks])
        idx_set = m.sem("index_set")
        gathered = [m.sem(f"gathered{i}") for i in (0, 1)]
        oh = m.sem("onehot_made")
        summed = m.sem("summed")
        moved = m.sem("moved")
        fixed = m.sem("fixed")
        ready = m.sem("batch_ready")
        if soft:
            low, low_back, low0 = g.low, g.low_back, g.low0
            place = m.sbuf("place_now", [P, 2, 4, P], BF16)
            turned = m.sbuf("turned", [P, 2, 2, 4, P], BF16)
            erd = m.sbuf("erd", [P, HP])
            fwd = m.sbuf("fwd", [P, P])
            top = m.sbuf("top", [HP, P])
            ers = m.sbuf("ers", [HP, P + 1])
            zz = m.sbuf("zz", [HP, 2, P + 1])
            zl = m.sbuf("zl", [HP, 2, P + 1])
            diff = m.sbuf("diff", [HP, P + 1])
            wrow = m.sbuf("wrow", [P, P + 1])
            wcol = m.sbuf("wcol", [P, HP])
            state = m.sbuf("state", [1, B + 1, H])
            carry = m.sbuf("carry", [1, P])
            cin = m.sbuf("cin", [HP, 1])
            spread = m.sbuf("spread", [P, OUT])
            select = m.sbuf("select", [HP, OUT])
            place_in = [m.sem(f"place_in{i}") for i in (0, 1)]
            place_used = m.sem("place_used")
            er_sum = m.sem("er_sum")
            d2p, p2d = m.sem("dve_to_pe"), m.sem("pe_to_dve")
            er_copied = m.sem("er_copied")
            d2a, exped = m.sem("dve_to_act"), m.sem("exped")
            if kind == "router":
                pay = m.sbuf("pay", [P, B, OUT])
                els = m.sbuf("els", [P, HP])
        QB = B // 4
        acc = g.acc
        row_ap = table[:, :]

        def chunk(b, j):
            return b * B + j

        with nc.Block() as block:
            @block.gpsimd
            def _(pool):
                with pool.Fori(0, nb // 2) as it:
                    for s in (0, 1):
                        b = it * 2 + s
                        wait_alone(pool, g, summed, b * B + B)
                        pool.tensor_copy(index[:, s, :], g.src[:, bass.ds(b * B + c0, B)]).then_inc(idx_set, 1)
                        wait_alone(pool, g, idx_set, b + 1)
                        for j in range(B):
                            pool.indirect_dma_start(rows[:, s, j, :], None, row_ap,
                                                    bass.IndirectOffsetOnAxis(index[:, s, j:j + 1], 0)).then_inc(gathered[s], 16)

            if soft:
                @block.sync
                def _(sp):
                    places = io["place"][c0 * P:(c0 + n_chunks) * P].rearrange("(q n) -> q n", n=4 * P)
                    with sp.Fori(0, nb * QB // 2) as i2:
                        for s in (0, 1):
                            i = i2 * 2 + s
                            sp.wait_ge(place_used, i + 1)
                            sp.dma_start(place[:, s].rearrange("p c e -> p (c e)"),
                                         places[bass.ds(i, 1), :].rearrange("q n -> (q n)").partition_broadcast(P)).then_inc(place_in[s], 16)

            @block.vector
            def _(dve):
                n = [0]
                if soft:
                    dve.memset(state[:, 0:1, :], LOW)
                    for t in (fwd, wrow, spread, carry):
                        dve.memset(t[:, :], 0.0)
                    dve.nop().then_inc(place_used, 2)
                    dve.drain()

                def ap(t, b):
                    return t[:, bass.ds(b, 1), :].rearrange("q b e -> q (b e)")

                with dve.Fori(0, nb // 2) as it:
                    for s in (0, 1):
                        b = it * 2 + s
                        if soft:
                            for q in range(QB):
                                i = b * QB + q
                                dve.wait_ge(place_in[q % 2], it * (16 * QB) + (s * QB // 2 + q // 2 + 1) * 16)
                                dve.wait_ge(er_sum, i + 1)
                                for t in (0, 1):
                                    last = dve.tensor_scalar(turned[:, q % 2, t], place[:, q % 2], g.pcol[:, t:t + 1], None, ALU.is_equal)
                                last.then_inc(place_used, 1)
                            dve.wait_ge(er_sum, b * QB + QB + 2)
                            if kind == "router":
                                dve.wait_ge(gathered[s], (it + 1) * (16 * B))
                                dve.tensor_copy(els[:, :].rearrange("p (j h) -> p j h", h=H), rows[:, s, :, score:score + H])
                            dve.tensor_reduce(erd[:, :], g.bank[7][:, 0:3 * HP].rearrange("p (q k) -> p q k", k=3), AX, ALU.add).then_inc(d2p, 1)
                            dve.wait_ge(p2d, b * 4 + 1)
                            el, _ = g.bank[4][0:HP, 0:P], g.bank[5][0:HP, 0:P]
                            dve.tensor_tensor_scan(fwd[0:HP, :], ap(low, b), el, LOW, ALU.add, ALU.max).then_inc(d2p, 1)
                            dve.drain()
                            dve.tensor_tensor_scan(top[:, ::-1], ap(low_back, b), fwd[0:HP, ::-1], LOW, ALU.add, ALU.max)
                            dve.wait_ge(p2d, b * 4 + 2)
                            lasts = g.bank[6][0:1, 0:HP].rearrange("o (j h) -> o j h", h=H)
                            same = g.same_low[0:1, bass.ds(b * B + c0, B)]
                            for h in range(H):
                                dve.tensor_tensor_scan(state[:, 1:, h], same, lasts[:, :, h], state[:, 0:1, h], ALU.add, ALU.max)
                            dve.drain()
                            cont = g.cont_low[0:1, bass.ds(b * B + c0, B)].unsqueeze(2).broadcast_to([1, B, H])
                            dve.tensor_tensor(carry[:, 0:HP].rearrange("o (j h) -> o j h", h=H), state[:, 0:B, :], cont, ALU.add).then_inc(d2p, 1)
                            dve.drain()
                            dve.tensor_copy(state[:, 0:1, :], state[:, B:B + 1, :])
                            dve.wait_ge(p2d, b * 4 + 3)
                            dve.tensor_copy(cin[:, :], g.bank[6][0:HP, 256:257])
                            dve.drain()
                            dve.wait_ge(er_copied, b + 1)
                            dve.scalar_tensor_tensor(out=top[:, :], in0=ap(low0, b), scalar=cin[:, 0:1], in1=top[:, :], op0=ALU.add, op1=ALU.max)
                            dve.tensor_tensor(zz[:, 0, 0:P], el, ers[:, 0:P], ALU.add)
                            dve.tensor_tensor(zz[:, 0, P:P + 1], cin[:, :], ers[:, P:P + 1], ALU.add)
                            dve.drain()
                            dve.tensor_tensor(zz[:, 1, 0:P], top[:, :], ers[:, 0:P], ALU.add)
                            dve.tensor_tensor(zz[:, 1, P:P + 1], top[:, 0:1], ers[:, P:P + 1], ALU.add)
                            dve.drain()
                            dve.scalar_tensor_tensor(out=zl[:, :, :], in0=zz[:, :, :], scalar=0.2, in1=zz[:, :, :], op0=ALU.mult, op1=ALU.max)
                            dve.drain()
                            dve.tensor_tensor(diff[:, :], zl[:, 0, :], zl[:, 1, :], ALU.subtract).then_inc(d2a, 1)
                            dve.wait_ge(exped, b + 1)
                            dve.tensor_scalar(spread[0:HP, :], g.select[kind][0:HP, 0:OUT], wrow[0:HP, P:P + 1], None, ALU.mult).then_inc(d2p, 1)
                            dve.wait_ge(p2d, b * 4 + 4)
                            dve.tensor_copy(wcol[:, :], g.bank[6][:, 0:HP])
                            dve.tensor_copy(keep[0:OUT, :], g.bank[6][0:OUT, 128:128 + B])
                        else:
                            dve.drain()
                            dve.tensor_copy(keep[:, :], g.keep[:, bass.ds(b * B + c0, B)])
                        dve.tensor_copy(rel[:, :], g.rel[:, bass.ds(b * B + c0, B)])
                        dve.drain()
                        if kind == "router":
                            w4 = wcol[:, :].rearrange("p (j h) -> p j h", h=H)
                            dve.wait_ge(gathered[s], (it + 1) * (16 * B))
                            dve.tensor_tensor(pay[:, :, 0:HEADS * NE].rearrange("p j (h x) -> p j h x", h=H),
                                              rows[:, s, :, 0:HEADS * NE].rearrange("p j (h x) -> p j h x", h=H),
                                              w4.unsqueeze(3).broadcast_to([P, B, H, NE]), ALU.mult)
                            dve.tensor_copy(pay[:, :, HEADS * NE:OUT], w4).then_inc(ready, 1)

                        def fix(j):
                            c = b * B + j
                            at = dve.value_load(g.base[0:1, bass.ds(c + c0, 1)], min_val=0, max_val=NPAD)
                            dve.wait_ge(moved, c + 5)
                            dve.wait_ge(fixed, c + 8)
                            a = acc[0:OUT, 0:blocks, bass.ds(at, 1)].rearrange("p k o -> p (k o)")
                            dve.scalar_tensor_tensor(out=a, in0=a, scalar=keep[0:OUT, j:j + 1], in1=first[0:OUT, j % 8, :],
                                                     op0=ALU.mult, op1=ALU.add).then_inc(fixed, 1)

                        for j in range(B):
                            c = b * B + j
                            dve.wait_ge(summed, c + 2 * B - 3)
                            if kind == "gat":
                                dve.tensor_scalar(onehot[:, j % 4, :], g.iota[:, :], rel[:, j:j + 1], wcol[:, j:j + 1], ALU.is_equal, ALU.mult).then_inc(oh, 1)
                            else:
                                dve.tensor_scalar(onehot[:, j % 4, :], g.iota[:, :], rel[:, j:j + 1], None, ALU.is_equal).then_inc(oh, 1)
                            if j >= 3:
                                fix(j - 3)
                        for j in range(B - 3, B):
                            fix(j)

            @block.tensor
            def _(pe):
                pe.nop().then_inc(summed, 2 * B)
                if soft:
                    pe.nop().then_inc(er_sum, 2)
                with pe.Fori(0, nb // 2) as it:
                    for s in (0, 1):
                        b = it * 2 + s
                        if soft:
                            for q in range(QB):
                                pe.wait_ge(place_used, b * QB + q + 3)
                                for r in range(4):
                                    j = 4 * q + r
                                    t0 = pe.value_load(g.tile[0:1, bass.ds(b * B + c0 + j, 1)], min_val=0, max_val=NT)
                                    for t in (0, 1):
                                        last = nc.tensor.matmul(g.bank[7][:, 3 * H * j:3 * H * (j + 1)], turned[:, q % 2, t, r, :],
                                                                g.er[:, bass.ds((t0 + t) * (3 * H), 3 * H)], start=t == 0, stop=t == 1)
                                last.then_inc(er_sum, 1)
                            pe.wait_ge(gathered[s], (it + 1) * (16 * B))
                            pe.wait_ge(d2p, b * 4 + 1)
                            nc.tensor.transpose(g.bank[4][0:HP, 0:P], els[:, :] if kind == "router" else rows[:, s, :, score], g.ident[:, :])
                            nc.tensor.transpose(g.bank[5][0:HP, 0:P], erd[:, :], g.ident[:, :]).then_inc(p2d, 1)
                            pe.wait_ge(d2p, b * 4 + 2)
                            nc.tensor.matmul(g.bank[6][0:1, 0:HP], fwd[:, P - 1:P], g.ident[:, 0:HP], start=True, stop=True).then_inc(p2d, 1)
                            pe.wait_ge(d2p, b * 4 + 3)
                            nc.tensor.matmul(g.bank[6][:, 256:257], carry[:, :], g.ones[0:1, 0:1],
                                             start=True, stop=True).then_inc(p2d, 1)
                            pe.wait_ge(d2p, b * 4 + 4)
                            nc.tensor.transpose(g.bank[6][:, 0:P], wrow[:, 0:P], g.ident[:, :])
                            grouping = g.group if kind == "router" else g.ident
                            nc.tensor.matmul(g.bank[6][0:OUT, 128:128 + B], spread[:, :], grouping[:, 0:B], start=True, stop=True).then_inc(p2d, 1)
                        else:
                            pe.wait_ge(gathered[s], (it + 1) * (16 * B))
                        if kind == "router":
                            pe.wait_ge(ready, b + 1)
                        for j in range(B):
                            c = b * B + j
                            pe.wait_ge(oh, c + 1)
                            pe.wait_ge(moved, c + 1)
                            out = g.bank[j % 4]
                            if kind == "router":
                                last = nc.tensor.matmul(out[0:OUT, 0:P], pay[:, j, :], onehot[:, j % 4, :], start=True, stop=True)
                            else:
                                for k in range(min(blocks, 2)):
                                    last = nc.tensor.matmul(out[:, k * P:(k + 1) * P], rows[:, s, j, k * P:(k + 1) * P], onehot[:, j % 4, :], start=True, stop=True)
                                if blocks == 3:
                                    last = nc.tensor.matmul(out[:, 2 * P:3 * P], g.ones[:, :], onehot[:, j % 4, :], start=True, stop=True)
                            last.then_inc(summed, 1)

            @block.scalar
            def _(act):
                act.nop().then_inc(moved, 4)
                act.nop().then_inc(fixed, 8)
                if soft:
                    act.preload_act_table(ACT.Exp)
                with act.Fori(0, nb // 2) as it:
                    for s in (0, 1):
                        b = it * 2 + s
                        if soft:
                            act.wait_ge(p2d, b * 4 + 1)
                            act.activation(ers[:, 0:P], g.bank[5][0:HP, 0:P], ACT.Copy)
                            act.activation(ers[:, P:P + 1], g.bank[5][0:HP, 0:1], ACT.Copy).then_inc(er_copied, 1)
                            act.wait_ge(d2a, b + 1)
                            act.activation(wrow[0:HP, :], diff[:, :], ACT.Exp).then_inc(exped, 1)
                        for j in range(B):
                            c = b * B + j
                            at = act.value_load(g.base[0:1, bass.ds(c + c0, 1)], min_val=0, max_val=NPAD)
                            act.wait_ge(summed, c + 2 * B + 1)
                            act.wait_ge(fixed, c + 1)
                            src = g.bank[j % 4][0:OUT, 0:blocks * P].rearrange("p (k n) -> p k n", k=blocks)
                            act.activation(first[0:OUT, j % 8, :], src[:, :, 0], ACT.Copy)
                            act.wait_ge(moved, c + 4)
                            act.activation(acc[0:OUT, 0:blocks, bass.ds(at + 1, P - 1)], src[:, :, 1:P], ACT.Copy).then_inc(moved, 1)


class Normaliser:

    def __init__(self, m):
        self.parts = m.sbuf("ln_parts", [P, G, 6])
        self.mv = m.sbuf("ln_mv", [P, G, 2])
        self.var = m.sbuf("ln_var", [P, G])
        self.root = m.sbuf("ln_root", [P, G])
        self.inv = m.sbuf("ln_inv", [P, G])
        self.tmp = m.sbuf("ln_tmp", [P, G])
        self.var_ready, self.root_ready = m.sem("var_ready"), m.sem("root_ready")

    def vector(self, dve, x, out, gi, done):
        for t in range(G):
            dve.bn_stats(self.parts[:, t, :], x[:, t, :])
        dve.drain()
        for t in range(G):
            dve.bn_aggr(self.mv[:, t, :], self.parts[:, t, :])
        dve.drain()
        dve.tensor_scalar(self.var[:, :], self.mv[:, :, 1], EPS, None, ALU.add).then_inc(self.var_ready, 1)
        dve.drain()
        dve.wait_ge(self.root_ready, gi + 1)
        newton(dve, self.var[:, :], self.root[:, :], self.inv[:, :], self.tmp[:, :])
        for t in range(G):
            last = dve.tensor_scalar(out[:, t, :], x[:, t, :], self.mv[:, t, 0:1], self.inv[:, t:t + 1], ALU.subtract, ALU.mult)
        last.then_inc(done, 1)

    def scalar(self, act, gi):
        act.wait_ge(self.var_ready, gi + 1)
        act.activation(self.root[:, :], self.var[:, :], ACT.Sqrt).then_inc(self.root_ready, 1)


def newton(dve, var, root, inv, tmp):
    dve.reciprocal(inv, root)
    dve.drain()
    dve.tensor_tensor(tmp, inv, inv, ALU.mult)
    dve.drain()
    dve.tensor_tensor(tmp, tmp, var, ALU.mult)
    dve.drain()
    dve.tensor_scalar(tmp, tmp, -0.5, 1.5, ALU.mult, ALU.add)
    dve.drain()
    dve.tensor_tensor(inv, inv, tmp, ALU.mult)
    dve.drain()


def turn(nc, g, x, turned):
    for i in range(2 * G):
        t, c = divmod(i, 2)
        last = nc.tensor.transpose(g.bank[i // 4][:, i % 4 * P:(i % 4 + 1) * P], x[:, t, c * P:(c + 1) * P], g.ident[:, :])
        if i % 4 == 3 or i == 2 * G - 1:
            last.then_inc(turned, 1)


def turned_copies(act, g, out, turned, before, done):
    flat = out[:, :, :, :].rearrange("p t c n -> p (t c n)")
    for q in range(4):
        w = min(512, 2 * G * P - q * 512)
        act.wait_ge(turned, before + q + 1)
        last = act.activation(flat[:, q * 512:q * 512 + w], g.bank[q][:, 0:w], ACT.Copy)
    last.then_inc(done, 1)


def project(nc, io, g, kind):
    from_acc = kind in ("gat1", "router")
    loads_x = kind != "gat1"
    H = HEADS if kind == "router" else 1
    M = {"gcn": HID, "gat0": D, "gat1": D, "router": HEADS * NE}[kind]
    OUT = M if kind == "gcn" else M + 2 * H
    table = io["table_" + {"gcn": "gcn", "router": "router"}.get(kind, "gat")]
    TW = table.shape[1]
    x_rows = {"gcn": io["x"], "gat0": io["res"], "router": io["res"]}.get(kind)
    layer = {"gat0": 0, "gat1": 1}.get(kind)
    with ExitStack() as stack:
        m = Memory(nc, stack, "project_" + kind)
        x = m.sbuf("x", [P, G, D])
        xn = m.sbuf("xn", [P, G, D])
        xt = m.sbuf("xt", [P, G, 2, P])
        wt = m.sbuf("wt", [P, 2, OUT])
        trow = m.sbuf("trow", [P, G, TW])
        norm = Normaliser(m)
        w_in, w_done, x_in = m.sem("w_in"), m.sem("w_done"), m.sem("x_in")
        xn_ready, turned, xt_ready = m.sem("xn_ready"), m.sem("turned"), m.sem("xt_ready")
        made, taken, stored = m.sem("made"), m.sem("taken"), m.sem("stored")
        stores = 48 if kind == "router" else 16
        loads = 1
        if kind == "gcn":
            dn = m.sbuf("dn", [P, G])
        else:
            att = m.sbuf("att", [P, 2, M])
            prod = m.sbuf("prod", [P, 2, M])
            er, er_rest = m.sbuf("er", [P, G, H]), m.sbuf("er_rest", [P, G, H])
            er_part = m.sbuf("er_part", [P, G, H], BF16)
            parts = m.sem("parts")
            loads = 3
        if from_acc:
            inv_den = m.sbuf("inv_den", [P, G * P])
            ot = m.sbuf("ot", [P, 2, G * P])
            bias = m.sbuf("bias", [P, 2])
            scaled, ot_ready, back, out_ready = m.sem("scaled"), m.sem("ot_ready"), m.sem("back"), m.sem("out_ready")
            loads = 5

        with nc.Block() as block:
            @block.sync
            def _(sp):
                w = {"gcn": io["W_conv"], "router": io["W_gat"]}.get(kind)
                w = io["W"][layer] if w is None else w
                sp.dma_start(wt[:, :, 0:M], w.rearrange("(c p) n -> p c n", p=P)).then_inc(w_in, 16)
                if kind != "gcn":
                    al, ar = (io["att_src"], io["att_dst"]) if kind == "router" else (io["attn_l"][layer], io["attn_r"][layer])
                    flat = (lambda a: a.rearrange("h x -> (h x)")) if kind == "router" else (lambda a: a)
                    sp.dma_start(att[:, 0, :], flat(al).partition_broadcast(P)).then_inc(w_in, 16)
                    sp.dma_start(att[:, 1, :], flat(ar).partition_broadcast(P)).then_inc(w_in, 16)
                if from_acc:
                    b = io["bias"][1 if kind == "router" else 0]
                    for c in (0, 1):
                        sp.dma_start(bias[:, c:c + 1], b[c * P:(c + 1) * P].rearrange("(p o) -> p o", o=1)).then_inc(w_in, 16)
                sp.nop().then_inc(stored, stores)
                with sp.Fori(0, NG) as gi:
                    if loads_x:
                        sp.wait_ge(stored, (gi + 1) * stores)
                        rows = x_rows.rearrange("(t p) d -> p t d", p=P)
                        sp.dma_start(x[:, :, :], rows[:, bass.ds(gi * G, G), :]).then_inc(x_in, 16)
                    if kind == "router":
                        sp.wait_ge(out_ready, gi + 1)
                        rows = io["res2"].rearrange("(t p) d -> p t d", p=P)
                        sp.dma_start(rows[:, bass.ds(gi * G, G), :], x[:, :, :]).then_inc(stored, 16)
                        sp.wait_ge(xt_ready, gi + 1)
                        sp.dma_start(io["xt"][bass.ds(gi, 1)].rearrange("o p n -> (o p) n"), xt[:, :, :, :].rearrange("p t c n -> p (t c n)")).then_inc(stored, 16)
                    sp.wait_ge(taken, gi * G + G + 4)
                    rows = table.rearrange("(t p) w -> p t w", p=P)
                    sp.dma_start(rows[:, bass.ds(gi * G, G), :], trow[:, :, :]).then_inc(stored, 16)
                sp.wait_ge(stored, (NG + 1) * stores)

            @block.vector
            def _(dve):
                dve.memset(trow[:, :, :], 0.0)
                dve.wait_ge(w_in, 16 * loads)
                if kind in ("gat0", "gat1"):
                    for side in (0, 1):
                        for c in (0, 1):
                            dve.tensor_tensor_reduce(out=prod[:, c, :], in0=wt[:, c, 0:M], in1=att[:, side, :], scale=1.0, scalar=0.0,
                                                     op0=ALU.mult, op1=ALU.add, accum_out=wt[:, c, M + side:M + side + 1])
                            dve.drain()
                if kind == "router":
                    for side in (0, 1):
                        dve.tensor_tensor(prod[:, :, :], wt[:, :, 0:M], att[:, side:side + 1, :].broadcast_to([P, 2, M]), ALU.mult)
                        dve.drain()
                        dve.tensor_reduce(wt[:, :, M + side * H:M + (side + 1) * H], prod[:, :, :].rearrange("p c (h x) -> p c h x", x=NE), AX, ALU.add)
                        dve.drain()
                if kind != "gcn":
                    dve.memset(g.er[:, :], 0.0)
                    dve.nop().then_inc(parts, 1)
                dve.drain()
                dve.nop().then_inc(w_done, 1)
                with dve.Fori(0, NG) as gi:
                    dve.wait_ge(taken, gi * G + 4)
                    if kind == "gcn":
                        dve.tensor_copy(dn[:, :], g.dinv[:, bass.ds(gi * G, G)])
                    if from_acc:
                        nodes = bass.ds(gi * (G * P), G * P)
                        dve.reciprocal(inv_den[:, :], g.acc[:, 2, nodes])
                        dve.drain()
                        for c in (0, 1):
                            last = dve.tensor_tensor(ot[:, c, :], g.acc[:, c, nodes], inv_den[:, :], ALU.mult)
                        last.then_inc(scaled, 1)
                    if kind == "router":
                        dve.wait_ge(x_in, (gi + 1) * 16)
                        for q in range(4):
                            w = min(2, G - 2 * q)
                            dve.wait_ge(back, gi * 4 + q + 1)
                            last = dve.tensor_tensor(x[:, 2 * q:2 * q + w, :], x[:, 2 * q:2 * q + w, :],
                                                     g.bank[q][:, 0:w * D].rearrange("p (t d) -> p t d", d=D), ALU.add)
                        last.then_inc(out_ready, 1)
                        dve.drain()
                    elif loads_x:
                        dve.wait_ge(x_in, (gi + 1) * 16)
                    if loads_x:
                        norm.vector(dve, x, xn, gi, xn_ready)
                    if kind != "gcn":
                        dve.wait_ge(taken, gi * G + G + 4)
                        part = g.er[:, bass.ds(gi * (G * 3 * H), G * 3 * H)].rearrange("p (t h k) -> p t h k", h=H, k=3)
                        dve.tensor_copy(er_part[:, :, :], er[:, :, :])
                        dve.drain()
                        dve.tensor_copy(part[:, :, :, 0], er_part[:, :, :])
                        dve.tensor_tensor(er_rest[:, :, :], er[:, :, :], er_part[:, :, :], ALU.subtract)
                        dve.drain()
                        dve.tensor_copy(er_part[:, :, :], er_rest[:, :, :])
                        dve.drain()
                        dve.tensor_copy(part[:, :, :, 1], er_part[:, :, :])
                        dve.tensor_tensor(er_rest[:, :, :], er_rest[:, :, :], er_part[:, :, :], ALU.subtract)
                        dve.drain()
                        dve.tensor_copy(part[:, :, :, 2], er_rest[:, :, :]).then_inc(parts, 1)
                        dve.drain()

            @block.tensor
            def _(pe):
                pe.wait_ge(w_done, 1)
                with pe.Fori(0, NG) as gi:
                    if kind == "router":
                        pe.wait_ge(ot_ready, gi + 1)
                        for t in range(G):
                            for c in (0, 1):
                                last = nc.tensor.transpose(g.bank[t // 2][:, t % 2 * D + c * P:t % 2 * D + (c + 1) * P], ot[:, c, t * P:(t + 1) * P], g.ident[:, :])
                            if t % 2 or t == G - 1:
                                last.then_inc(back, 1)
                    if loads_x:
                        pe.wait_ge(xn_ready, gi + 1)
                        turn(nc, g, xn, turned)
                    pe.wait_ge(xt_ready, gi + 1)
                    for t in range(G):
                        pe.wait_ge(taken, gi * G + t + 2)
                        for c in (0, 1):
                            last = nc.tensor.matmul(g.bank[4 + t % 4][:, 0:OUT], xt[:, t, c, :], wt[:, c, :], start=c == 0, stop=c == 1)
                        last.then_inc(made, 1)

            @block.scalar
            def _(act):
                act.nop().then_inc(taken, 4)
                act.wait_ge(w_done, 1)
                with act.Fori(0, NG) as gi:
                    if from_acc:
                        act.wait_ge(scaled, gi + 1)
                        for c in (0, 1):
                            if kind == "router":
                                last = act.activation(ot[:, c, :], ot[:, c, :], ACT.Identity, bias=bias[:, c:c + 1])
                            else:
                                last = act.activation(xt[:, :, c, :], ot[:, c, :].rearrange("p (t n) -> p t n", n=P), ACT.Relu, bias=bias[:, c:c + 1])
                        last.then_inc(ot_ready if kind == "router" else xt_ready, 1)
                    if loads_x:
                        norm.scalar(act, gi)
                    act.wait_ge(stored, (gi + 1) * stores)
                    if loads_x:
                        turned_copies(act, g, xt, turned, gi * 4, xt_ready)
                    if kind != "gcn":
                        act.wait_ge(parts, gi + 1)
                    for t in range(G):
                        act.wait_ge(made, gi * G + t + 1)
                        bank = g.bank[4 + t % 4]
                        if kind == "gcn":
                            last = act.activation(trow[:, t, :], bank[:, 0:OUT], ACT.Copy, scale=dn[:, t:t + 1])
                        else:
                            act.activation(trow[:, t, 0:M + H], bank[:, 0:M + H], ACT.Copy)
                            last = act.activation(er[:, t, :], bank[:, M + H:OUT], ACT.Copy)
                        last.then_inc(taken, 1)


def experts(nc, io, g, kind):
    switch = kind == "switch"
    NM = 1 if switch else NE
    ins = {k: io[("s_" if switch else "t_") + k] for k in ("W1", "b1", "W2", "b2")}
    E = EXPERTS if switch else NE
    x_rows, out_rows = (io["x"], io["res"]) if switch else (io["res2"], io["out"])
    RW = HEADS * NE
    BLOCKS = NM * G
    SUBS = ((0, 4), (4, G - 4))
    with ExitStack() as stack:
        m = Memory(nc, stack, kind)
        x = m.sbuf("x", [P, G, D])
        xt = m.sbuf("xt", [P, G, 2, P])
        w1 = m.sbuf("w1", [P, 2, FH])
        w2 = m.sbuf("w2", [P, FT, D])
        b1 = m.sbuf("b1", [P, FT])
        b2 = m.sbuf("b2", [EXPERTS, D])
        ot = m.sbuf("ot", [P, G * P])
        chosen = m.sbuf("chosen", [P, G, EXPERTS])
        wide = m.sbuf("wide", [P, NM, G, P])
        gate = m.sbuf("gate", [P, NM, G * P])
        chosen_t = m.sbuf("chosen_t", [EXPERTS, G * P])
        zero = m.sbuf("zero", [P, 4 * P], BF16)
        raw = m.sbuf("raw", [P, 4, 4 * P])
        hidden = m.sbuf("hidden", [P, 4, 4 * P])
        norm = Normaliser(m)
        w_in, w_done, x_in = m.sem("w_in"), m.sem("w_done"), m.sem("x_in")
        ot_ready, sums, xn_ready = m.sem("ot_ready"), m.sem("sums"), m.sem("xn_ready")
        turned, xt_ready, logits_up = m.sem("turned"), m.sem("xt_ready"), m.sem("logits_up")
        routed, spread, gated = m.sem("routed"), m.sem("spread"), m.sem("gated")
        h_made, h_raw, h_ready, h_used = m.sem("h_made"), m.sem("h_raw"), m.sem("h_ready"), m.sem("h_used")
        x_ready, stored = m.sem("x_ready"), m.sem("stored")
        if switch:
            xn = m.sbuf("xn", [P, G, D])
            wlin = m.sbuf("wlin", [P, D])
            bconv = m.sbuf("bconv", [P, 1])
            bconv_wide = m.sbuf("bconv_wide", [P, P])
            blin = m.sbuf("blin", [P, D])
            rw = m.sbuf("rw", [EXPERTS, D])
            rwt = m.sbuf("rwt", [P, 2, EXPERTS])
            rb = m.sbuf("rb", [P, EXPERTS])
            dn = m.sbuf("dn", [P, G])
            logits = m.sbuf("logits", [P, G, EXPERTS])
            top = m.sbuf("top", [P, G, 8])
            topi = m.sbuf("topi", [P, G, 8], U32)
            best = m.sbuf("best", [P, G])
            own = m.sbuf("own", [P, FT])
            setup = m.sem("setup")
        else:
            den = m.sbuf("den", [P, G, HEADS])
            agg = m.sbuf("agg", [P, G, RW])
            aggn = m.sbuf("aggn", [P, G, RW])
            rows3 = m.sbuf("rows3", [P, 3, RW])
            scores = m.sbuf("scores", [P, 2, G, 8])
            top = m.sbuf("top", [P, 2, G, 8])
            topi = m.sbuf("topi", [P, 2, G, 8], U32)
            best = m.sbuf("best", [P, 2, G])
            hot = m.sbuf("hot", [P, 2, G, NE])
            gap, rise = m.sbuf("gap", [P, G]), m.sbuf("rise", [P, G])
            share = m.sbuf("share", [P, 2, G])
            gap_ready, gap_exped = m.sem("gap_ready"), m.sem("gap_exped")

        with nc.Block() as block:
            @block.sync
            def _(sp):
                n = 0
                with nc.allow_non_contiguous_dma(reason="biases by partition"):
                    for c in (0, 1):
                        sp.dma_start(w1[:, c, :], ins["W1"][c * P:(c + 1) * P, :]).then_inc(w_in, 16)
                    sp.dma_start(w2[:, :, :], ins["W2"].rearrange("e h d -> (e h) d").rearrange("(f p) d -> p f d", p=P)).then_inc(w_in, 16)
                    sp.dma_start(b1[:, :], ins["b1"]).then_inc(w_in, 16)
                    sp.wait_ge(w_done, 1)
                    sp.dma_start(b2[0:E, :], ins["b2"]).then_inc(w_in, 16)
                    n += 5
                    if switch:
                        sp.dma_start(wlin[:, :], io["W_lin"]).then_inc(w_in, 16)
                        sp.dma_start(bconv[:, :], io["b_conv"].rearrange("(p o) -> p o", o=1)).then_inc(w_in, 16)
                        sp.dma_start(blin[:, :], io["b_lin"].partition_broadcast(P)).then_inc(w_in, 16)
                        sp.dma_start(rw[:, :], io["router_w"]).then_inc(w_in, 16)
                        sp.dma_start(rb[:, :], io["router_b"].partition_broadcast(P)).then_inc(w_in, 16)
                        n += 5
                    else:
                        for i, k in enumerate(("b_gat", "ln_gamma", "ln_beta")):
                            sp.dma_start(rows3[:, i, :], io[k].partition_broadcast(P)).then_inc(w_in, 16)
                        n += 3
                assert n == (10 if switch else 8)
                sp.nop().then_inc(stored, 16)
                with sp.Fori(0, NG) as gi:
                    sp.wait_ge(stored, (gi + 1) * 16)
                    rows = x_rows.rearrange("(t p) d -> p t d", p=P)
                    sp.dma_start(x[:, :, :], rows[:, bass.ds(gi * G, G), :]).then_inc(x_in, 16)
                    if not switch:
                        sp.wait_ge(x_ready, gi + 1)
                        sp.dma_start(xt[:, :, :, :].rearrange("p t c n -> p (t c n)"), io["xt"][bass.ds(gi, 1)].rearrange("o p n -> (o p) n")).then_inc(xt_ready, 16)
                    sp.wait_ge(x_ready, gi + 2)
                    rows = out_rows.rearrange("(t p) d -> p t d", p=P)
                    sp.dma_start(rows[:, bass.ds(gi * G, G), :], x[:, :, :]).then_inc(stored, 16)
                sp.wait_ge(stored, (NG + 1) * 16)

            @block.vector
            def _(dve):
                dve.nop().then_inc(x_ready, 1)
                dve.nop().then_inc(h_ready, 4)
                dve.memset(b2[:, :], 0.0)
                dve.memset(zero[:, :], 0.0)
                dve.memset(chosen[:, :, :], 0.0)
                if not switch:
                    dve.memset(scores[:, :, :, :], LOW)
                dve.drain()
                dve.nop().then_inc(w_done, 1)
                dve.wait_ge(w_in, 16 * (10 if switch else 8))
                if switch:
                    dve.tensor_scalar(bconv_wide[:, :], g.ones[:, :], bconv[:, 0:1], None, ALU.mult).then_inc(setup, 1)
                    dve.wait_ge(setup, 2)
                    dve.tensor_tensor(blin[:, :], blin[:, :], g.bank[0][:, 0:D], ALU.add)
                    for c in (0, 1):
                        dve.tensor_copy(rwt[:, c, :], g.bank[1][:, c * EXPERTS:(c + 1) * EXPERTS])
                    dve.tensor_scalar(own[0:EH, :], g.iota[0:EH, 0:FT], 2.0, None, ALU.mult)
                    dve.tensor_scalar(own[EH:P, :], g.iota[EH:P, 0:FT], 2.0, 1.0, ALU.mult, ALU.add)
                    dve.drain()
                    dve.nop().then_inc(setup, 1)
                with dve.Fori(0, NG) as gi:
                    if switch:
                        dve.tensor_copy(dn[:, :], g.dinv[:, bass.ds(gi * G, G)])
                        dve.wait_ge(x_in, (gi + 1) * 16)
                        dve.tensor_tensor(x[:, :, :], x[:, :, :], blin[:, :].unsqueeze(1).broadcast_to([P, G, D]), ALU.add)
                        dve.drain()
                        for t in range(G):
                            if t % 2 == 0:
                                dve.wait_ge(sums, gi * 4 + t // 2 + 1)
                            dve.scalar_tensor_tensor(out=x[:, t, :], in0=g.bank[t // 2][:, t % 2 * D:(t % 2 + 1) * D], scalar=dn[:, t:t + 1],
                                                     in1=x[:, t, :], op0=ALU.mult, op1=ALU.add)
                        dve.drain()
                        norm.vector(dve, x, xn, gi, xn_ready)
                        dve.wait_ge(logits_up, gi + 1)
                        dve.tensor_tensor(logits[:, :, :], g.bank[6][:, 0:G * EXPERTS].rearrange("p (t e) -> p t e", e=EXPERTS),
                                          rb[:, :].unsqueeze(1).broadcast_to([P, G, EXPERTS]), ALU.add)
                        dve.drain()
                        for t in range(G):
                            dve.max(out=top[:, t, :], in_=logits[:, t, :])
                        dve.drain()
                        for t in range(G):
                            dve.max_index(out=topi[:, t, :], in_max=top[:, t, :], in_values=logits[:, t, :])
                        dve.drain()
                        dve.tensor_copy(best[:, :], topi[:, :, 0])
                        dve.drain()
                        dve.tensor_tensor(chosen[:, :, :], g.iota[:, 0:EXPERTS].unsqueeze(1).broadcast_to([P, G, EXPERTS]),
                                          best[:, :].unsqueeze(2).broadcast_to([P, G, EXPERTS]), ALU.is_equal)
                        dve.tensor_copy(wide[:, 0, :, :], best[:, :].unsqueeze(2).broadcast_to([P, G, P])).then_inc(routed, 1)
                    else:
                        dve.wait_ge(sums, gi + 1)
                        for q, (t0, n) in enumerate(SUBS):
                            v = g.bank[q][:, 0:n * P].rearrange("p (t k) -> p t k", k=P)
                            dve.tensor_scalar(den[:, t0:t0 + n, :], v[:, :, RW:RW + HEADS], 1e-16, None, ALU.add)
                        dve.drain()
                        dve.reciprocal(den[:, :, :], den[:, :, :])
                        dve.drain()
                        for q, (t0, n) in enumerate(SUBS):
                            for t in range(n):
                                v = g.bank[q][:, t * P:t * P + RW].rearrange("p (h x) -> p h x", x=NE)
                                dve.tensor_tensor(agg[:, t0 + t, :].rearrange("p (h x) -> p h x", x=NE), v,
                                                  den[:, t0 + t, :].unsqueeze(2).broadcast_to([P, HEADS, NE]), ALU.mult)
                        dve.drain()
                        r3 = [rows3[:, i:i + 1, :].broadcast_to([P, G, RW]) for i in range(3)]
                        dve.tensor_tensor(agg[:, :, :], agg[:, :, :], r3[0], ALU.add)
                        dve.drain()
                        norm.vector(dve, agg, aggn, gi, xn_ready)
                        dve.drain()
                        dve.tensor_tensor(aggn[:, :, :], aggn[:, :, :], r3[1], ALU.mult)
                        dve.drain()
                        dve.tensor_tensor(aggn[:, :, :], aggn[:, :, :], r3[2], ALU.add)
                        dve.drain()
                        dve.tensor_reduce(scores[:, 0, :, 0:NE], aggn[:, :, :].rearrange("p t (h x) -> p t x h", x=NE), AX, ALU.add)
                        dve.drain()
                        dve.tensor_scalar(scores[:, 0, :, 0:NE], scores[:, 0, :, 0:NE], 1.0 / HEADS, None, ALU.mult)
                        dve.drain()
                        for k in (0, 1):
                            for t in range(G):
                                dve.max(out=top[:, k, t, :], in_=scores[:, k, t, :])
                            dve.drain()
                            for t in range(G):
                                dve.max_index(out=topi[:, k, t, :], in_max=top[:, k, t, :], in_values=scores[:, k, t, :])
                            dve.drain()
                            dve.tensor_copy(best[:, k, :], topi[:, k, :, 0])
                            dve.drain()
                            dve.tensor_tensor(hot[:, k, :, :], g.iota[:, 0:NE].unsqueeze(1).broadcast_to([P, G, NE]),
                                              best[:, k, :].unsqueeze(2).broadcast_to([P, G, NE]), ALU.is_equal)
                            dve.drain()
                            if k == 0:
                                dve.scalar_tensor_tensor(out=scores[:, 1, :, 0:NE], in0=hot[:, 0, :, :], scalar=LOW / 2, in1=scores[:, 0, :, 0:NE], op0=ALU.mult, op1=ALU.add)
                                dve.drain()
                        dve.tensor_tensor(gap[:, :], top[:, 1, :, 0], top[:, 0, :, 0], ALU.subtract).then_inc(gap_ready, 1)
                        dve.wait_ge(gap_exped, gi + 1)
                        dve.tensor_scalar(share[:, 0, :], rise[:, :], 1.0, None, ALU.add)
                        dve.drain()
                        dve.reciprocal(share[:, 0, :], share[:, 0, :])
                        dve.drain()
                        dve.tensor_tensor(share[:, 1, :], share[:, 0, :], rise[:, :], ALU.mult)
                        dve.drain()
                        for k in (0, 1):
                            dve.tensor_tensor(hot[:, k, :, :], hot[:, k, :, :], share[:, k, :].unsqueeze(2).broadcast_to([P, G, NE]), ALU.mult)
                        dve.drain()
                        dve.tensor_tensor(chosen[:, :, 0:NE], hot[:, 0, :, :], hot[:, 1, :, :], ALU.add)
                        dve.drain()
                        for e in range(NE):
                            last = dve.tensor_copy(wide[:, e, :, :], chosen[:, :, e:e + 1].broadcast_to([P, G, P]))
                        last.then_inc(routed, 1)
                    BK = -(-BLOCKS // 4)
                    dve.wait_ge(gated, (gi + 1) * (BK + 2))
                    for f in range(FT):
                        for s, (t0, n) in enumerate(SUBS):
                            k = 2 * f + s
                            dve.wait_ge(h_raw, gi * (2 * FT) + k + 5)
                            dve.wait_ge(h_used, gi * (2 * FT) + k + 1)
                            cols = slice(t0 * P, (t0 + n) * P)
                            if switch:
                                dve.scalar_tensor_tensor(out=hidden[:, k % 4, 0:n * P], in0=gate[:, 0, cols], scalar=own[:, f:f + 1],
                                                         in1=raw[:, k % 4, 0:n * P], op0=ALU.is_equal, op1=ALU.mult).then_inc(h_ready, 1)
                            else:
                                dve.tensor_tensor(hidden[:, k % 4, 0:n * P], gate[:, f // (FT // NE), cols], raw[:, k % 4, 0:n * P], ALU.mult).then_inc(h_ready, 1)
                    if not switch:
                        dve.wait_ge(x_in, (gi + 1) * 16)
                    for q in range(4):
                        w = min(2, G - 2 * q)
                        if q % 2 == 0:
                            dve.wait_ge(h_used, (gi + 1) * (2 * FT) + 3 + q // 2)
                        xs, ps = x[:, 2 * q:2 * q + w, :], g.bank[q][:, 0:w * D].rearrange("p (t d) -> p t d", d=D)
                        if switch:
                            last = dve.scalar_tensor_tensor(out=xs, in0=ps, scalar=0.0, in1=xs, op0=ALU.max, op1=ALU.add)
                        else:
                            last = dve.tensor_tensor(xs, ps, xs, ALU.add)
                    last.then_inc(x_ready, 1)

            @block.tensor
            def _(pe):
                pe.nop().then_inc(h_used, 4)
                pe.wait_ge(w_in, 16 * (10 if switch else 8))
                if switch:
                    pe.wait_ge(setup, 1)
                    nc.tensor.matmul(g.bank[0][:, 0:D], bconv_wide[:, :], wlin[:, :], start=True, stop=True)
                    for c in (0, 1):
                        last = nc.tensor.transpose(g.bank[1][:, c * EXPERTS:(c + 1) * EXPERTS], rw[:, c * P:(c + 1) * P], g.ident[0:EXPERTS, 0:EXPERTS])
                    last.then_inc(setup, 1)
                    pe.wait_ge(setup, 3)
                with pe.Fori(0, NG) as gi:
                    pe.wait_ge(x_ready, gi + 1)
                    pe.wait_ge(ot_ready, gi + 1)
                    if switch:
                        for t in range(G):
                            last = nc.tensor.matmul(g.bank[t // 2][:, t % 2 * D:(t % 2 + 1) * D], ot[:, t * P:(t + 1) * P], wlin[:, :], start=True, stop=True)
                            if t % 2 or t == G - 1:
                                last.then_inc(sums, 1)
                        pe.wait_ge(xn_ready, gi + 1)
                        turn(nc, g, xn, turned)
                        pe.wait_ge(xt_ready, gi + 1)
                        for t in range(G):
                            for c in (0, 1):
                                last = nc.tensor.matmul(g.bank[6][:, t * EXPERTS:(t + 1) * EXPERTS], xt[:, t, c, :], rwt[:, c, :], start=c == 0, stop=c == 1)
                        last.then_inc(logits_up, 1)
                    else:
                        for t in range(G):
                            last = nc.tensor.transpose(g.bank[t // 4][:, t % 4 * P:(t % 4 + 1) * P], ot[:, t * P:(t + 1) * P], g.ident[:, :])
                        last.then_inc(sums, 1)
                        pe.wait_ge(xt_ready, (gi + 1) * 16)
                    pe.wait_ge(routed, gi + 1)
                    BK = -(-BLOCKS // 4)
                    for i in range(BLOCKS):
                        q = i // 4
                        if q >= 4 and i % 4 == 0:
                            pe.wait_ge(gated, gi * (BK + 2) + q - 3)
                        last = nc.tensor.transpose(g.bank[q % 4][:, i % 4 * P:(i % 4 + 1) * P], wide[:, i // G, i % G, :], g.ident[:, :])
                        if i % 4 == 3 or i == BLOCKS - 1:
                            last.then_inc(spread, 1)
                    for s, (t0, n) in enumerate(SUBS):
                        for t in range(n):
                            last = nc.tensor.transpose(g.bank[6 + s][0:EXPERTS, t * P:(t + 1) * P], chosen[:, t0 + t, :], g.ident[:, :])
                        last.then_inc(spread, 1)
                    pe.wait_ge(gated, (gi + 1) * (BK + 2))
                    for q in range(4):
                        nc.tensor.matmul(g.bank[q][:, :], zero[:, 0:P], zero[:, :], start=True, stop=False)
                    for t in range(G):
                        nc.tensor.matmul(g.bank[t // 2][:, t % 2 * D:(t % 2 + 1) * D], chosen_t[:, t * P:(t + 1) * P], b2[:, :], start=False, stop=False)

                    def up(f):
                        for s, (t0, n) in enumerate(SUBS):
                            k = 2 * f + s
                            pe.wait_ge(h_raw, gi * (2 * FT) + k + 1)
                            for c in (0, 1):
                                last = nc.tensor.matmul(g.bank[4 + k % 4][:, 0:n * P].rearrange("p (t n) -> p t n", n=P), w1[:, c, f * P:(f + 1) * P],
                                                        xt[:, t0:t0 + n, c, :], start=c == 0, stop=c == 1)
                            last.then_inc(h_made, 1)

                    def down(f):
                        for s, (t0, n) in enumerate(SUBS):
                            k = 2 * f + s
                            pe.wait_ge(h_ready, gi * (2 * FT) + k + 5)
                            for t in range(n):
                                last = nc.tensor.matmul(g.bank[(t0 + t) // 2][:, (t0 + t) % 2 * D:((t0 + t) % 2 + 1) * D], hidden[:, k % 4, t * P:(t + 1) * P],
                                                        w2[:, f, :], start=False,
                                                        stop=f == FT - 1 and ((t0 + t) % 2 == 1 or t0 + t == G - 1))
                            last.then_inc(h_used, 1)

                    up(0)
                    for f in range(FT):
                        if f + 1 < FT:
                            up(f + 1)
                        down(f)

            @block.scalar
            def _(act):
                act.nop().then_inc(h_raw, 4)
                act.wait_ge(w_in, 16 * (10 if switch else 8))
                with act.Fori(0, NG) as gi:
                    act.activation(ot[:, :], g.acc[:, 0, bass.ds(gi * (G * P), G * P)], ACT.Copy).then_inc(ot_ready, 1)
                    norm.scalar(act, gi)
                    if switch:
                        turned_copies(act, g, xt, turned, gi * 4, xt_ready)
                    else:
                        act.wait_ge(gap_ready, gi + 1)
                        act.activation(rise[:, :], gap[:, :], ACT.Exp).then_inc(gap_exped, 1)
                    BK = -(-BLOCKS // 4)
                    flat = gate[:, :, :].rearrange("p m n -> p (m n)")
                    for q in range(BK):
                        w = min(512, BLOCKS * P - q * 512)
                        act.wait_ge(spread, gi * (BK + 2) + q + 1)
                        act.activation(flat[:, q * 512:q * 512 + w], g.bank[q % 4][:, 0:w], ACT.Copy).then_inc(gated, 1)
                    for s, (t0, n) in enumerate(SUBS):
                        act.wait_ge(spread, gi * (BK + 2) + BK + s + 1)
                        act.activation(chosen_t[:, t0 * P:(t0 + n) * P], g.bank[6 + s][0:EXPERTS, 0:n * P], ACT.Copy).then_inc(gated, 1)
                    for f in range(FT):
                        for s, (t0, n) in enumerate(SUBS):
                            k = 2 * f + s
                            act.wait_ge(h_made, gi * (2 * FT) + k + 1)
                            act.wait_ge(h_ready, gi * (2 * FT) + k + 1)
                            act.activation(raw[:, k % 4, 0:n * P], g.bank[4 + k % 4][:, 0:n * P], ACT.Relu if switch else ACT.Gelu, bias=b1[:, f:f + 1]).then_inc(h_raw, 1)


def make_globals(nc, m, g):
    g.passes = g.lows = g.carried = 0
    g.bank = [m.stack.enter_context(nc.psum_tensor(f"bank{i}", [P, 512], F32)) for i in range(8)]
    g.ident = m.sbuf("ident", [P, P])
    g.ones = m.sbuf("ones", [P, P])
    g.carrier = m.sbuf("carrier", [1, 9])
    g.iota = m.sbuf("iota", [P, P])
    g.pcol = m.sbuf("pcol", [P, 2])
    g.group = m.sbuf("group", [P, B])
    g.select_router = m.sbuf("select_router", [P, HEADS * NE + HEADS])
    g.select = {"gat": g.ones, "router": g.select_router}
    g.dinv = m.sbuf("dinv", [P, NT])
    g.src = m.sbuf("src_of", [P, CH], I16)
    g.rel = m.sbuf("rel", [P, CH], BF16)
    g.keep = m.sbuf("keep", [P, C1])
    g.base = m.sbuf("base", [1, CH], I16)
    g.tile = m.sbuf("tile", [1, CH], I16)
    g.cont_low = m.sbuf("cont_low", [1, CH], BF16)
    g.same_low = m.sbuf("same_low", [1, CH], BF16)
    g.er = m.sbuf("er", [P, (NT + 2) * 3 * HEADS], BF16)
    g.low = g.low0 = None


def run_stage_memory(nc, g, name, memset):
    with nc.Block() as block:
        @block.vector
        def _(dve):
            for t in memset:
                dve.memset(t, 0.0)


def gnn_ffn(nc, *args):
    io = dict(zip(NAMES + ("out",), args))
    for name, shape, dt in (("keys", (1 << SORT_BITS,), I32), ("place", (CH * P,), BF16), ("table_gcn", (NPAD, HID), F32),
                            ("table_gat", (NPAD, D + 4), F32), ("table_router", (NPAD, HEADS * NE + HEADS), F32),
                            ("res", (NPAD, D), F32), ("res2", (NPAD, D), F32), ("xt", (NG, P, 2 * G * P), F32)):
        io[name] = nc.dram_tensor(name, shape, dt, kind="Internal").ap()

    class Shared:
        pass

    g = Shared()
    with ExitStack() as stack:
        m = Memory(nc, stack, "g")
        make_globals(nc, m, g)
        sort_edges(nc, io, g)
        index_edges(nc, io, g)
        g.acc = m.sbuf("acc", [P, 3, WIN])
        run_stage_memory(nc, g, "zero", [g.acc[:, :, :]])
        project(nc, io, g, "gcn")
        gather_pass(nc, io, g, "gcn", io["table_gcn"], 0, C1)
        experts(nc, io, g, "switch")
        for layer in (0, 1):
            project(nc, io, g, f"gat{layer}")
            with ExitStack() as low:
                ml = Memory(nc, low, f"gat{layer}_low")
                g.low, g.low_back = ml.sbuf("low", [B, C1 // B, P], BF16), ml.sbuf("low_back", [B, C1 // B, P], BF16)
                g.low0 = ml.sbuf("low0", [B, C1 // B, P], BF16)
                running_lows(nc, io, g, 0, C1, 1)
                gather_pass(nc, io, g, "gat", io["table_gat"], 0, C1)
        project(nc, io, g, "router")
        with ExitStack() as low:
            ml = Memory(nc, low, "router_low")
            g.low, g.low_back = ml.sbuf("low", [B * HEADS, C2 // B, P], BF16), ml.sbuf("low_back", [B * HEADS, C2 // B, P], BF16)
            g.low0 = ml.sbuf("low0", [B * HEADS, C2 // B, P], BF16)
            running_lows(nc, io, g, C1, C2, HEADS)
            gather_pass(nc, io, g, "router", io["table_router"], C1, C2)
        experts(nc, io, g, "top2")


_INS = ("x", "src", "dst", "L0_gnn_W_conv", "L0_gnn_b_conv", "L0_gnn_W_lin", "L0_gnn_b_lin", "L0_ffn_router_w",
        "L0_ffn_router_b", "L0_ffn_W1", "L0_ffn_b1", "L0_ffn_W2", "L0_ffn_b2", "L1_gnn_W", "L1_gnn_attn_l",
        "L1_gnn_attn_r", "L1_gnn_bias", "L1_ffn_W_gat", "L1_ffn_att_src", "L1_ffn_att_dst", "L1_ffn_b_gat",
        "L1_ffn_ln_gamma", "L1_ffn_ln_beta", "L1_ffn_W1", "L1_ffn_b1", "L1_ffn_W2", "L1_ffn_b2", "L1_ffn_edge_index")
NAMES = ("x", "src", "dst", "W_conv", "b_conv", "W_lin", "b_lin", "router_w", "router_b", "s_W1", "s_b1", "s_W2", "s_b2",
         "W", "attn_l", "attn_r", "bias", "W_gat", "att_src", "att_dst", "b_gat", "ln_gamma", "ln_beta",
         "t_W1", "t_b1", "t_W2", "t_b2", "edges")


def kernel(**inputs):
    import numpy as _np
    import concourse.bacc as _bacc
    from concourse import mybir as _mybir
    from concourse.bass_utils import run_bass_kernel_spmd as _run

    nc = _bacc.Bacc("TRN2", target_bir_lowering=False, num_devices=1)
    arrays, args = {}, []
    for name in _INS:
        a = _np.ascontiguousarray(inputs[name])
        if name == "x":
            a = _np.concatenate([a, _np.zeros((NPAD - a.shape[0], a.shape[1]), a.dtype)])
        elif name.endswith("ffn_W1"):
            a = _np.ascontiguousarray(a.transpose(1, 0, 2).reshape(D, -1))
        elif name.endswith("ffn_b1"):
            a = _np.ascontiguousarray(a.reshape(-1, P).T)
        arrays[f"in_{name}_dram"] = a
        args.append(nc.dram_tensor(f"in_{name}_dram", a.shape, _mybir.dt.from_np(a.dtype), kind="ExternalInput").ap())
    args.append(nc.dram_tensor("out_0_dram", (NPAD, D), F32, kind="ExternalOutput").ap())
    gnn_ffn(nc, *args)
    r = _run(nc, [arrays], core_ids=[0])
    return r.results[0]["out_0_dram"][:N_NODES]
```

```python
import numpy as np
from contextlib import ExitStack

import concourse.bass as bass
import concourse.mybir as mybir

P = 128
N_NODES = 6250
D = 256
NT = -(-N_NODES // P)
NPAD = NT * P
G = 7
NG = NT // G
HID = 128
EXPERTS, EH = 32, 64
FH = EXPERTS * EH
FT = FH // P
HEADS, NE = 4, 4
MH = 2 * D
E1, E2 = 100000, 131072
B = 32
SB = 13
MASK = (1 << SB) - 1
KEY1 = 0x40000000
KEY2 = KEY1 | 1 << (2 * SB)
LAST = 0x4FFFFFFF
SORT_BITS = 18
F = (1 << SORT_BITS) // P
C1 = B * -(-(E1 + NPAD) // (B * P))
C2 = B * -(-(E2 + NPAD) // (B * P))
FILL1 = C1 * P - E1 - NPAD
CH = C1 + C2
EP1 = 125
EF1, EF2 = E1 // EP1, E2 // P
WIN = NPAD + P
LOW = -1e30
EPS = 1e-5
RQ = 8
GH = 16
POOL_GROUPS = 26
assert C1 * P + E2 + NPAD <= 1 << SORT_BITS and CH <= F and FILL1 % 2 == 0 and NT % G == 0
assert EF1 + EF2 + 2 * NT + 2 <= F and C1 // B % 2 == 0 and C2 // B % 2 == 0

F32 = mybir.dt.float32
BF16 = mybir.dt.bfloat16
I32 = mybir.dt.int32
I16 = mybir.dt.int16
U32 = mybir.dt.uint32
ALU = mybir.AluOpType
ACT = mybir.ActivationFunctionType
AX = mybir.AxisListType.X
EDVE = mybir.EngineType.DVE


class Memory:

    def __init__(self, nc, stack, stage):
        self.nc, self.stack, self.stage = nc, stack, stage
        self.sems = []
        if stage != "g":
            stack.callback(self.give_back)

    def sbuf(self, name, shape, dt=F32):
        return self.stack.enter_context(self.nc.sbuf_tensor(f"{self.stage}_{name}", shape, dt))

    def sem(self, name):
        s = self.nc.alloc_semaphore(name=f"{self.stage}_{name}")
        self.sems.append(s)
        return s

    def give_back(self):
        if not self.sems:
            return
        self.nc.clear_and_free_semaphores(self.sems)
        self.nc.all_engine_barrier()


def wait_alone(pool, g, sem, value):
    pool.wait_ge(sem, value)
    g.carried = g.carried % 32 + 1
    pool.tensor_tensor(g.carrier[:, g.carried:g.carried + 1], g.carrier[:, 0:1], g.carrier[:, 0:1], ALU.mult)


def sort_plan():
    fb = F.bit_length() - 1
    plan = []
    for k in range(1, SORT_BITS + 1):
        if k > fb:
            plan.append(("sign", k))
            plan.append(("flip",))
            for j in range(k - 1, fb - 1, -1):
                plan.append(("swap", None, j - fb, P))
            plan.append(("flip",))
        elif k == fb:
            plan.append(("sign", k))
        for j in range(min(k, fb) - 1, -1, -1):
            plan.append(("swap", k if k < fb else None, j, F))
    return plan


def swap_views(x, k, j, width):
    d = 1 << j
    if k is None:
        v = x.rearrange("p (a h d) -> p a h d", h=2, d=d)
        return [(v[:, :, 0, :], v[:, :, 1, :], True)]
    m = 1 << (k - j - 1)
    v = x.rearrange("p (a u m h d) -> p a u m h d", u=2, m=m, h=2, d=d)
    return [(v[:, :, u, :, 0, :], v[:, :, u, :, 1, :], u == 0) for u in (0, 1)]


def sort_edges(nc, io, g):
    with ExitStack() as stack:
        m = Memory(nc, stack, "sort")
        e1s, e1d = m.sbuf("e1s", [EP1, EF1], I32), m.sbuf("e1d", [EP1, EF1], I32)
        e2s, e2d = m.sbuf("e2s", [P, EF2], I32), m.sbuf("e2d", [P, EF2], I32)
        node = m.sbuf("node", [P, NT], I32)
        keys = [m.sbuf("keys_a", [P, F]), m.sbuf("keys_b", [P, F])]
        part = m.sbuf("part", [P, 1], I32)
        head = m.sbuf("head", [P, 1], I32)
        heads = m.sbuf("heads", [P, HEADS * NE + HEADS], I32)
        bits = m.sbuf("bits", [P, 9], I32)
        sign = m.sbuf("sign", [P, 9])
        flipsign = m.sbuf("flipsign", [P, 9])
        lo, hi = m.sbuf("lo", [EP1, EF1], I32), m.sbuf("hi", [EP1, EF1], I32)
        digit = m.sbuf("digit", [EP1, 2, 2, GH])
        oh_lo, oh_hi = m.sbuf("oh_lo", [EP1, 2, GH, P], BF16), m.sbuf("oh_hi", [EP1, 2, GH, NT], BF16)
        digit2 = m.sbuf("digit2", [EP1, 2, 2, GH])
        oh_lo2, oh_hi2 = m.sbuf("oh_lo2", [EP1, 2, GH, P], BF16), m.sbuf("oh_hi2", [EP1, 2, GH, NT], BF16)
        iotab = m.sbuf("iotab", [P, P], BF16)
        onehots2, counted2 = m.sem("onehots2"), m.sem("counted2")
        zero = m.sbuf("zero", [P, P], BF16)
        degree = m.sbuf("degree", [P, 3, NT])
        edges_in = m.sem("edges_in")
        made = m.sem("made")
        split = m.sem("split")
        step = m.sem("sort_step")
        flipped = m.sem("flipped")
        copied = m.sem("copied")
        onehots = m.sem("onehots")
        digits = m.sem("digits")
        counted = m.sem("counted")
        stored = m.sem("keys_stored")
        degree_sum, degree_done = m.sem("degree_sum"), m.sem("degree_done")
        plan = sort_plan()
        n_groups = EF1 // GH
        dve_groups = n_groups - POOL_GROUPS
        done = {}
        end = {}

        with nc.Block() as block:
            @block.gpsimd
            def _(pool):
                pool.memset(g.carrier[:, :], 1.0).then_inc(made, 1)
                pool.iota(node[:, :], [[1, NT]], base=0, channel_multiplier=NT).then_inc(made, 1)
                pool.iota(part[:, :], [[0, 1]], base=0, channel_multiplier=1).then_inc(made, 1)
                pool.iota(g.iota[:, :], [[1, P]], base=0, channel_multiplier=0, allow_small_or_imprecise_dtypes=True).then_inc(made, 1)
                pool.memset(g.ones[:, :], 1.0).then_inc(made, 1)
                pool.memset(zero[:, :], 0.0).then_inc(made, 1)
                pool.memset(g.ident[:, :], 0.0).then_inc(made, 1)
                pool.memset(g.group[:, :], 1.0).then_inc(made, 1)
                pool.iota(heads[:, 0:HEADS * NE], [[1, HEADS], [0, NE]], base=0, channel_multiplier=0).then_inc(made, 1)
                pool.iota(heads[:, HEADS * NE:], [[1, HEADS]], base=0, channel_multiplier=0).then_inc(made, 1)
                pool.wait_ge(made, 10)
                pool.affine_select(out=g.ident[:, :], in_=g.ident[:, :], compare_op=ALU.not_equal, fill=1.0, base=0,
                                   pattern=[[-1, P]], channel_multiplier=1).then_inc(made, 1)
                pool.affine_select(out=g.group[:, :], in_=g.group[:, :], compare_op=ALU.is_ge, fill=0.0, base=0,
                                   pattern=[[-HEADS, B]], channel_multiplier=1).then_inc(made, 1)
                pool.wait_ge(made, 12)
                pool.affine_select(out=g.group[:, :], in_=g.group[:, :], compare_op=ALU.is_ge, fill=0.0, base=HEADS - 1,
                                   pattern=[[HEADS, B]], channel_multiplier=-1).then_inc(made, 1)
                pool.wait_ge(split, 2)
                with pool.Fori(0, POOL_GROUPS // 2) as it:
                    for s in (0, 1):
                        i = it * 2 + s
                        wait_alone(pool, g, counted, i + 2)
                        cols = bass.ds(i * GH, GH)
                        pool.tensor_copy(digit[:, s, 0, :], lo[:, cols]).then_inc(digits, 1)
                        pool.tensor_copy(digit[:, s, 1, :], hi[:, cols]).then_inc(digits, 1)
                        wait_alone(pool, g, digits, i * 2 + 2)
                        for q in range(GH):
                            pool.tensor_scalar(oh_lo[:, s, q, :], g.iota[0:EP1, :], digit[:, s, 0, q:q + 1], None, ALU.is_equal)
                            last = pool.tensor_scalar(oh_hi[:, s, q, :], g.iota[0:EP1, 0:NT], digit[:, s, 1, q:q + 1], None, ALU.is_equal)
                        last.then_inc(onehots, 1)

            @block.vector
            def _(dve):
                n = [0]

                def did(ins):
                    n[0] += 1
                    ins.then_inc(step, 1)

                def after():
                    dve.wait_ge(step, n[0])

                k0 = keys[0][:, :].bitcast(I32)
                did(dve.memset(k0, LAST))
                dve.wait_ge(edges_in, 4 * 16)
                dve.tensor_scalar(lo[:, :], e1d[:, :], P - 1, None, ALU.bitwise_and).then_inc(split, 1)
                dve.tensor_scalar(hi[:, :], e1d[:, :], 7, None, ALU.logical_shift_right).then_inc(split, 1)
                dve.wait_ge(made, 10)
                did(dve.tensor_copy(iotab[:, :], g.iota[:, :]))
                after()
                c = 0
                spans = []
                for s, d in ((e1s, e1d), (e2s, e2d)):
                    did(dve.tensor_tensor(s[:, :], s[:, :], d[:, :], ALU.subtract))
                after()
                for s in (e1s, e2s):
                    did(dve.tensor_scalar(s[:, :], s[:, :], MASK, None, ALU.bitwise_and))
                after()
                for s, d, rows, w, key in ((e1s, e1d, EP1, EF1, KEY1), (e2s, e2d, P, EF2, KEY2)):
                    did(dve.scalar_tensor_tensor(out=k0[0:rows, c:c + w], in0=d[:, :], scalar=SB, in1=s[:, :],
                                                 op0=ALU.logical_shift_left, op1=ALU.bitwise_or))
                    spans.append((rows, c, w, key))
                    c += w
                dve.wait_ge(made, 3)
                for key in (KEY1, KEY2):
                    did(dve.tensor_scalar(k0[:, c:c + NT], node[:, :], SB, None, ALU.logical_shift_left))
                    spans.append((P, c, NT, key))
                    c += NT
                did(dve.memset(k0[0:FILL1 // 2, c:c + 2], KEY1 | ((1 << 2 * SB) - 1)))
                after()
                for rows, c, w, key in spans:
                    did(dve.tensor_scalar(k0[0:rows, c:c + w], k0[0:rows, c:c + w], key, None, ALU.bitwise_or))
                for b in range(9):
                    did(dve.tensor_scalar(bits[:, b:b + 1], part[:, :], b, 1, ALU.logical_shift_right, ALU.bitwise_and))
                after()
                dve.wait_ge(made, 10)
                did(dve.tensor_scalar(head[:, :], part[:, :], HEADS - 1, None, ALU.bitwise_and))
                after()
                did(dve.tensor_tensor(g.select_router[:, :], heads[:, :], head[:, :].broadcast_to([P, HEADS * NE + HEADS]), ALU.is_equal))
                did(dve.tensor_scalar(sign[:, :], bits[:, :], -2.0, 1.0, ALU.mult, ALU.add))
                after()
                did(dve.tensor_tensor(flipsign[:, 1:9], sign[:, 0:8], sign[:, 1:9], ALU.mult))
                did(dve.tensor_copy(flipsign[:, 0:1], sign[:, 0:1]))
                after()
                at, flips = 0, 0
                fb = F.bit_length() - 1
                for i, s in enumerate(plan):
                    x, y = keys[at], keys[1 - at]
                    if s[0] == "swap":
                        _, k, j, width = s
                        for (xl, xh, up), (yl, yh, _) in zip(swap_views(x[:, :], k, j, width), swap_views(y[:, :], k, j, width)):
                            did(dve.tensor_tensor(yl, xl, xh, ALU.min if up else ALU.max))
                            did(dve.tensor_tensor(yh, xl, xh, ALU.max if up else ALU.min))
                    elif s[0] == "sign":
                        b = s[1] - fb
                        did(dve.tensor_scalar(y[:, :], x[:, :], flipsign[:, b:b + 1], None, ALU.mult))
                    else:
                        flips += 1
                        for q in (0, 1):
                            dve.wait_ge(flipped, 4 * (flips - 1) + q + 1)
                            did(dve.tensor_copy(y[:, q * 512:(q + 1) * 512], g.bank[q][:, :]))
                        dve.wait_ge(copied, 2 * flips)
                    after()
                    done[i] = n[0]
                    at = 1 - at
                end.update(at=at, total=n[0])
                with dve.Fori(0, dve_groups // 2) as it:
                    for t in (0, 1):
                        i = it * 2 + t
                        dve.wait_ge(counted2, i + 1)
                        cols = bass.ds((POOL_GROUPS + i) * GH, GH)
                        dve.tensor_copy(digit2[:, t, 0, :], lo[:, cols])
                        dve.tensor_copy(digit2[:, t, 1, :], hi[:, cols])
                        dve.drain()
                        for q in range(GH):
                            dve.tensor_scalar(oh_lo2[:, t, q, :], iotab[0:EP1, :], digit2[:, t, 0, q:q + 1], None, ALU.is_equal)
                            last = dve.tensor_scalar(oh_hi2[:, t, q, :], iotab[0:EP1, 0:NT], digit2[:, t, 1, q:q + 1], None, ALU.is_equal)
                        last.then_inc(onehots2, 1)
                dve.wait_ge(degree_sum, 1)
                dve.tensor_scalar(degree[:, 0, :], g.bank[7][:, 0:NT], 1.0, None, ALU.add).then_inc(degree_done, 1)
                dve.wait_ge(degree_done, 2)
                newton(dve, degree[:, 0, :], degree[:, 1, :], g.dinv[:, :], degree[:, 2, :])

            @block.tensor
            def _(pe):
                pe.wait_ge(made, 12)
                hist = g.bank[7][:, 0:NT]
                nc.tensor.matmul(hist, zero[:, :], zero[:, 0:NT], start=True, stop=False).then_inc(counted, 3)
                pe.nop().then_inc(counted2, 2)
                todo = [POOL_GROUPS // 2]

                def count_some(most):
                    now = min(most, todo[0])
                    if not now:
                        return
                    first = POOL_GROUPS // 2 - todo[0]
                    todo[0] -= now
                    with pe.Fori(first, first + now) as it:
                        for s in (0, 1):
                            i = it * 2 + s
                            pe.wait_ge(onehots, i + 1)
                            for q in range(GH):
                                last = nc.tensor.matmul(hist, oh_lo[:, s, q, :], oh_hi[:, s, q, :], start=False, stop=False)
                            last.then_inc(counted, 1)

                count_some(POOL_GROUPS // 4)
                flips = 0
                at = 0
                for i, s in enumerate(plan):
                    if s[0] == "flip":
                        pe.wait_ge(step, done[i - 1])
                        if flips:
                            pe.wait_ge(copied, 2 * flips)
                        for q in range(4):
                            for r in range(4):
                                c = (4 * q + r) * P
                                last = nc.tensor.transpose(g.bank[q][:, r * P:(r + 1) * P], keys[at][:, c:c + P], g.ident[:, :])
                            last.then_inc(flipped, 1)
                        flips += 1
                        if flips % 2 == 0:
                            count_some(1)
                    at = 1 - at
                count_some(n_groups)
                with pe.Fori(0, dve_groups // 2) as it:
                    for t in (0, 1):
                        i = it * 2 + t
                        pe.wait_ge(onehots2, i + 1)
                        for q in range(GH):
                            last = nc.tensor.matmul(hist, oh_lo2[:, t, q, :], oh_hi2[:, t, q, :], start=False, stop=False)
                        last.then_inc(counted2, 1)
                nc.tensor.matmul(hist, zero[:, :], zero[:, 0:NT], start=False, stop=True).then_inc(degree_sum, 1)

            @block.scalar
            def _(act):
                flips = 0
                at = 0
                for i, s in enumerate(plan):
                    if s[0] == "flip":
                        for q in (2, 3):
                            act.wait_ge(flipped, 4 * flips + q + 1)
                            act.activation(keys[1 - at][:, q * 512:(q + 1) * 512], g.bank[q][:, :], ACT.Copy).then_inc(copied, 1)
                        flips += 1
                    at = 1 - at
                act.wait_ge(degree_done, 1)
                act.activation(degree[:, 1, :], degree[:, 0, :], ACT.Sqrt).then_inc(degree_done, 1)

            @block.sync
            def _(sp):
                sp.dma_start(e1s[:, :], io["src"].rearrange("(p f) -> p f", p=EP1)).then_inc(edges_in, 16)
                sp.dma_start(e1d[:, :], io["dst"].rearrange("(p f) -> p f", p=EP1)).then_inc(edges_in, 16)
                sp.dma_start(e2s[:, :], io["edges"][0].rearrange("(p f) -> p f", p=P)).then_inc(edges_in, 16)
                sp.dma_start(e2d[:, :], io["edges"][1].rearrange("(p f) -> p f", p=P)).then_inc(edges_in, 16)
                sp.wait_ge(step, end["total"])
                sp.dma_start(io["keys"].rearrange("(p f) -> p f", p=P), keys[end["at"]][:, :].bitcast(I32)).then_inc(stored, 16)
                sp.wait_ge(stored, 16)


def index_edges(nc, io, g):
    with ExitStack() as stack:
        m = Memory(nc, stack, "index")
        rows = m.sbuf("nat", [P, F], I32)
        col = m.sbuf("col", [P, F], I32)
        tmp = m.sbuf("tmp", [P, F], I32)
        nodef = m.sbuf("nodef", [P, F])
        ends = m.sbuf("ends", [1, 2, F], I32)
        endf = m.sbuf("endf", [1, 2, F])
        cont = m.sbuf("cont", [1, F])
        loaded, turned, s = m.sem("loaded"), m.sem("turned"), m.sem("step")
        spread, taken = m.sem("spread"), m.sem("taken")
        at = {}
        with nc.Block() as block:
            @block.vector
            def _(dve):
                n = [0]

                def did(ins):
                    n[0] += 1
                    ins.then_inc(s, 1)
                    dve.wait_ge(s, n[0])

                dve.wait_ge(loaded, 48)
                for q in range(4):
                    dve.wait_ge(turned, q + 1)
                    out = col[:, :].bitcast(F32).rearrange("e (p r) -> e r p", r=F // P)[:, 4 * q:4 * q + 4, :]
                    ins = dve.tensor_copy(out, g.bank[q][:, :].rearrange("e (r p) -> e r p", r=4))
                    ins.then_inc(taken, 1)
                dve.wait_ge(taken, 4)
                did(dve.tensor_scalar(tmp[:, :], col[:, :], MASK, None, ALU.bitwise_and))
                did(dve.tensor_scalar(col[:, :], col[:, :], SB, MASK, ALU.logical_shift_right, ALU.bitwise_and))
                did(dve.tensor_tensor(tmp[:, :], tmp[:, :], col[:, :], ALU.add))
                did(dve.tensor_scalar(tmp[:, :], tmp[:, :], MASK, None, ALU.bitwise_and))
                did(dve.tensor_scalar(g.src[:, :], tmp[:, 0:CH], float(N_NODES - 1), None, ALU.min))
                did(dve.tensor_copy(nodef[:, :], col[:, :]))
                did(dve.tensor_scalar(ends[:, :, :], ends[:, :, :], SB, MASK, ALU.logical_shift_right, ALU.bitwise_and))
                did(dve.tensor_copy(endf[:, :, :], ends[:, :, :]))
                did(dve.memset(cont[:, 0:1], 0.0))
                did(dve.tensor_tensor(cont[:, 1:F], endf[:, 0, 1:F], endf[:, 1, 0:F - 1], ALU.is_equal))
                did(dve.memset(g.cont_low[:, 0:1], LOW))
                did(dve.tensor_tensor(endf[:, 0, 1:F], endf[:, 1, 1:F], endf[:, 1, 0:F - 1], ALU.not_equal))
                did(dve.tensor_scalar(g.same_low[:, 1:CH], endf[:, 0, 1:CH], LOW, None, ALU.mult))
                did(dve.memset(g.same_low[:, 0:1], LOW))
                did(dve.tensor_scalar(g.cont_low[:, 1:CH], cont[:, 1:CH], -LOW, LOW, ALU.mult, ALU.add))
                did(dve.tensor_scalar(g.base[:, :], ends[:, 0, 0:CH], float(NPAD), None, ALU.min))
                did(dve.tensor_copy(endf[:, 0, 0:CH], g.base[:, :]))
                at.update(flags=n[0])
                for q in range(4):
                    w = min(512, CH - q * 512)
                    dve.wait_ge(spread, q + 1)
                    dve.tensor_tensor(g.rel[:, q * 512:q * 512 + w], nodef[:, q * 512:q * 512 + w], g.bank[q][:, 0:w], ALU.subtract).then_inc(taken, 1)
                for q in range(-(-C1 // 512)):
                    w = min(512, C1 - q * 512)
                    dve.wait_ge(spread, q + 5)
                    dve.tensor_copy(g.keep[:, q * 512:q * 512 + w], g.bank[q][:, 0:w]).then_inc(taken, 1)

            @block.sync
            def _(sp):
                sp.dma_start(rows[:, :], io["keys"].rearrange("(p f) -> p f", p=P)).then_inc(loaded, 16)
                chunks = io["keys"].rearrange("(c e) -> c e", e=P)
                with nc.allow_non_contiguous_dma(reason="one key of each chunk"):
                    sp.dma_start(ends[:, 0, :], chunks[:, 0:1].rearrange("c e -> e c")).then_inc(loaded, 16)
                    sp.dma_start(ends[:, 1, :], chunks[:, P - 1:P].rearrange("c e -> e c")).then_inc(loaded, 16)

            @block.tensor
            def _(pe):
                pe.wait_ge(loaded, 48)
                natf = rows[:, :].bitcast(F32)
                for q in range(4):
                    for r in range(4):
                        c = (4 * q + r) * P
                        last = nc.tensor.transpose(g.bank[q][:, r * P:(r + 1) * P], natf[:, c:c + P], g.ident[:, :])
                    last.then_inc(turned, 1)
                pe.wait_ge(s, at["flags"])
                for q in range(4):
                    pe.wait_ge(taken, 4 + q)
                    nc.tensor.matmul(g.bank[q][:, :], g.ones[0:1, :], endf[0:1, 0, q * 512:(q + 1) * 512], start=True, stop=True).then_inc(spread, 1)
                for q in range(-(-C1 // 512)):
                    pe.wait_ge(taken, 8 + q)
                    nc.tensor.matmul(g.bank[q][:, :], g.ones[0:1, :], cont[0:1, q * 512:(q + 1) * 512], start=True, stop=True).then_inc(spread, 1)


def running_lows(nc, io, g, c0, n_chunks, H):
    nb, HP = n_chunks // B, B * H
    with ExitStack() as stack:
        m = Memory(nc, stack, f"low{g.lows}")
        g.lows += 1
        krow = m.sbuf("krow", [HP, nb, P], I32)
        krowf = m.sbuf("krowf", [HP, nb, P])
        other = m.sbuf("other", [HP, nb, P])
        delta = m.sbuf("delta", [HP, nb, P], I32)
        key_in, s = m.sem("key_in"), m.sem("step")
        with nc.Block() as block:
            @block.sync
            def _(sp):
                keys_of = io["keys"][c0 * P:(c0 + n_chunks) * P].rearrange("(b j e) -> j b e", j=B, e=P)
                for h in range(H):
                    sp.dma_start(krow[h:HP:H, :, :], keys_of).then_inc(key_in, 16)
            @block.vector
            def _(dve):
                n = [0]

                def did(ins):
                    n[0] += 1
                    ins.then_inc(s, 1)
                    dve.wait_ge(s, n[0])

                did(dve.memset(g.low[:, :, :], LOW))
                did(dve.memset(g.low_back[:, :, :], LOW))
                dve.wait_ge(key_in, 16 * H)
                did(dve.tensor_scalar(delta[:, :, :], krow[:, :, :], MASK, None, ALU.bitwise_and))
                did(dve.tensor_scalar(g.low_own[:, :, :], delta[:, :, :], 0.0, LOW, ALU.not_equal, ALU.mult))
                did(dve.tensor_scalar(krow[:, :, :], krow[:, :, :], SB, MASK, ALU.logical_shift_right, ALU.bitwise_and))
                did(dve.tensor_copy(krowf[:, :, :], krow[:, :, :]))
                did(dve.tensor_tensor(other[:, :, 1:P], krowf[:, :, 1:P], krowf[:, :, 0:P - 1], ALU.not_equal))
                did(dve.tensor_scalar(g.low[:, :, 1:P], other[:, :, 1:P], LOW, None, ALU.mult))
                did(dve.tensor_scalar(g.low_back[:, :, 1:P][:, :, ::-1], other[:, :, 1:P], LOW, None, ALU.mult))
                did(dve.tensor_tensor(other[:, :, :], krowf[:, :, :], krowf[:, :, 0:1].broadcast_to([HP, nb, P]), ALU.not_equal))
                did(dve.tensor_scalar(g.low0[:, :, :], other[:, :, :], LOW, None, ALU.mult))


class WindowStarts:

    def __init__(self, eng, g):
        self.eng, self.base, self.regs, self.loads, self.name = eng, g.base, [], 0, g.passes

    def of(self, chunk, j):
        if j % 8 == 0:
            for r in self.regs:
                self.eng.free_register(r)
            self.loads += 1
            self.regs = [self.eng.alloc_register(f"window{self.name}_{self.loads}_{i}") for i in range(8)]
            self.eng.load(self.regs, self.base[0:1, bass.ds(chunk, 8)])
        return bass.RuntimeValue.of_register_unchecked(self.regs[j % 8], min_val=0, max_val=NPAD)


def gather_pass(nc, io, g, kind, table, c0, n_chunks):
    soft = kind != "gcn"
    H = HEADS if kind == "router" else 1
    HP = B * H
    W = table.shape[1]
    blocks = {"gcn": 1, "gat": 3, "router": 1}[kind]
    OUT = HEADS * NE + HEADS if kind == "router" else P
    score = {"gat": D, "router": HEADS * NE}.get(kind)
    nb = n_chunks // B
    with ExitStack() as stack:
        m = Memory(nc, stack, kind + str(g.passes))
        g.passes += 1
        rows = m.sbuf("rows", [P, 2, B, W])
        index = m.sbuf("index", [P, 2, B], I32)
        rel = m.sbuf("rel_now", [P, 2, B])
        keep = m.sbuf("keep_now", [P, 2, B])
        onehot = m.sbuf("onehot", [P, 4, P])
        first_col = m.sbuf("first_col", [P, 8, blocks])
        idx_set = m.sem("index_set")
        gathered = [m.sem(f"gathered{i}") for i in (0, 1)]
        oh = m.sem("onehot_made")
        summed = m.sem("summed")
        moved = m.sem("moved")
        fixed = m.sem("fixed")
        ready = m.sem("batch_ready")
        if soft:
            low, low_back, low0, low_own = g.low, g.low_back, g.low0, g.low_own
            fwd = m.sbuf("fwd", [P, 2, P])
            top = m.sbuf("top", [HP, P])
            own = m.sbuf("own", [HP, P])
            zz = m.sbuf("zz", [HP, 2, P + 1])
            zl = m.sbuf("zl", [HP, 2, P + 1])
            diff = m.sbuf("diff", [HP, P + 1])
            wrow = m.sbuf("wrow", [P, P + 1])
            wcol = m.sbuf("wcol", [P, 2, HP])
            state = m.sbuf("state", [1, 2, B + 1, H])
            carry = m.sbuf("carry", [1, 2, P])
            cin = m.sbuf("cin", [HP, 2])
            spread = m.sbuf("spread", [P, OUT])
            select = m.sbuf("select", [HP, OUT])
            d2p, p2d = m.sem("dve_to_pe"), m.sem("pe_to_dve")
            d2a, exped = m.sem("dve_to_act"), m.sem("exped")
            if kind == "router":
                pay = m.sbuf("pay", [P, 2, B, OUT])
                els = m.sbuf("els", [P, 2, HP])
        acc = g.acc
        row_ap = table[:, :]

        def chunk(b, j):
            return b * B + j

        SCORES_AT = 17
        PD = 4 if kind == "router" else 3

        def after(it, s):
            return (it, 1) if s == 0 else (it + 1, 0)

        def batches(eng, first, body):
            first()
            with eng.Fori(0, nb // 2 - 1) as it:
                for s in (0, 1):
                    body(it, s, False)
            body(nb // 2 - 1, 0, False)
            body(nb // 2 - 1, 1, True)

        with nc.Block() as block:
            @block.gpsimd
            def _(pool):
                with pool.Fori(0, nb // 2) as it:
                    for s in (0, 1):
                        b = it * 2 + s
                        for q in range(B // RQ):
                            wait_alone(pool, g, summed, b * B + (q + 1) * RQ)
                            if q == 0:
                                pool.tensor_copy(index[:, s, :], g.src[:, bass.ds(b * B + c0, B)]).then_inc(idx_set, 1)
                                wait_alone(pool, g, idx_set, b + 1)
                            for j in range(q * RQ, (q + 1) * RQ):
                                pool.indirect_dma_start(rows[:, s, j, :], None, row_ap,
                                                        bass.IndirectOffsetOnAxis(index[:, s, j:j + 1], 0)).then_inc(gathered[s], 16)

            @block.vector
            def _(dve):
                if soft:
                    dve.memset(state[:, :, 0:1, :], LOW)
                    for t in (fwd[:, :, :], wrow[:, :], spread[:, :], carry[:, :, :]):
                        dve.memset(t, 0.0)
                    dve.drain()

                def ap(t, b):
                    return t[:, bass.ds(b, 1), :].rearrange("q b e -> q (b e)")

                def scores_by_column(it, s):
                    dve.wait_ge(gathered[s], (it + 1) * (16 * B))
                    for k in (0, 1):
                        last = dve.tensor_copy(els[:, k, :].rearrange("p (j h) -> p j h", h=H), rows[:, s, :, score + k * H:score + (k + 1) * H])
                    last.then_inc(d2p, 1)

                el, er = g.bank[4][0:HP, 0:P], g.bank[4][0:HP, P:2 * P]

                def maxima(it, s):
                    b = it * 2 + s
                    dve.wait_ge(p2d, b * 4 + 1)
                    dve.tensor_tensor(own[:, :], er, ap(low_own, b), ALU.add)
                    dve.tensor_tensor_scan(fwd[0:HP, 0, :], ap(low, b), el, LOW, ALU.add, ALU.max)
                    dve.drain()
                    dve.tensor_tensor_scan(fwd[0:HP, 1, :], ap(low, b), own[:, :], LOW, ALU.add, ALU.max).then_inc(d2p, 1)
                    dve.tensor_tensor_scan(top[:, ::-1], ap(low_back, b), fwd[0:HP, 0, ::-1], LOW, ALU.add, ALU.max)

                def carried(it, s):
                    b = it * 2 + s
                    dve.wait_ge(p2d, b * 4 + 2)
                    same = g.same_low[0:1, bass.ds(b * B + c0, B)]
                    for k in (0, 1):
                        lasts = g.bank[6][0:1, k * HP:(k + 1) * HP].rearrange("o (j h) -> o j h", h=H)
                        for h in range(H):
                            dve.tensor_tensor_scan(state[:, k, 1:, h], same, lasts[:, :, h], state[:, k, 0:1, h], ALU.add, ALU.max)
                    dve.drain()
                    cont = g.cont_low[0:1, bass.ds(b * B + c0, B)].unsqueeze(2).broadcast_to([1, B, H])
                    for k in (0, 1):
                        last = dve.tensor_tensor(carry[:, k, 0:HP].rearrange("o (j h) -> o j h", h=H), state[:, k, 0:B, :], cont, ALU.add)
                    last.then_inc(d2p, 1)
                    dve.drain()
                    dve.tensor_copy(state[:, :, 0, :], state[:, :, B, :])

                def exponents(it, s):
                    b = it * 2 + s
                    dve.wait_ge(p2d, b * 4 + 3)
                    dve.tensor_copy(cin[:, :], g.bank[6][0:HP, 256:258])
                    dve.drain()
                    dve.scalar_tensor_tensor(out=own[:, :], in0=ap(low0, b), scalar=cin[:, 1:2], in1=fwd[0:HP, 1, :], op0=ALU.add, op1=ALU.max)
                    dve.scalar_tensor_tensor(out=top[:, :], in0=ap(low0, b), scalar=cin[:, 0:1], in1=top[:, :], op0=ALU.add, op1=ALU.max)
                    dve.drain()
                    dve.tensor_tensor(zz[:, 0, 0:P], el, own[:, :], ALU.add)
                    dve.tensor_tensor(zz[:, 0, P:P + 1], cin[:, 0:1], own[:, 0:1], ALU.add)
                    dve.tensor_tensor(zz[:, 1, 0:P], top[:, :], own[:, :], ALU.add)
                    dve.tensor_tensor(zz[:, 1, P:P + 1], top[:, 0:1], own[:, 0:1], ALU.add)
                    dve.drain()
                    dve.scalar_tensor_tensor(out=zl[:, :, :], in0=zz[:, :, :], scalar=0.2, in1=zz[:, :, :], op0=ALU.mult, op1=ALU.max)
                    dve.drain()
                    dve.tensor_tensor(diff[:, :], zl[:, 0, :], zl[:, 1, :], ALU.subtract).then_inc(d2a, 1)

                def carried_factors(it, s):
                    dve.wait_ge(exped, it * 2 + s + 1)
                    dve.tensor_scalar(spread[0:HP, :], g.select[kind][0:HP, 0:OUT], wrow[0:HP, P:P + 1], None, ALU.mult).then_inc(d2p, 1)

                def weights(it, s):
                    b = it * 2 + s
                    if soft:
                        dve.wait_ge(p2d, b * 4 + 4)
                        dve.tensor_copy(wcol[:, s, :], g.bank[6][:, 0:HP])
                        dve.tensor_copy(keep[0:OUT, s, :], g.bank[6][0:OUT, 128:128 + B])
                    else:
                        dve.tensor_copy(keep[:, s, :], g.keep[:, bass.ds(b * B + c0, B)])
                    dve.tensor_copy(rel[:, s, :], g.rel[:, bass.ds(b * B + c0, B)])
                    dve.drain()

                def payload(it, s):
                    w4 = wcol[:, s, :].rearrange("p (j h) -> p j h", h=H)
                    dve.tensor_tensor(pay[:, s, :, 0:HEADS * NE].rearrange("p j (h x) -> p j h x", h=H),
                                      rows[:, s, :, 0:HEADS * NE].rearrange("p j (h x) -> p j h x", h=H),
                                      w4.unsqueeze(3).broadcast_to([P, B, H, NE]), ALU.mult)
                    dve.tensor_copy(pay[:, s, :, HEADS * NE:OUT], w4).then_inc(ready, 1)

                steps = {}
                if soft:
                    if kind == "router":
                        steps[SCORES_AT] = scores_by_column
                    for k, step in enumerate((maxima, carried, exponents, carried_factors)):
                        steps[SCORES_AT + 2 + 2 * k] = step
                steps[B - 4] = weights
                if kind == "router":
                    steps[B - 3] = payload

                def first():
                    for j in sorted(steps):
                        steps[j](0, 0)

                starts = WindowStarts(dve, g)

                def fix(it, s, j):
                    c = (it * 2 + s) * B + j
                    at = starts.of(c + c0, j)
                    dve.wait_ge(moved, c + 5)
                    dve.wait_ge(fixed, c + 8)
                    a = acc[0:OUT, 0:blocks, bass.ds(at, 1)].rearrange("p k o -> p (k o)")
                    dve.scalar_tensor_tensor(out=a, in0=a, scalar=keep[0:OUT, s, j:j + 1], in1=first_col[0:OUT, j % 8, :],
                                             op0=ALU.mult, op1=ALU.add).then_inc(fixed, 1)

                def body(it, s, last):
                    for j in range(B):
                        if not last and j in steps:
                            steps[j](*after(it, s))
                        c = (it * 2 + s) * B + j
                        dve.wait_ge(summed, c + 2 * B - 3)
                        if kind == "gat":
                            dve.tensor_scalar(onehot[:, j % 4, :], g.iota[:, :], rel[:, s, j:j + 1], wcol[:, s, j:j + 1], ALU.is_equal, ALU.mult).then_inc(oh, 1)
                        else:
                            dve.tensor_scalar(onehot[:, j % 4, :], g.iota[:, :], rel[:, s, j:j + 1], None, ALU.is_equal).then_inc(oh, 1)
                        if j >= 3:
                            fix(it, s, j - 3)
                    for j in range(B - 3, B):
                        fix(it, s, j)

                batches(dve, first, body)

            @block.tensor
            def _(pe):
                pe.nop().then_inc(summed, 2 * B)

                def scores_by_row(it, s):
                    pe.wait_ge(gathered[s], (it + 1) * (16 * B))
                    if kind == "router":
                        pe.wait_ge(d2p, (it * 2 + s) * PD + 1)
                    for k in (0, 1):
                        last = nc.tensor.transpose(g.bank[4][0:HP, k * P:(k + 1) * P],
                                                   els[:, k, :] if kind == "router" else rows[:, s, :, score + k], g.ident[:, :])
                    last.then_inc(p2d, 1)

                def lasts_in_row(it, s):
                    pe.wait_ge(d2p, (it * 2 + s) * PD + PD - 2)
                    for k in (0, 1):
                        last = nc.tensor.matmul(g.bank[6][0:1, k * HP:(k + 1) * HP], fwd[:, k, P - 1:P], g.ident[:, 0:HP], start=True, stop=True)
                    last.then_inc(p2d, 1)

                def carried_in_column(it, s):
                    pe.wait_ge(d2p, (it * 2 + s) * PD + PD - 1)
                    for k in (0, 1):
                        last = nc.tensor.matmul(g.bank[6][:, 256 + k:257 + k], carry[:, k, :], g.ones[0:1, 0:1], start=True, stop=True)
                    last.then_inc(p2d, 1)

                def weights_by_edge(it, s):
                    pe.wait_ge(d2p, (it * 2 + s) * PD + PD)
                    nc.tensor.transpose(g.bank[6][:, 0:P], wrow[:, 0:P], g.ident[:, :])
                    grouping = g.group if kind == "router" else g.ident
                    nc.tensor.matmul(g.bank[6][0:OUT, 128:128 + B], spread[:, :], grouping[:, 0:B], start=True, stop=True).then_inc(p2d, 1)

                steps = {}
                if soft:
                    steps[SCORES_AT + 1] = scores_by_row
                    steps[SCORES_AT + 3] = lasts_in_row
                    steps[SCORES_AT + 5] = carried_in_column
                    steps[SCORES_AT + 9] = weights_by_edge

                def first():
                    for j in sorted(steps):
                        steps[j](0, 0)

                def body(it, s, last_batch):
                    b = it * 2 + s
                    if not soft:
                        pe.wait_ge(gathered[s], (it + 1) * (16 * B))
                    if kind == "router":
                        pe.wait_ge(ready, b + 1)
                    for j in range(B):
                        if not last_batch and j in steps:
                            steps[j](*after(it, s))
                        c = b * B + j
                        pe.wait_ge(oh, c + 1)
                        pe.wait_ge(moved, c + 1)
                        out = g.bank[j % 4]
                        if kind == "router":
                            last = nc.tensor.matmul(out[0:OUT, 0:P], pay[:, s, j, :], onehot[:, j % 4, :], start=True, stop=True)
                        else:
                            for k in range(min(blocks, 2)):
                                last = nc.tensor.matmul(out[:, k * P:(k + 1) * P], rows[:, s, j, k * P:(k + 1) * P], onehot[:, j % 4, :], start=True, stop=True)
                            if blocks == 3:
                                last = nc.tensor.matmul(out[:, 2 * P:3 * P], g.ones[:, :], onehot[:, j % 4, :], start=True, stop=True)
                        last.then_inc(summed, 1)

                batches(pe, first, body)

            @block.scalar
            def _(act):
                act.nop().then_inc(moved, 4)
                act.nop().then_inc(fixed, 8)
                if soft:
                    act.preload_act_table(ACT.Exp)

                def exps(it, s):
                    act.wait_ge(d2a, it * 2 + s + 1)
                    act.activation(wrow[0:HP, :], diff[:, :], ACT.Exp).then_inc(exped, 1)

                steps = {SCORES_AT + 7: exps} if soft else {}

                def first():
                    for j in sorted(steps):
                        steps[j](0, 0)

                starts = WindowStarts(act, g)

                def body(it, s, last):
                    for j in range(B):
                        if not last and j in steps:
                            steps[j](*after(it, s))
                        c = (it * 2 + s) * B + j
                        at = starts.of(c + c0, j)
                        act.wait_ge(summed, c + 2 * B + 1)
                        act.wait_ge(fixed, c + 1)
                        src = g.bank[j % 4][0:OUT, 0:blocks * P].rearrange("p (k n) -> p k n", k=blocks)
                        act.activation(first_col[0:OUT, j % 8, :], src[:, :, 0], ACT.Copy)
                        act.wait_ge(moved, c + 4)
                        act.activation(acc[0:OUT, 0:blocks, bass.ds(at + 1, P - 1)], src[:, :, 1:P], ACT.Copy).then_inc(moved, 1)

                batches(act, first, body)


class Normaliser:

    def __init__(self, m):
        self.parts = m.sbuf("ln_parts", [P, G, 6])
        self.mv = m.sbuf("ln_mv", [P, G, 2])
        self.var = m.sbuf("ln_var", [P, G])
        self.root = m.sbuf("ln_root", [P, G])
        self.inv = m.sbuf("ln_inv", [P, G])
        self.tmp = m.sbuf("ln_tmp", [P, G])
        self.var_ready, self.root_ready = m.sem("var_ready"), m.sem("root_ready")

    def vector(self, dve, x, out, gi, done):
        for t in range(G):
            dve.bn_stats(self.parts[:, t, :], x[:, t, :])
        dve.drain()
        for t in range(G):
            dve.bn_aggr(self.mv[:, t, :], self.parts[:, t, :])
        dve.drain()
        dve.tensor_scalar(self.var[:, :], self.mv[:, :, 1], EPS, None, ALU.add).then_inc(self.var_ready, 1)
        dve.drain()
        dve.wait_ge(self.root_ready, gi + 1)
        newton(dve, self.var[:, :], self.root[:, :], self.inv[:, :], self.tmp[:, :])
        for t in range(G):
            last = dve.tensor_scalar(out[:, t, :], x[:, t, :], self.mv[:, t, 0:1], self.inv[:, t:t + 1], ALU.subtract, ALU.mult)
        last.then_inc(done, 1)

    def scalar(self, act, gi):
        act.wait_ge(self.var_ready, gi + 1)
        act.activation(self.root[:, :], self.var[:, :], ACT.Sqrt).then_inc(self.root_ready, 1)


def newton(dve, var, root, inv, tmp):
    dve.reciprocal(inv, root)
    dve.drain()
    dve.tensor_tensor(tmp, inv, inv, ALU.mult)
    dve.drain()
    dve.tensor_tensor(tmp, tmp, var, ALU.mult)
    dve.drain()
    dve.tensor_scalar(tmp, tmp, -0.5, 1.5, ALU.mult, ALU.add)
    dve.drain()
    dve.tensor_tensor(inv, inv, tmp, ALU.mult)
    dve.drain()


def turn(nc, g, x, turned):
    for i in range(2 * G):
        t, c = divmod(i, 2)
        last = nc.tensor.transpose(g.bank[i // 4][:, i % 4 * P:(i % 4 + 1) * P], x[:, t, c * P:(c + 1) * P], g.ident[:, :])
        if i % 4 == 3 or i == 2 * G - 1:
            last.then_inc(turned, 1)


def turned_copies(act, g, out, turned, before, done):
    flat = out[:, :, :, :].rearrange("p t c n -> p (t c n)")
    for q in range(4):
        w = min(512, 2 * G * P - q * 512)
        act.wait_ge(turned, before + q + 1)
        last = act.activation(flat[:, q * 512:q * 512 + w], g.bank[q][:, 0:w], ACT.Copy)
    last.then_inc(done, 1)


def project(nc, io, g, kind):
    from_acc = kind in ("gat1", "router")
    loads_x = kind != "gat1"
    H = HEADS if kind == "router" else 1
    M = {"gcn": HID, "gat0": D, "gat1": D, "router": HEADS * NE}[kind]
    OUT = M if kind == "gcn" else M + 2 * H
    table = io["table_" + {"gcn": "gcn", "router": "router"}.get(kind, "gat")]
    TW = table.shape[1]
    x_rows = {"gcn": io["x"], "gat0": io["res"], "router": io["res"]}.get(kind)
    layer = {"gat0": 0, "gat1": 1}.get(kind)
    with ExitStack() as stack:
        m = Memory(nc, stack, "project_" + kind)
        x = m.sbuf("x", [P, G, D])
        xn = m.sbuf("xn", [P, G, D])
        xt = m.sbuf("xt", [P, G, 2, P])
        wt = m.sbuf("wt", [P, 2, OUT])
        trow = m.sbuf("trow", [P, G, TW])
        norm = Normaliser(m)
        w_in, w_done, x_in = m.sem("w_in"), m.sem("w_done"), m.sem("x_in")
        xn_ready, turned, xt_ready = m.sem("xn_ready"), m.sem("turned"), m.sem("xt_ready")
        made, taken, stored = m.sem("made"), m.sem("taken"), m.sem("stored")
        stores = 48 if kind == "router" else 16
        loads = 1
        if kind == "gcn":
            dn = m.sbuf("dn", [P, G])
        else:
            att = m.sbuf("att", [P, 2, M])
            prod = m.sbuf("prod", [P, 2, M])
            loads = 3
        if from_acc:
            inv_den = m.sbuf("inv_den", [P, G * P])
            ot = m.sbuf("ot", [P, 2, G * P])
            bias = m.sbuf("bias", [P, 2])
            scaled, ot_ready, back, out_ready = m.sem("scaled"), m.sem("ot_ready"), m.sem("back"), m.sem("out_ready")
            loads = 5

        with nc.Block() as block:
            @block.sync
            def _(sp):
                w = {"gcn": io["W_conv"], "router": io["W_gat"]}.get(kind)
                w = io["W"][layer] if w is None else w
                sp.dma_start(wt[:, :, 0:M], w.rearrange("(c p) n -> p c n", p=P)).then_inc(w_in, 16)
                if kind != "gcn":
                    al, ar = (io["att_src"], io["att_dst"]) if kind == "router" else (io["attn_l"][layer], io["attn_r"][layer])
                    flat = (lambda a: a.rearrange("h x -> (h x)")) if kind == "router" else (lambda a: a)
                    sp.dma_start(att[:, 0, :], flat(al).partition_broadcast(P)).then_inc(w_in, 16)
                    sp.dma_start(att[:, 1, :], flat(ar).partition_broadcast(P)).then_inc(w_in, 16)
                if from_acc:
                    b = io["bias"][1 if kind == "router" else 0]
                    for c in (0, 1):
                        sp.dma_start(bias[:, c:c + 1], b[c * P:(c + 1) * P].rearrange("(p o) -> p o", o=1)).then_inc(w_in, 16)
                sp.nop().then_inc(stored, stores)
                with sp.Fori(0, NG) as gi:
                    if loads_x:
                        sp.wait_ge(stored, (gi + 1) * stores)
                        rows = x_rows.rearrange("(t p) d -> p t d", p=P)
                        sp.dma_start(x[:, :, :], rows[:, bass.ds(gi * G, G), :]).then_inc(x_in, 16)
                    if kind == "router":
                        sp.wait_ge(out_ready, gi + 1)
                        rows = io["res2"].rearrange("(t p) d -> p t d", p=P)
                        sp.dma_start(rows[:, bass.ds(gi * G, G), :], x[:, :, :]).then_inc(stored, 16)
                        sp.wait_ge(xt_ready, gi + 1)
                        sp.dma_start(io["xt"][bass.ds(gi, 1)].rearrange("o p n -> (o p) n"), xt[:, :, :, :].rearrange("p t c n -> p (t c n)")).then_inc(stored, 16)
                    sp.wait_ge(taken, gi * G + G + 4)
                    rows = table.rearrange("(t p) w -> p t w", p=P)
                    sp.dma_start(rows[:, bass.ds(gi * G, G), :], trow[:, :, :]).then_inc(stored, 16)
                sp.wait_ge(stored, (NG + 1) * stores)

            @block.vector
            def _(dve):
                dve.memset(trow[:, :, :], 0.0)
                dve.wait_ge(w_in, 16 * loads)
                if kind in ("gat0", "gat1"):
                    for side in (0, 1):
                        for c in (0, 1):
                            dve.tensor_tensor_reduce(out=prod[:, c, :], in0=wt[:, c, 0:M], in1=att[:, side, :], scale=1.0, scalar=0.0,
                                                     op0=ALU.mult, op1=ALU.add, accum_out=wt[:, c, M + side:M + side + 1])
                            dve.drain()
                if kind == "router":
                    for side in (0, 1):
                        dve.tensor_tensor(prod[:, :, :], wt[:, :, 0:M], att[:, side:side + 1, :].broadcast_to([P, 2, M]), ALU.mult)
                        dve.drain()
                        dve.tensor_reduce(wt[:, :, M + side * H:M + (side + 1) * H], prod[:, :, :].rearrange("p c (h x) -> p c h x", x=NE), AX, ALU.add)
                        dve.drain()
                dve.drain()
                dve.nop().then_inc(w_done, 1)
                with dve.Fori(0, NG) as gi:
                    dve.wait_ge(taken, gi * G + 4)
                    if kind == "gcn":
                        dve.tensor_copy(dn[:, :], g.dinv[:, bass.ds(gi * G, G)])
                    if from_acc:
                        nodes = bass.ds(gi * (G * P), G * P)
                        dve.reciprocal(inv_den[:, :], g.acc[:, 2, nodes])
                        dve.drain()
                        for c in (0, 1):
                            last = dve.tensor_tensor(ot[:, c, :], g.acc[:, c, nodes], inv_den[:, :], ALU.mult)
                        last.then_inc(scaled, 1)
                    if kind == "router":
                        dve.wait_ge(x_in, (gi + 1) * 16)
                        for q in range(4):
                            w = min(2, G - 2 * q)
                            dve.wait_ge(back, gi * 4 + q + 1)
                            last = dve.tensor_tensor(x[:, 2 * q:2 * q + w, :], x[:, 2 * q:2 * q + w, :],
                                                     g.bank[q][:, 0:w * D].rearrange("p (t d) -> p t d", d=D), ALU.add)
                        last.then_inc(out_ready, 1)
                        dve.drain()
                    elif loads_x:
                        dve.wait_ge(x_in, (gi + 1) * 16)
                    if loads_x:
                        norm.vector(dve, x, xn, gi, xn_ready)

            @block.tensor
            def _(pe):
                pe.wait_ge(w_done, 1)
                with pe.Fori(0, NG) as gi:
                    if kind == "router":
                        pe.wait_ge(ot_ready, gi + 1)
                        for t in range(G):
                            for c in (0, 1):
                                last = nc.tensor.transpose(g.bank[t // 2][:, t % 2 * D + c * P:t % 2 * D + (c + 1) * P], ot[:, c, t * P:(t + 1) * P], g.ident[:, :])
                            if t % 2 or t == G - 1:
                                last.then_inc(back, 1)
                    if loads_x:
                        pe.wait_ge(xn_ready, gi + 1)
                        turn(nc, g, xn, turned)
                    pe.wait_ge(xt_ready, gi + 1)
                    for t in range(G):
                        pe.wait_ge(taken, gi * G + t + 2)
                        for c in (0, 1):
                            last = nc.tensor.matmul(g.bank[4 + t % 4][:, 0:OUT], xt[:, t, c, :], wt[:, c, :], start=c == 0, stop=c == 1)
                        last.then_inc(made, 1)

            @block.scalar
            def _(act):
                act.nop().then_inc(taken, 4)
                act.wait_ge(w_done, 1)
                with act.Fori(0, NG) as gi:
                    if from_acc:
                        act.wait_ge(scaled, gi + 1)
                        for c in (0, 1):
                            if kind == "router":
                                last = act.activation(ot[:, c, :], ot[:, c, :], ACT.Identity, bias=bias[:, c:c + 1])
                            else:
                                last = act.activation(xt[:, :, c, :], ot[:, c, :].rearrange("p (t n) -> p t n", n=P), ACT.Relu, bias=bias[:, c:c + 1])
                        last.then_inc(ot_ready if kind == "router" else xt_ready, 1)
                    if loads_x:
                        norm.scalar(act, gi)
                    act.wait_ge(stored, (gi + 1) * stores)
                    if loads_x:
                        turned_copies(act, g, xt, turned, gi * 4, xt_ready)
                    for t in range(G):
                        act.wait_ge(made, gi * G + t + 1)
                        bank = g.bank[4 + t % 4]
                        if kind == "gcn":
                            last = act.activation(trow[:, t, :], bank[:, 0:OUT], ACT.Copy, scale=dn[:, t:t + 1])
                        else:
                            last = act.activation(trow[:, t, 0:OUT], bank[:, 0:OUT], ACT.Copy)
                        last.then_inc(taken, 1)


def experts(nc, io, g, kind):
    switch = kind == "switch"
    NM = 1 if switch else NE
    ins = {k: io[("s_" if switch else "t_") + k] for k in ("W1", "b1", "W2", "b2")}
    E = EXPERTS if switch else NE
    x_rows, out_rows = (io["x"], io["res"]) if switch else (io["res2"], io["out"])
    RW = HEADS * NE
    BLOCKS = NM * G
    SUBS = ((0, 4), (4, G - 4))
    with ExitStack() as stack:
        m = Memory(nc, stack, kind)
        x = m.sbuf("x", [P, G, D])
        xt = m.sbuf("xt", [P, G, 2, P])
        w1 = m.sbuf("w1", [P, 2, FH])
        w2 = m.sbuf("w2", [P, FT, D])
        b1 = m.sbuf("b1", [P, FT])
        b2 = m.sbuf("b2", [EXPERTS, D])
        ot = m.sbuf("ot", [P, G * P])
        chosen = m.sbuf("chosen", [P, G, EXPERTS])
        wide = m.sbuf("wide", [P, NM, G, P])
        gate = m.sbuf("gate", [P, NM, G * P])
        chosen_t = m.sbuf("chosen_t", [EXPERTS, G * P])
        zero = m.sbuf("zero", [P, 4 * P], BF16)
        raw = m.sbuf("raw", [P, 4, 4 * P])
        hidden = m.sbuf("hidden", [P, 4, 4 * P])
        norm = Normaliser(m)
        w_in, w_done, x_in = m.sem("w_in"), m.sem("w_done"), m.sem("x_in")
        ot_ready, sums, xn_ready = m.sem("ot_ready"), m.sem("sums"), m.sem("xn_ready")
        turned, xt_ready, logits_up = m.sem("turned"), m.sem("xt_ready"), m.sem("logits_up")
        routed, spread, gated = m.sem("routed"), m.sem("spread"), m.sem("gated")
        h_made, h_raw, h_ready, h_used = m.sem("h_made"), m.sem("h_raw"), m.sem("h_ready"), m.sem("h_used")
        x_ready, stored = m.sem("x_ready"), m.sem("stored")
        if switch:
            xn = m.sbuf("xn", [P, G, D])
            wlin = m.sbuf("wlin", [P, D])
            bconv = m.sbuf("bconv", [P, 1])
            bconv_wide = m.sbuf("bconv_wide", [P, P])
            blin = m.sbuf("blin", [P, D])
            rw = m.sbuf("rw", [EXPERTS, D])
            rwt = m.sbuf("rwt", [P, 2, EXPERTS])
            rb = m.sbuf("rb", [P, EXPERTS])
            dn = m.sbuf("dn", [P, G])
            logits = m.sbuf("logits", [P, G, EXPERTS])
            top = m.sbuf("top", [P, G, 8])
            topi = m.sbuf("topi", [P, G, 8], U32)
            best = m.sbuf("best", [P, G])
            own = m.sbuf("own", [P, FT])
            setup = m.sem("setup")
        else:
            den = m.sbuf("den", [P, G, HEADS])
            agg = m.sbuf("agg", [P, G, RW])
            aggn = m.sbuf("aggn", [P, G, RW])
            rows3 = m.sbuf("rows3", [P, 3, RW])
            scores = m.sbuf("scores", [P, 2, G, 8])
            top = m.sbuf("top", [P, 2, G, 8])
            topi = m.sbuf("topi", [P, 2, G, 8], U32)
            best = m.sbuf("best", [P, 2, G])
            hot = m.sbuf("hot", [P, 2, G, NE])
            gap, rise = m.sbuf("gap", [P, G]), m.sbuf("rise", [P, G])
            share = m.sbuf("share", [P, 2, G])
            gap_ready, gap_exped = m.sem("gap_ready"), m.sem("gap_exped")

        with nc.Block() as block:
            @block.sync
            def _(sp):
                n = 0
                with nc.allow_non_contiguous_dma(reason="biases by partition"):
                    for c in (0, 1):
                        sp.dma_start(w1[:, c, :], ins["W1"][c * P:(c + 1) * P, :]).then_inc(w_in, 16)
                    sp.dma_start(w2[:, :, :], ins["W2"].rearrange("e h d -> (e h) d").rearrange("(f p) d -> p f d", p=P)).then_inc(w_in, 16)
                    sp.dma_start(b1[:, :], ins["b1"]).then_inc(w_in, 16)
                    sp.wait_ge(w_done, 1)
                    sp.dma_start(b2[0:E, :], ins["b2"]).then_inc(w_in, 16)
                    n += 5
                    if switch:
                        sp.dma_start(wlin[:, :], io["W_lin"]).then_inc(w_in, 16)
                        sp.dma_start(bconv[:, :], io["b_conv"].rearrange("(p o) -> p o", o=1)).then_inc(w_in, 16)
                        sp.dma_start(blin[:, :], io["b_lin"].partition_broadcast(P)).then_inc(w_in, 16)
                        sp.dma_start(rw[:, :], io["router_w"]).then_inc(w_in, 16)
                        sp.dma_start(rb[:, :], io["router_b"].partition_broadcast(P)).then_inc(w_in, 16)
                        n += 5
                    else:
                        for i, k in enumerate(("b_gat", "ln_gamma", "ln_beta")):
                            sp.dma_start(rows3[:, i, :], io[k].partition_broadcast(P)).then_inc(w_in, 16)
                        n += 3
                assert n == (10 if switch else 8)
                sp.nop().then_inc(stored, 16)
                with sp.Fori(0, NG) as gi:
                    sp.wait_ge(stored, (gi + 1) * 16)
                    rows = x_rows.rearrange("(t p) d -> p t d", p=P)
                    sp.dma_start(x[:, :, :], rows[:, bass.ds(gi * G, G), :]).then_inc(x_in, 16)
                    if not switch:
                        sp.wait_ge(x_ready, gi + 1)
                        sp.dma_start(xt[:, :, :, :].rearrange("p t c n -> p (t c n)"), io["xt"][bass.ds(gi, 1)].rearrange("o p n -> (o p) n")).then_inc(xt_ready, 16)
                    sp.wait_ge(x_ready, gi + 2)
                    rows = out_rows.rearrange("(t p) d -> p t d", p=P)
                    sp.dma_start(rows[:, bass.ds(gi * G, G), :], x[:, :, :]).then_inc(stored, 16)
                sp.wait_ge(stored, (NG + 1) * 16)

            @block.vector
            def _(dve):
                dve.nop().then_inc(x_ready, 1)
                dve.nop().then_inc(h_ready, 4)
                dve.memset(b2[:, :], 0.0)
                dve.memset(zero[:, :], 0.0)
                dve.memset(chosen[:, :, :], 0.0)
                if not switch:
                    dve.memset(scores[:, :, :, :], LOW)
                dve.drain()
                dve.nop().then_inc(w_done, 1)
                dve.wait_ge(w_in, 16 * (10 if switch else 8))
                if switch:
                    dve.tensor_scalar(bconv_wide[:, :], g.ones[:, :], bconv[:, 0:1], None, ALU.mult).then_inc(setup, 1)
                    dve.wait_ge(setup, 2)
                    dve.tensor_tensor(blin[:, :], blin[:, :], g.bank[0][:, 0:D], ALU.add)
                    for c in (0, 1):
                        dve.tensor_copy(rwt[:, c, :], g.bank[1][:, c * EXPERTS:(c + 1) * EXPERTS])
                    dve.tensor_scalar(own[0:EH, :], g.iota[0:EH, 0:FT], 2.0, None, ALU.mult)
                    dve.tensor_scalar(own[EH:P, :], g.iota[EH:P, 0:FT], 2.0, 1.0, ALU.mult, ALU.add)
                    dve.drain()
                    dve.nop().then_inc(setup, 1)
                with dve.Fori(0, NG) as gi:
                    if switch:
                        dve.tensor_copy(dn[:, :], g.dinv[:, bass.ds(gi * G, G)])
                        dve.wait_ge(x_in, (gi + 1) * 16)
                        dve.tensor_tensor(x[:, :, :], x[:, :, :], blin[:, :].unsqueeze(1).broadcast_to([P, G, D]), ALU.add)
                        dve.drain()
                        for t in range(G):
                            if t % 2 == 0:
                                dve.wait_ge(sums, gi * 4 + t // 2 + 1)
                            dve.scalar_tensor_tensor(out=x[:, t, :], in0=g.bank[t // 2][:, t % 2 * D:(t % 2 + 1) * D], scalar=dn[:, t:t + 1],
                                                     in1=x[:, t, :], op0=ALU.mult, op1=ALU.add)
                        dve.drain()
                        norm.vector(dve, x, xn, gi, xn_ready)
                        dve.wait_ge(logits_up, gi + 1)
                        dve.tensor_tensor(logits[:, :, :], g.bank[6][:, 0:G * EXPERTS].rearrange("p (t e) -> p t e", e=EXPERTS),
                                          rb[:, :].unsqueeze(1).broadcast_to([P, G, EXPERTS]), ALU.add)
                        dve.drain()
                        for t in range(G):
                            dve.max(out=top[:, t, :], in_=logits[:, t, :])
                        dve.drain()
                        for t in range(G):
                            dve.max_index(out=topi[:, t, :], in_max=top[:, t, :], in_values=logits[:, t, :])
                        dve.drain()
                        dve.tensor_copy(best[:, :], topi[:, :, 0])
                        dve.drain()
                        dve.tensor_tensor(chosen[:, :, :], g.iota[:, 0:EXPERTS].unsqueeze(1).broadcast_to([P, G, EXPERTS]),
                                          best[:, :].unsqueeze(2).broadcast_to([P, G, EXPERTS]), ALU.is_equal)
                        dve.tensor_copy(wide[:, 0, :, :], best[:, :].unsqueeze(2).broadcast_to([P, G, P])).then_inc(routed, 1)
                    else:
                        dve.wait_ge(sums, gi + 1)
                        for q, (t0, n) in enumerate(SUBS):
                            v = g.bank[q][:, 0:n * P].rearrange("p (t k) -> p t k", k=P)
                            dve.tensor_scalar(den[:, t0:t0 + n, :], v[:, :, RW:RW + HEADS], 1e-16, None, ALU.add)
                        dve.drain()
                        dve.reciprocal(den[:, :, :], den[:, :, :])
                        dve.drain()
                        for q, (t0, n) in enumerate(SUBS):
                            for t in range(n):
                                v = g.bank[q][:, t * P:t * P + RW].rearrange("p (h x) -> p h x", x=NE)
                                dve.tensor_tensor(agg[:, t0 + t, :].rearrange("p (h x) -> p h x", x=NE), v,
                                                  den[:, t0 + t, :].unsqueeze(2).broadcast_to([P, HEADS, NE]), ALU.mult)
                        dve.drain()
                        r3 = [rows3[:, i:i + 1, :].broadcast_to([P, G, RW]) for i in range(3)]
                        dve.tensor_tensor(agg[:, :, :], agg[:, :, :], r3[0], ALU.add)
                        dve.drain()
                        norm.vector(dve, agg, aggn, gi, xn_ready)
                        dve.drain()
                        dve.tensor_tensor(aggn[:, :, :], aggn[:, :, :], r3[1], ALU.mult)
                        dve.drain()
                        dve.tensor_tensor(aggn[:, :, :], aggn[:, :, :], r3[2], ALU.add)
                        dve.drain()
                        dve.tensor_reduce(scores[:, 0, :, 0:NE], aggn[:, :, :].rearrange("p t (h x) -> p t x h", x=NE), AX, ALU.add)
                        dve.drain()
                        dve.tensor_scalar(scores[:, 0, :, 0:NE], scores[:, 0, :, 0:NE], 1.0 / HEADS, None, ALU.mult)
                        dve.drain()
                        for k in (0, 1):
                            for t in range(G):
                                dve.max(out=top[:, k, t, :], in_=scores[:, k, t, :])
                            dve.drain()
                            for t in range(G):
                                dve.max_index(out=topi[:, k, t, :], in_max=top[:, k, t, :], in_values=scores[:, k, t, :])
                            dve.drain()
                            dve.tensor_copy(best[:, k, :], topi[:, k, :, 0])
                            dve.drain()
                            dve.tensor_tensor(hot[:, k, :, :], g.iota[:, 0:NE].unsqueeze(1).broadcast_to([P, G, NE]),
                                              best[:, k, :].unsqueeze(2).broadcast_to([P, G, NE]), ALU.is_equal)
                            dve.drain()
                            if k == 0:
                                dve.scalar_tensor_tensor(out=scores[:, 1, :, 0:NE], in0=hot[:, 0, :, :], scalar=LOW / 2, in1=scores[:, 0, :, 0:NE], op0=ALU.mult, op1=ALU.add)
                                dve.drain()
                        dve.tensor_tensor(gap[:, :], top[:, 1, :, 0], top[:, 0, :, 0], ALU.subtract).then_inc(gap_ready, 1)
                        dve.wait_ge(gap_exped, gi + 1)
                        dve.tensor_scalar(share[:, 0, :], rise[:, :], 1.0, None, ALU.add)
                        dve.drain()
                        dve.reciprocal(share[:, 0, :], share[:, 0, :])
                        dve.drain()
                        dve.tensor_tensor(share[:, 1, :], share[:, 0, :], rise[:, :], ALU.mult)
                        dve.drain()
                        for k in (0, 1):
                            dve.tensor_tensor(hot[:, k, :, :], hot[:, k, :, :], share[:, k, :].unsqueeze(2).broadcast_to([P, G, NE]), ALU.mult)
                        dve.drain()
                        dve.tensor_tensor(chosen[:, :, 0:NE], hot[:, 0, :, :], hot[:, 1, :, :], ALU.add)
                        dve.drain()
                        for e in range(NE):
                            last = dve.tensor_copy(wide[:, e, :, :], chosen[:, :, e:e + 1].broadcast_to([P, G, P]))
                        last.then_inc(routed, 1)
                    BK = -(-BLOCKS // 4)
                    dve.wait_ge(gated, (gi + 1) * (BK + 2))
                    for f in range(FT):
                        for s, (t0, n) in enumerate(SUBS):
                            k = 2 * f + s
                            dve.wait_ge(h_raw, gi * (2 * FT) + k + 5)
                            dve.wait_ge(h_used, gi * (2 * FT) + k + 1)
                            cols = slice(t0 * P, (t0 + n) * P)
                            if switch:
                                dve.scalar_tensor_tensor(out=hidden[:, k % 4, 0:n * P], in0=gate[:, 0, cols], scalar=own[:, f:f + 1],
                                                         in1=raw[:, k % 4, 0:n * P], op0=ALU.is_equal, op1=ALU.mult).then_inc(h_ready, 1)
                            else:
                                dve.tensor_tensor(hidden[:, k % 4, 0:n * P], gate[:, f // (FT // NE), cols], raw[:, k % 4, 0:n * P], ALU.mult).then_inc(h_ready, 1)
                    if not switch:
                        dve.wait_ge(x_in, (gi + 1) * 16)
                    for q in range(4):
                        w = min(2, G - 2 * q)
                        if q % 2 == 0:
                            dve.wait_ge(h_used, (gi + 1) * (2 * FT) + 3 + q // 2)
                        xs, ps = x[:, 2 * q:2 * q + w, :], g.bank[q][:, 0:w * D].rearrange("p (t d) -> p t d", d=D)
                        if switch:
                            last = dve.scalar_tensor_tensor(out=xs, in0=ps, scalar=0.0, in1=xs, op0=ALU.max, op1=ALU.add)
                        else:
                            last = dve.tensor_tensor(xs, ps, xs, ALU.add)
                    last.then_inc(x_ready, 1)

            @block.tensor
            def _(pe):
                pe.nop().then_inc(h_used, 4)
                pe.wait_ge(w_in, 16 * (10 if switch else 8))
                if switch:
                    pe.wait_ge(setup, 1)
                    nc.tensor.matmul(g.bank[0][:, 0:D], bconv_wide[:, :], wlin[:, :], start=True, stop=True)
                    for c in (0, 1):
                        last = nc.tensor.transpose(g.bank[1][:, c * EXPERTS:(c + 1) * EXPERTS], rw[:, c * P:(c + 1) * P], g.ident[0:EXPERTS, 0:EXPERTS])
                    last.then_inc(setup, 1)
                    pe.wait_ge(setup, 3)
                with pe.Fori(0, NG) as gi:
                    pe.wait_ge(x_ready, gi + 1)
                    pe.wait_ge(ot_ready, gi + 1)
                    if switch:
                        for t in range(G):
                            last = nc.tensor.matmul(g.bank[t // 2][:, t % 2 * D:(t % 2 + 1) * D], ot[:, t * P:(t + 1) * P], wlin[:, :], start=True, stop=True)
                            if t % 2 or t == G - 1:
                                last.then_inc(sums, 1)
                        pe.wait_ge(xn_ready, gi + 1)
                        turn(nc, g, xn, turned)
                        pe.wait_ge(xt_ready, gi + 1)
                        for t in range(G):
                            for c in (0, 1):
                                last = nc.tensor.matmul(g.bank[6][:, t * EXPERTS:(t + 1) * EXPERTS], xt[:, t, c, :], rwt[:, c, :], start=c == 0, stop=c == 1)
                        last.then_inc(logits_up, 1)
                    else:
                        for t in range(G):
                            last = nc.tensor.transpose(g.bank[t // 4][:, t % 4 * P:(t % 4 + 1) * P], ot[:, t * P:(t + 1) * P], g.ident[:, :])
                        last.then_inc(sums, 1)
                        pe.wait_ge(xt_ready, (gi + 1) * 16)
                    pe.wait_ge(routed, gi + 1)
                    BK = -(-BLOCKS // 4)
                    for i in range(BLOCKS):
                        q = i // 4
                        if q >= 4 and i % 4 == 0:
                            pe.wait_ge(gated, gi * (BK + 2) + q - 3)
                        last = nc.tensor.transpose(g.bank[q % 4][:, i % 4 * P:(i % 4 + 1) * P], wide[:, i // G, i % G, :], g.ident[:, :])
                        if i % 4 == 3 or i == BLOCKS - 1:
                            last.then_inc(spread, 1)
                    for s, (t0, n) in enumerate(SUBS):
                        for t in range(n):
                            last = nc.tensor.transpose(g.bank[6 + s][0:EXPERTS, t * P:(t + 1) * P], chosen[:, t0 + t, :], g.ident[:, :])
                        last.then_inc(spread, 1)
                    pe.wait_ge(gated, (gi + 1) * (BK + 2))
                    for q in range(4):
                        nc.tensor.matmul(g.bank[q][:, :], zero[:, 0:P], zero[:, :], start=True, stop=False)
                    for t in range(G):
                        nc.tensor.matmul(g.bank[t // 2][:, t % 2 * D:(t % 2 + 1) * D], chosen_t[:, t * P:(t + 1) * P], b2[:, :], start=False, stop=False)

                    def up(f):
                        for s, (t0, n) in enumerate(SUBS):
                            k = 2 * f + s
                            pe.wait_ge(h_raw, gi * (2 * FT) + k + 1)
                            for c in (0, 1):
                                last = nc.tensor.matmul(g.bank[4 + k % 4][:, 0:n * P].rearrange("p (t n) -> p t n", n=P), w1[:, c, f * P:(f + 1) * P],
                                                        xt[:, t0:t0 + n, c, :], start=c == 0, stop=c == 1)
                            last.then_inc(h_made, 1)

                    def down(f):
                        for s, (t0, n) in enumerate(SUBS):
                            k = 2 * f + s
                            pe.wait_ge(h_ready, gi * (2 * FT) + k + 5)
                            for t in range(n):
                                last = nc.tensor.matmul(g.bank[(t0 + t) // 2][:, (t0 + t) % 2 * D:((t0 + t) % 2 + 1) * D], hidden[:, k % 4, t * P:(t + 1) * P],
                                                        w2[:, f, :], start=False,
                                                        stop=f == FT - 1 and ((t0 + t) % 2 == 1 or t0 + t == G - 1))
                            last.then_inc(h_used, 1)

                    up(0)
                    for f in range(FT):
                        if f + 1 < FT:
                            up(f + 1)
                        down(f)

            @block.scalar
            def _(act):
                act.nop().then_inc(h_raw, 4)
                act.wait_ge(w_in, 16 * (10 if switch else 8))
                with act.Fori(0, NG) as gi:
                    act.activation(ot[:, :], g.acc[:, 0, bass.ds(gi * (G * P), G * P)], ACT.Copy).then_inc(ot_ready, 1)
                    norm.scalar(act, gi)
                    if switch:
                        turned_copies(act, g, xt, turned, gi * 4, xt_ready)
                    else:
                        act.wait_ge(gap_ready, gi + 1)
                        act.activation(rise[:, :], gap[:, :], ACT.Exp).then_inc(gap_exped, 1)
                    BK = -(-BLOCKS // 4)
                    flat = gate[:, :, :].rearrange("p m n -> p (m n)")
                    for q in range(BK):
                        w = min(512, BLOCKS * P - q * 512)
                        act.wait_ge(spread, gi * (BK + 2) + q + 1)
                        act.activation(flat[:, q * 512:q * 512 + w], g.bank[q % 4][:, 0:w], ACT.Copy).then_inc(gated, 1)
                    for s, (t0, n) in enumerate(SUBS):
                        act.wait_ge(spread, gi * (BK + 2) + BK + s + 1)
                        act.activation(chosen_t[:, t0 * P:(t0 + n) * P], g.bank[6 + s][0:EXPERTS, 0:n * P], ACT.Copy).then_inc(gated, 1)
                    for f in range(FT):
                        for s, (t0, n) in enumerate(SUBS):
                            k = 2 * f + s
                            act.wait_ge(h_made, gi * (2 * FT) + k + 1)
                            act.wait_ge(h_ready, gi * (2 * FT) + k + 1)
                            act.activation(raw[:, k % 4, 0:n * P], g.bank[4 + k % 4][:, 0:n * P], ACT.Relu if switch else ACT.Gelu, bias=b1[:, f:f + 1]).then_inc(h_raw, 1)


def make_globals(nc, m, g):
    g.passes = g.lows = g.carried = 0
    g.bank = [m.stack.enter_context(nc.psum_tensor(f"bank{i}", [P, 512], F32)) for i in range(8)]
    g.ident = m.sbuf("ident", [P, P])
    g.ones = m.sbuf("ones", [P, P])
    g.carrier = m.sbuf("carrier", [1, 33])
    g.iota = m.sbuf("iota", [P, P])
    g.group = m.sbuf("group", [P, B])
    g.select_router = m.sbuf("select_router", [P, HEADS * NE + HEADS])
    g.select = {"gat": g.ones, "router": g.select_router}
    g.dinv = m.sbuf("dinv", [P, NT])
    g.src = m.sbuf("src_of", [P, CH], I16)
    g.rel = m.sbuf("rel", [P, CH], BF16)
    g.keep = m.sbuf("keep", [P, C1])
    g.base = m.sbuf("base", [1, CH], I16)
    g.cont_low = m.sbuf("cont_low", [1, CH], BF16)
    g.same_low = m.sbuf("same_low", [1, CH], BF16)
    g.low = g.low_back = g.low0 = g.low_own = None


def run_stage_memory(nc, g, name, memset):
    with nc.Block() as block:
        @block.vector
        def _(dve):
            for t in memset:
                dve.memset(t, 0.0)


def gnn_ffn(nc, *args):
    io = dict(zip(NAMES + ("out",), args))
    for name, shape, dt in (("keys", (1 << SORT_BITS,), I32), ("table_gcn", (NPAD, HID), F32),
                            ("table_gat", (NPAD, D + 4), F32), ("table_router", (NPAD, HEADS * NE + 2 * HEADS), F32),
                            ("res", (NPAD, D), F32), ("res2", (NPAD, D), F32), ("xt", (NG, P, 2 * G * P), F32)):
        io[name] = nc.dram_tensor(name, shape, dt, kind="Internal").ap()

    class Shared:
        pass

    g = Shared()
    with ExitStack() as stack:
        m = Memory(nc, stack, "g")
        make_globals(nc, m, g)
        sort_edges(nc, io, g)
        index_edges(nc, io, g)
        g.acc = m.sbuf("acc", [P, 3, WIN])
        run_stage_memory(nc, g, "zero", [g.acc[:, :, :]])
        project(nc, io, g, "gcn")
        gather_pass(nc, io, g, "gcn", io["table_gcn"], 0, C1)
        experts(nc, io, g, "switch")
        for layer in (0, 1):
            project(nc, io, g, f"gat{layer}")
            with ExitStack() as low:
                ml = Memory(nc, low, f"gat{layer}_low")
                g.low, g.low_back = ml.sbuf("low", [B, C1 // B, P], BF16), ml.sbuf("low_back", [B, C1 // B, P], BF16)
                g.low0, g.low_own = ml.sbuf("low0", [B, C1 // B, P], BF16), ml.sbuf("low_own", [B, C1 // B, P], BF16)
                running_lows(nc, io, g, 0, C1, 1)
                gather_pass(nc, io, g, "gat", io["table_gat"], 0, C1)
        project(nc, io, g, "router")
        with ExitStack() as low:
            ml = Memory(nc, low, "router_low")
            g.low, g.low_back = ml.sbuf("low", [B * HEADS, C2 // B, P], BF16), ml.sbuf("low_back", [B * HEADS, C2 // B, P], BF16)
            g.low0, g.low_own = ml.sbuf("low0", [B * HEADS, C2 // B, P], BF16), ml.sbuf("low_own", [B * HEADS, C2 // B, P], BF16)
            running_lows(nc, io, g, C1, C2, HEADS)
            gather_pass(nc, io, g, "router", io["table_router"], C1, C2)
        experts(nc, io, g, "top2")


_INS = ("x", "src", "dst", "L0_gnn_W_conv", "L0_gnn_b_conv", "L0_gnn_W_lin", "L0_gnn_b_lin", "L0_ffn_router_w",
        "L0_ffn_router_b", "L0_ffn_W1", "L0_ffn_b1", "L0_ffn_W2", "L0_ffn_b2", "L1_gnn_W", "L1_gnn_attn_l",
        "L1_gnn_attn_r", "L1_gnn_bias", "L1_ffn_W_gat", "L1_ffn_att_src", "L1_ffn_att_dst", "L1_ffn_b_gat",
        "L1_ffn_ln_gamma", "L1_ffn_ln_beta", "L1_ffn_W1", "L1_ffn_b1", "L1_ffn_W2", "L1_ffn_b2", "L1_ffn_edge_index")
NAMES = ("x", "src", "dst", "W_conv", "b_conv", "W_lin", "b_lin", "router_w", "router_b", "s_W1", "s_b1", "s_W2", "s_b2",
         "W", "attn_l", "attn_r", "bias", "W_gat", "att_src", "att_dst", "b_gat", "ln_gamma", "ln_beta",
         "t_W1", "t_b1", "t_W2", "t_b2", "edges")


def kernel(**inputs):
    import numpy as _np
    import concourse.bacc as _bacc
    from concourse import mybir as _mybir
    from concourse.bass_utils import run_bass_kernel_spmd as _run

    nc = _bacc.Bacc("TRN2", target_bir_lowering=False, num_devices=1)
    arrays, args = {}, []
    for name in _INS:
        a = _np.ascontiguousarray(inputs[name])
        if name == "x":
            a = _np.concatenate([a, _np.zeros((NPAD - a.shape[0], a.shape[1]), a.dtype)])
        elif name.endswith("ffn_W1"):
            a = _np.ascontiguousarray(a.transpose(1, 0, 2).reshape(D, -1))
        elif name.endswith("ffn_b1"):
            a = _np.ascontiguousarray(a.reshape(-1, P).T)
        arrays[f"in_{name}_dram"] = a
        args.append(nc.dram_tensor(f"in_{name}_dram", a.shape, _mybir.dt.from_np(a.dtype), kind="ExternalInput").ap())
    args.append(nc.dram_tensor("out_0_dram", (NPAD, D), F32, kind="ExternalOutput").ap())
    gnn_ffn(nc, *args)
    r = _run(nc, [arrays], core_ids=[0])
    return r.results[0]["out_0_dram"][:N_NODES]
```

```python
import numpy as np
from contextlib import ExitStack

import concourse.bass as bass
import concourse.mybir as mybir

P = 128
N_NODES = 6250
D = 256
NT = -(-N_NODES // P)
NPAD = NT * P
G = 7
NG = NT // G
HID = 128
EXPERTS, EH = 32, 64
FH = EXPERTS * EH
FT = FH // P
HEADS, NE = 4, 4
MH = 2 * D
E1, E2 = 100000, 131072
B = 32
SB = 13
MASK = (1 << SB) - 1
KEY1 = 0x40000000
KEY2 = KEY1 | 1 << (2 * SB)
LAST = 0x4FFFFFFF
SORT_BITS = 18
F = (1 << SORT_BITS) // P
C1 = B * -(-(E1 + NPAD) // (B * P))
C2 = B * -(-(E2 + NPAD) // (B * P))
FILL1 = C1 * P - E1 - NPAD
CH = C1 + C2
EP1 = 125
EF1, EF2 = E1 // EP1, E2 // P
WIN = NPAD + P
LOW = -1e30
EPS = 1e-5
RQ = 8
PAIRS = (NT + 1) // 2
GH = 16
POOL_GROUPS = 26
assert C1 * P + E2 + NPAD <= 1 << SORT_BITS and CH <= F and FILL1 % 2 == 0 and NT % G == 0 and NG % 2 == 1
assert EF1 + EF2 + 2 * NT + 2 <= F and C1 // B % 2 == 0 and C2 // B % 2 == 0

F32 = mybir.dt.float32
BF16 = mybir.dt.bfloat16
I32 = mybir.dt.int32
I16 = mybir.dt.int16
U32 = mybir.dt.uint32
ALU = mybir.AluOpType
ACT = mybir.ActivationFunctionType
AX = mybir.AxisListType.X
EDVE = mybir.EngineType.DVE


class Memory:

    def __init__(self, nc, stack, stage):
        self.nc, self.stack, self.stage = nc, stack, stage
        self.sems = []
        if stage != "g":
            stack.callback(self.give_back)

    def sbuf(self, name, shape, dt=F32):
        return self.stack.enter_context(self.nc.sbuf_tensor(f"{self.stage}_{name}", shape, dt))

    def sem(self, name):
        s = self.nc.alloc_semaphore(name=f"{self.stage}_{name}")
        self.sems.append(s)
        return s

    def give_back(self):
        if not self.sems:
            return
        self.nc.clear_and_free_semaphores(self.sems)
        self.nc.all_engine_barrier()


def wait_alone(pool, g, sem, value):
    pool.wait_ge(sem, value)
    g.carried = g.carried % 32 + 1
    pool.tensor_tensor(g.carrier[:, g.carried:g.carried + 1], g.carrier[:, 0:1], g.carrier[:, 0:1], ALU.mult)


def sort_plan():
    fb = F.bit_length() - 1
    plan = []
    for k in range(1, SORT_BITS + 1):
        if k > fb:
            plan.append(("sign", k))
            plan.append(("flip",))
            for j in range(k - 1, fb - 1, -1):
                plan.append(("swap", None, j - fb, P))
            plan.append(("flip",))
        elif k == fb:
            plan.append(("sign", k))
        for j in range(min(k, fb) - 1, -1, -1):
            plan.append(("swap", k if k < fb else None, j, F))
    return plan


def swap_views(x, k, j, width):
    d = 1 << j
    if k is None:
        v = x.rearrange("p (a h d) -> p a h d", h=2, d=d)
        return [(v[:, :, 0, :], v[:, :, 1, :], True)]
    m = 1 << (k - j - 1)
    v = x.rearrange("p (a u m h d) -> p a u m h d", u=2, m=m, h=2, d=d)
    return [(v[:, :, u, :, 0, :], v[:, :, u, :, 1, :], u == 0) for u in (0, 1)]


def sort_edges(nc, io, g):
    with ExitStack() as stack:
        m = Memory(nc, stack, "sort")
        e1s, e1d = m.sbuf("e1s", [EP1, EF1], I32), m.sbuf("e1d", [EP1, EF1], I32)
        e2s, e2d = m.sbuf("e2s", [P, EF2], I32), m.sbuf("e2d", [P, EF2], I32)
        node = m.sbuf("node", [P, NT], I32)
        keys = [m.sbuf("keys_a", [P, F]), m.sbuf("keys_b", [P, F])]
        part = m.sbuf("part", [P, 1], I32)
        head = m.sbuf("head", [P, 1], I32)
        heads = m.sbuf("heads", [P, HEADS * NE + HEADS], I32)
        bits = m.sbuf("bits", [P, 9], I32)
        sign = m.sbuf("sign", [P, 9])
        flipsign = m.sbuf("flipsign", [P, 9])
        lo, hi = m.sbuf("lo", [EP1, EF1], I32), m.sbuf("hi", [EP1, EF1], I32)
        digit = m.sbuf("digit", [EP1, 2, 2, GH])
        oh_lo, oh_hi = m.sbuf("oh_lo", [EP1, 2, GH, P], BF16), m.sbuf("oh_hi", [EP1, 2, GH, NT], BF16)
        digit2 = m.sbuf("digit2", [EP1, 2, 2, GH])
        oh_lo2, oh_hi2 = m.sbuf("oh_lo2", [EP1, 2, GH, P], BF16), m.sbuf("oh_hi2", [EP1, 2, GH, NT], BF16)
        iotab = m.sbuf("iotab", [P, P], BF16)
        onehots2, counted2 = m.sem("onehots2"), m.sem("counted2")
        zero = m.sbuf("zero", [P, P], BF16)
        degree = m.sbuf("degree", [P, 3, NT])
        edges_in = m.sem("edges_in")
        made = m.sem("made")
        split = m.sem("split")
        step = m.sem("sort_step")
        flipped = m.sem("flipped")
        copied = m.sem("copied")
        onehots = m.sem("onehots")
        digits = m.sem("digits")
        counted = m.sem("counted")
        stored = m.sem("keys_stored")
        degree_sum, degree_done = m.sem("degree_sum"), m.sem("degree_done")
        plan = sort_plan()
        n_groups = EF1 // GH
        dve_groups = n_groups - POOL_GROUPS
        done = {}
        end = {}

        with nc.Block() as block:
            @block.gpsimd
            def _(pool):
                pool.memset(g.carrier[:, :], 1.0).then_inc(made, 1)
                pool.iota(node[:, :], [[1, NT]], base=0, channel_multiplier=NT).then_inc(made, 1)
                pool.iota(part[:, :], [[0, 1]], base=0, channel_multiplier=1).then_inc(made, 1)
                pool.iota(g.iota[:, :], [[1, P]], base=0, channel_multiplier=0, allow_small_or_imprecise_dtypes=True).then_inc(made, 1)
                pool.memset(g.ones[:, :], 1.0).then_inc(made, 1)
                pool.memset(zero[:, :], 0.0).then_inc(made, 1)
                pool.memset(g.ident[:, :], 0.0).then_inc(made, 1)
                pool.memset(g.group[:, :], 1.0).then_inc(made, 1)
                pool.iota(heads[:, 0:HEADS * NE], [[1, HEADS], [0, NE]], base=0, channel_multiplier=0).then_inc(made, 1)
                pool.iota(heads[:, HEADS * NE:], [[1, HEADS]], base=0, channel_multiplier=0).then_inc(made, 1)
                pool.wait_ge(made, 10)
                pool.affine_select(out=g.ident[:, :], in_=g.ident[:, :], compare_op=ALU.not_equal, fill=1.0, base=0,
                                   pattern=[[-1, P]], channel_multiplier=1).then_inc(made, 1)
                pool.affine_select(out=g.group[:, :], in_=g.group[:, :], compare_op=ALU.is_ge, fill=0.0, base=0,
                                   pattern=[[-HEADS, B]], channel_multiplier=1).then_inc(made, 1)
                pool.wait_ge(made, 12)
                pool.affine_select(out=g.group[:, :], in_=g.group[:, :], compare_op=ALU.is_ge, fill=0.0, base=HEADS - 1,
                                   pattern=[[HEADS, B]], channel_multiplier=-1).then_inc(made, 1)
                pool.wait_ge(split, 2)
                with pool.Fori(0, POOL_GROUPS // 2) as it:
                    for s in (0, 1):
                        i = it * 2 + s
                        wait_alone(pool, g, counted, i + 2)
                        cols = bass.ds(i * GH, GH)
                        pool.tensor_copy(digit[:, s, 0, :], lo[:, cols]).then_inc(digits, 1)
                        pool.tensor_copy(digit[:, s, 1, :], hi[:, cols]).then_inc(digits, 1)
                        wait_alone(pool, g, digits, i * 2 + 2)
                        for q in range(GH):
                            pool.tensor_scalar(oh_lo[:, s, q, :], g.iota[0:EP1, :], digit[:, s, 0, q:q + 1], None, ALU.is_equal)
                            last = pool.tensor_scalar(oh_hi[:, s, q, :], g.iota[0:EP1, 0:NT], digit[:, s, 1, q:q + 1], None, ALU.is_equal)
                        last.then_inc(onehots, 1)

            @block.vector
            def _(dve):
                n = [0]

                def did(ins):
                    n[0] += 1
                    ins.then_inc(step, 1)

                def after():
                    dve.wait_ge(step, n[0])

                k0 = keys[0][:, :].bitcast(I32)
                did(dve.memset(k0, LAST))
                dve.wait_ge(edges_in, 4 * 16)
                dve.tensor_scalar(lo[:, :], e1d[:, :], P - 1, None, ALU.bitwise_and).then_inc(split, 1)
                dve.tensor_scalar(hi[:, :], e1d[:, :], 7, None, ALU.logical_shift_right).then_inc(split, 1)
                dve.wait_ge(made, 10)
                did(dve.tensor_copy(iotab[:, :], g.iota[:, :]))
                after()
                c = 0
                spans = []
                for s, d in ((e1s, e1d), (e2s, e2d)):
                    did(dve.tensor_tensor(s[:, :], s[:, :], d[:, :], ALU.subtract))
                after()
                for s in (e1s, e2s):
                    did(dve.tensor_scalar(s[:, :], s[:, :], MASK, None, ALU.bitwise_and))
                after()
                for s, d, rows, w, key in ((e1s, e1d, EP1, EF1, KEY1), (e2s, e2d, P, EF2, KEY2)):
                    did(dve.scalar_tensor_tensor(out=k0[0:rows, c:c + w], in0=d[:, :], scalar=SB, in1=s[:, :],
                                                 op0=ALU.logical_shift_left, op1=ALU.bitwise_or))
                    spans.append((rows, c, w, key))
                    c += w
                dve.wait_ge(made, 3)
                for key in (KEY1, KEY2):
                    did(dve.tensor_scalar(k0[:, c:c + NT], node[:, :], SB, None, ALU.logical_shift_left))
                    spans.append((P, c, NT, key))
                    c += NT
                did(dve.memset(k0[0:FILL1 // 2, c:c + 2], KEY1 | ((1 << 2 * SB) - 1)))
                after()
                for rows, c, w, key in spans:
                    did(dve.tensor_scalar(k0[0:rows, c:c + w], k0[0:rows, c:c + w], key, None, ALU.bitwise_or))
                for b in range(9):
                    did(dve.tensor_scalar(bits[:, b:b + 1], part[:, :], b, 1, ALU.logical_shift_right, ALU.bitwise_and))
                after()
                dve.wait_ge(made, 10)
                did(dve.tensor_scalar(head[:, :], part[:, :], HEADS - 1, None, ALU.bitwise_and))
                after()
                did(dve.tensor_tensor(g.select_router[:, :], heads[:, :], head[:, :].broadcast_to([P, HEADS * NE + HEADS]), ALU.is_equal))
                did(dve.tensor_scalar(sign[:, :], bits[:, :], -2.0, 1.0, ALU.mult, ALU.add))
                after()
                did(dve.tensor_tensor(flipsign[:, 1:9], sign[:, 0:8], sign[:, 1:9], ALU.mult))
                did(dve.tensor_copy(flipsign[:, 0:1], sign[:, 0:1]))
                after()
                at, flips = 0, 0
                fb = F.bit_length() - 1
                for i, s in enumerate(plan):
                    x, y = keys[at], keys[1 - at]
                    if s[0] == "swap":
                        _, k, j, width = s
                        for (xl, xh, up), (yl, yh, _) in zip(swap_views(x[:, :], k, j, width), swap_views(y[:, :], k, j, width)):
                            did(dve.tensor_tensor(yl, xl, xh, ALU.min if up else ALU.max))
                            did(dve.tensor_tensor(yh, xl, xh, ALU.max if up else ALU.min))
                    elif s[0] == "sign":
                        b = s[1] - fb
                        did(dve.tensor_scalar(y[:, :], x[:, :], flipsign[:, b:b + 1], None, ALU.mult))
                    else:
                        flips += 1
                        for q in (0, 1):
                            dve.wait_ge(flipped, 4 * (flips - 1) + q + 1)
                            did(dve.tensor_copy(y[:, q * 512:(q + 1) * 512], g.bank[q][:, :]))
                        dve.wait_ge(copied, 2 * flips)
                    after()
                    done[i] = n[0]
                    at = 1 - at
                end.update(at=at, total=n[0])
                with dve.Fori(0, dve_groups // 2) as it:
                    for t in (0, 1):
                        i = it * 2 + t
                        dve.wait_ge(counted2, i + 1)
                        cols = bass.ds((POOL_GROUPS + i) * GH, GH)
                        dve.tensor_copy(digit2[:, t, 0, :], lo[:, cols])
                        dve.tensor_copy(digit2[:, t, 1, :], hi[:, cols])
                        dve.drain()
                        for q in range(GH):
                            dve.tensor_scalar(oh_lo2[:, t, q, :], iotab[0:EP1, :], digit2[:, t, 0, q:q + 1], None, ALU.is_equal)
                            last = dve.tensor_scalar(oh_hi2[:, t, q, :], iotab[0:EP1, 0:NT], digit2[:, t, 1, q:q + 1], None, ALU.is_equal)
                        last.then_inc(onehots2, 1)
                dve.wait_ge(degree_sum, 1)
                dve.tensor_scalar(degree[:, 0, :], g.bank[7][:, 0:NT], 1.0, None, ALU.add).then_inc(degree_done, 1)
                dve.wait_ge(degree_done, 2)
                newton(dve, degree[:, 0, :], degree[:, 1, :], g.dinv[:, :], degree[:, 2, :])

            @block.tensor
            def _(pe):
                pe.wait_ge(made, 12)
                hist = g.bank[7][:, 0:NT]
                nc.tensor.matmul(hist, zero[:, :], zero[:, 0:NT], start=True, stop=False).then_inc(counted, 3)
                pe.nop().then_inc(counted2, 2)
                todo = [POOL_GROUPS // 2]

                def count_some(most):
                    now = min(most, todo[0])
                    if not now:
                        return
                    first = POOL_GROUPS // 2 - todo[0]
                    todo[0] -= now
                    with pe.Fori(first, first + now) as it:
                        for s in (0, 1):
                            i = it * 2 + s
                            pe.wait_ge(onehots, i + 1)
                            for q in range(GH):
                                last = nc.tensor.matmul(hist, oh_lo[:, s, q, :], oh_hi[:, s, q, :], start=False, stop=False)
                            last.then_inc(counted, 1)

                count_some(POOL_GROUPS // 4)
                flips = 0
                at = 0
                for i, s in enumerate(plan):
                    if s[0] == "flip":
                        pe.wait_ge(step, done[i - 1])
                        if flips:
                            pe.wait_ge(copied, 2 * flips)
                        for q in range(4):
                            for r in range(4):
                                c = (4 * q + r) * P
                                last = nc.tensor.transpose(g.bank[q][:, r * P:(r + 1) * P], keys[at][:, c:c + P], g.ident[:, :])
                            last.then_inc(flipped, 1)
                        flips += 1
                        if flips % 2 == 0:
                            count_some(1)
                    at = 1 - at
                count_some(n_groups)
                with pe.Fori(0, dve_groups // 2) as it:
                    for t in (0, 1):
                        i = it * 2 + t
                        pe.wait_ge(onehots2, i + 1)
                        for q in range(GH):
                            last = nc.tensor.matmul(hist, oh_lo2[:, t, q, :], oh_hi2[:, t, q, :], start=False, stop=False)
                        last.then_inc(counted2, 1)
                nc.tensor.matmul(hist, zero[:, :], zero[:, 0:NT], start=False, stop=True).then_inc(degree_sum, 1)

            @block.scalar
            def _(act):
                flips = 0
                at = 0
                for i, s in enumerate(plan):
                    if s[0] == "flip":
                        for q in (2, 3):
                            act.wait_ge(flipped, 4 * flips + q + 1)
                            act.activation(keys[1 - at][:, q * 512:(q + 1) * 512], g.bank[q][:, :], ACT.Copy).then_inc(copied, 1)
                        flips += 1
                    at = 1 - at
                act.wait_ge(degree_done, 1)
                act.activation(degree[:, 1, :], degree[:, 0, :], ACT.Sqrt).then_inc(degree_done, 1)

            @block.sync
            def _(sp):
                sp.dma_start(e1s[:, :], io["src"].rearrange("(p f) -> p f", p=EP1)).then_inc(edges_in, 16)
                sp.dma_start(e1d[:, :], io["dst"].rearrange("(p f) -> p f", p=EP1)).then_inc(edges_in, 16)
                sp.dma_start(e2s[:, :], io["edges"][0].rearrange("(p f) -> p f", p=P)).then_inc(edges_in, 16)
                sp.dma_start(e2d[:, :], io["edges"][1].rearrange("(p f) -> p f", p=P)).then_inc(edges_in, 16)
                sp.wait_ge(step, end["total"])
                sp.dma_start(io["keys"].rearrange("(p f) -> p f", p=P), keys[end["at"]][:, :].bitcast(I32)).then_inc(stored, 16)
                sp.wait_ge(stored, 16)


def index_edges(nc, io, g):
    with ExitStack() as stack:
        m = Memory(nc, stack, "index")
        rows = m.sbuf("nat", [P, F], I32)
        col = m.sbuf("col", [P, F], I32)
        tmp = m.sbuf("tmp", [P, F], I32)
        nodef = m.sbuf("nodef", [P, F])
        ends = m.sbuf("ends", [1, 2, F], I32)
        endf = m.sbuf("endf", [1, 2, F])
        cont = m.sbuf("cont", [1, F])
        loaded, turned, s = m.sem("loaded"), m.sem("turned"), m.sem("step")
        spread, taken = m.sem("spread"), m.sem("taken")
        at = {}
        with nc.Block() as block:
            @block.vector
            def _(dve):
                n = [0]

                def did(ins):
                    n[0] += 1
                    ins.then_inc(s, 1)
                    dve.wait_ge(s, n[0])

                dve.wait_ge(loaded, 48)
                for q in range(4):
                    dve.wait_ge(turned, q + 1)
                    out = col[:, :].bitcast(F32).rearrange("e (p r) -> e r p", r=F // P)[:, 4 * q:4 * q + 4, :]
                    ins = dve.tensor_copy(out, g.bank[q][:, :].rearrange("e (r p) -> e r p", r=4))
                    ins.then_inc(taken, 1)
                dve.wait_ge(taken, 4)
                did(dve.tensor_scalar(tmp[:, :], col[:, :], MASK, None, ALU.bitwise_and))
                did(dve.tensor_scalar(col[:, :], col[:, :], SB, MASK, ALU.logical_shift_right, ALU.bitwise_and))
                did(dve.tensor_tensor(tmp[:, :], tmp[:, :], col[:, :], ALU.add))
                did(dve.tensor_scalar(tmp[:, :], tmp[:, :], MASK, None, ALU.bitwise_and))
                did(dve.tensor_scalar(g.src[:, :], tmp[:, 0:CH], float(N_NODES - 1), None, ALU.min))
                did(dve.tensor_copy(nodef[:, :], col[:, :]))
                did(dve.tensor_scalar(ends[:, :, :], ends[:, :, :], SB, MASK, ALU.logical_shift_right, ALU.bitwise_and))
                did(dve.tensor_copy(endf[:, :, :], ends[:, :, :]))
                did(dve.memset(cont[:, 0:1], 0.0))
                did(dve.tensor_tensor(cont[:, 1:F], endf[:, 0, 1:F], endf[:, 1, 0:F - 1], ALU.is_equal))
                did(dve.memset(g.cont_low[:, 0:1], LOW))
                did(dve.tensor_tensor(endf[:, 0, 1:F], endf[:, 1, 1:F], endf[:, 1, 0:F - 1], ALU.not_equal))
                did(dve.tensor_scalar(g.same_low[:, 1:CH], endf[:, 0, 1:CH], LOW, None, ALU.mult))
                did(dve.memset(g.same_low[:, 0:1], LOW))
                did(dve.tensor_scalar(g.cont_low[:, 1:CH], cont[:, 1:CH], -LOW, LOW, ALU.mult, ALU.add))
                did(dve.tensor_scalar(g.base[:, :], ends[:, 0, 0:CH], float(NPAD), None, ALU.min))
                did(dve.tensor_copy(endf[:, 0, 0:CH], g.base[:, :]))
                at.update(flags=n[0])
                for q in range(4):
                    w = min(512, CH - q * 512)
                    dve.wait_ge(spread, q + 1)
                    dve.tensor_tensor(g.rel[:, q * 512:q * 512 + w], nodef[:, q * 512:q * 512 + w], g.bank[q][:, 0:w], ALU.subtract).then_inc(taken, 1)
                for q in range(-(-C1 // 512)):
                    w = min(512, C1 - q * 512)
                    dve.wait_ge(spread, q + 5)
                    dve.tensor_copy(g.keep[:, q * 512:q * 512 + w], g.bank[q][:, 0:w]).then_inc(taken, 1)

            @block.sync
            def _(sp):
                sp.dma_start(rows[:, :], io["keys"].rearrange("(p f) -> p f", p=P)).then_inc(loaded, 16)
                chunks = io["keys"].rearrange("(c e) -> c e", e=P)
                with nc.allow_non_contiguous_dma(reason="one key of each chunk"):
                    sp.dma_start(ends[:, 0, :], chunks[:, 0:1].rearrange("c e -> e c")).then_inc(loaded, 16)
                    sp.dma_start(ends[:, 1, :], chunks[:, P - 1:P].rearrange("c e -> e c")).then_inc(loaded, 16)

            @block.tensor
            def _(pe):
                pe.wait_ge(loaded, 48)
                natf = rows[:, :].bitcast(F32)
                for q in range(4):
                    for r in range(4):
                        c = (4 * q + r) * P
                        last = nc.tensor.transpose(g.bank[q][:, r * P:(r + 1) * P], natf[:, c:c + P], g.ident[:, :])
                    last.then_inc(turned, 1)
                pe.wait_ge(s, at["flags"])
                for q in range(4):
                    pe.wait_ge(taken, 4 + q)
                    nc.tensor.matmul(g.bank[q][:, :], g.ones[0:1, :], endf[0:1, 0, q * 512:(q + 1) * 512], start=True, stop=True).then_inc(spread, 1)
                for q in range(-(-C1 // 512)):
                    pe.wait_ge(taken, 8 + q)
                    nc.tensor.matmul(g.bank[q][:, :], g.ones[0:1, :], cont[0:1, q * 512:(q + 1) * 512], start=True, stop=True).then_inc(spread, 1)


def running_lows(nc, io, g, c0, n_chunks, H):
    nb, HP = n_chunks // B, B * H
    with ExitStack() as stack:
        m = Memory(nc, stack, f"low{g.lows}")
        g.lows += 1
        krow = m.sbuf("krow", [HP, nb, P], I32)
        krowf = m.sbuf("krowf", [HP, nb, P])
        other = m.sbuf("other", [HP, nb, P])
        delta = m.sbuf("delta", [HP, nb, P], I32)
        key_in, s = m.sem("key_in"), m.sem("step")
        with nc.Block() as block:
            @block.sync
            def _(sp):
                keys_of = io["keys"][c0 * P:(c0 + n_chunks) * P].rearrange("(b j e) -> j b e", j=B, e=P)
                for h in range(H):
                    sp.dma_start(krow[h:HP:H, :, :], keys_of).then_inc(key_in, 16)
            @block.vector
            def _(dve):
                n = [0]

                def did(ins):
                    n[0] += 1
                    ins.then_inc(s, 1)
                    dve.wait_ge(s, n[0])

                did(dve.memset(g.low[:, :, :], LOW))
                did(dve.memset(g.low_back[:, :, :], LOW))
                dve.wait_ge(key_in, 16 * H)
                did(dve.tensor_scalar(delta[:, :, :], krow[:, :, :], MASK, None, ALU.bitwise_and))
                did(dve.tensor_scalar(g.low_own[:, :, :], delta[:, :, :], 0.0, LOW, ALU.not_equal, ALU.mult))
                did(dve.tensor_scalar(krow[:, :, :], krow[:, :, :], SB, MASK, ALU.logical_shift_right, ALU.bitwise_and))
                did(dve.tensor_copy(krowf[:, :, :], krow[:, :, :]))
                did(dve.tensor_tensor(other[:, :, 1:P], krowf[:, :, 1:P], krowf[:, :, 0:P - 1], ALU.not_equal))
                did(dve.tensor_scalar(g.low[:, :, 1:P], other[:, :, 1:P], LOW, None, ALU.mult))
                did(dve.tensor_scalar(g.low_back[:, :, 1:P][:, :, ::-1], other[:, :, 1:P], LOW, None, ALU.mult))
                did(dve.tensor_tensor(other[:, :, :], krowf[:, :, :], krowf[:, :, 0:1].broadcast_to([HP, nb, P]), ALU.not_equal))
                did(dve.tensor_scalar(g.low0[:, :, :], other[:, :, :], LOW, None, ALU.mult))


class WindowStarts:

    def __init__(self, eng, g):
        self.eng, self.base, self.regs, self.loads, self.name = eng, g.base, [], 0, g.passes

    def of(self, chunk, j):
        if j % 8 == 0:
            for r in self.regs:
                self.eng.free_register(r)
            self.loads += 1
            self.regs = [self.eng.alloc_register(f"window{self.name}_{self.loads}_{i}") for i in range(8)]
            self.eng.load(self.regs, self.base[0:1, bass.ds(chunk, 8)])
        return bass.RuntimeValue.of_register_unchecked(self.regs[j % 8], min_val=0, max_val=NPAD)


def gather_pass(nc, io, g, kind, table, c0, n_chunks):
    soft = kind != "gcn"
    H = HEADS if kind == "router" else 1
    HP = B * H
    W = table.shape[1]
    blocks = {"gcn": 1, "gat": 3, "router": 1}[kind]
    OUT = HEADS * NE + HEADS if kind == "router" else P
    score = {"gat": D, "router": HEADS * NE}.get(kind)
    nb = n_chunks // B
    with ExitStack() as stack:
        m = Memory(nc, stack, kind + str(g.passes))
        g.passes += 1
        rows = m.sbuf("rows", [P, 2, B, W])
        index = m.sbuf("index", [P, 2, B], I32)
        rel = m.sbuf("rel_now", [P, 2, B])
        keep = m.sbuf("keep_now", [P, 2, B])
        onehot = m.sbuf("onehot", [P, 4, P])
        first_col = m.sbuf("first_col", [P, 8, blocks])
        idx_set = m.sem("index_set")
        gathered = [m.sem(f"gathered{i}") for i in (0, 1)]
        oh = m.sem("onehot_made")
        summed = m.sem("summed")
        moved = m.sem("moved")
        fixed = m.sem("fixed")
        ready = m.sem("batch_ready")
        if soft:
            low, low_back, low0, low_own = g.low, g.low_back, g.low0, g.low_own
            fwd = m.sbuf("fwd", [P, 2, P])
            top = m.sbuf("top", [HP, P])
            own = m.sbuf("own", [HP, P])
            zz = m.sbuf("zz", [HP, 2, P + 1])
            zl = m.sbuf("zl", [HP, 2, P + 1])
            diff = m.sbuf("diff", [HP, P + 1])
            wrow = m.sbuf("wrow", [P, P + 1])
            wcol = m.sbuf("wcol", [P, 2, HP])
            state = m.sbuf("state", [1, 2, B + 1, H])
            carry = m.sbuf("carry", [1, 2, P])
            cin = m.sbuf("cin", [HP, 2])
            spread = m.sbuf("spread", [P, OUT])
            select = m.sbuf("select", [HP, OUT])
            d2p, p2d = m.sem("dve_to_pe"), m.sem("pe_to_dve")
            d2a, exped = m.sem("dve_to_act"), m.sem("exped")
            if kind == "router":
                pay = m.sbuf("pay", [P, 2, B, OUT])
                els = m.sbuf("els", [P, 2, HP])
        acc = g.acc
        row_ap = table[:, :]
        work = kind == "router"
        if work:
            xt = m.sbuf("xt", [P, 3, 2, 2, P])
            w1 = m.sbuf("w1", [P, 2, FH])
            w2 = m.sbuf("w2", [P, FT, D])
            b1 = m.sbuf("b1", [P, FT])
            b2 = m.sbuf("b2", [P, NE, D])
            zero = m.sbuf("zero", [P, 2 * D], BF16)
            hidden = m.sbuf("hidden", [P, 2, 2 * P])
            mine = m.sbuf("mine", [P, 2, 2, D])
            w_in, zeroed, xt_in = m.sem("w_in"), m.sem("zeroed"), [m.sem(f"xt_in{i}") for i in range(3)]
            h_made, h_ready, h_used = m.sem("h_made"), m.sem("h_ready"), m.sem("h_used")
            mine_ready, stored = m.sem("mine_ready"), [m.sem(f"stored{i}") for i in (0, 1)]
            FE = FT // NE
            QUADS, QU = nb // 4, 3 * FT // 4
            assert nb % 4 == 2 and PAIRS == 3 * QUADS + 1

            def blocks_at(r, tail):
                n = FT // 2 if tail else QU
                return {k * B // n: (r * n + k) for k in range(n)}

        def chunk(b, j):
            return b * B + j

        SCORES_AT = 17
        PD = 4 if kind == "router" else 3

        def after(it, s):
            return (it, 1) if s == 0 else (it + 1, 0)

        def batches(eng, first, body):
            first()
            if work:
                with eng.Fori(0, QUADS) as quad:
                    for r in range(4):
                        body(quad * 2 + r // 2, r % 2, False, (quad, r, False))
                body(nb // 2 - 1, 0, False, (QUADS, 0, True))
                body(nb // 2 - 1, 1, True, (QUADS, 1, True))
            else:
                with eng.Fori(0, nb // 2 - 1) as it:
                    for s in (0, 1):
                        body(it, s, False, None)
                body(nb // 2 - 1, 0, False, None)
                body(nb // 2 - 1, 1, True, None)

        with nc.Block() as block:
            @block.gpsimd
            def _(pool):
                with pool.Fori(0, nb // 2) as it:
                    for s in (0, 1):
                        b = it * 2 + s
                        for q in range(B // RQ):
                            wait_alone(pool, g, summed, b * B + (q + 1) * RQ)
                            if q == 0:
                                pool.tensor_copy(index[:, s, :], g.src[:, bass.ds(b * B + c0, B)]).then_inc(idx_set, 1)
                                wait_alone(pool, g, idx_set, b + 1)
                            for j in range(q * RQ, (q + 1) * RQ):
                                pool.indirect_dma_start(rows[:, s, j, :], None, row_ap,
                                                        bass.IndirectOffsetOnAxis(index[:, s, j:j + 1], 0)).then_inc(gathered[s], 16)

            if work:
                @block.sync
                def _(sp):
                    for c in (0, 1):
                        sp.dma_start(w1[:, c, :], io["t_W1"][c * P:(c + 1) * P, :]).then_inc(w_in, 16)
                    sp.dma_start(w2[:, :, :], io["t_W2"].rearrange("e h d -> (e h) d").rearrange("(f p) d -> p f d", p=P)).then_inc(w_in, 16)
                    sp.dma_start(b1[:, :], io["t_b1"]).then_inc(w_in, 16)
                    sp.dma_start(b2[:, :, :].rearrange("p e d -> p (e d)"), io["t_b2"].rearrange("e d -> (e d)").partition_broadcast(P)).then_inc(w_in, 16)
                    for i in (0, 1):
                        sp.nop().then_inc(stored[i], 16)

                    def load(tile, s):
                        sp.dma_start(xt[:, s].rearrange("p t c n -> p (t c n)"), io["xt"][:, bass.ds(tile * (2 * P), 4 * P)]).then_inc(xt_in[s], 16)

                    def pair(three, p, tile, next_tile):
                        if next_tile is not None:
                            sp.wait_ge(h_made, (three * 3 + p) * FT + 1)
                            load(next_tile, (p + 1) % 3)
                        for e in range(NE):
                            sp.wait_ge(mine_ready, (three * 3 + p) * NE + e + 2)
                            sp.dma_start(io["expert_out"][e].rearrange("(t p) d -> p t d", p=P)[:, bass.ds(tile, 2), :], mine[:, e % 2]).then_inc(stored[e % 2], 16)

                    tile_of = lambda n: min(2 * n, NT - 2)
                    load(0, 0)
                    with sp.Fori(0, QUADS - 1) as three:
                        for p in range(3):
                            pair(three, p, (three * 3 + p) * 2, (three * 3 + p + 1) * 2)
                    for n in range(3 * (QUADS - 1), PAIRS):
                        pair(n // 3, n % 3, tile_of(n), tile_of(n + 1) if n + 1 < PAIRS else None)
                    for i in (0, 1):
                        sp.wait_ge(stored[i], 16 + 16 * NE // 2 * PAIRS)

            @block.vector
            def _(dve):
                if work:
                    dve.memset(zero[:, :], 0.0).then_inc(zeroed, 1)
                if soft:
                    dve.memset(state[:, :, 0:1, :], LOW)
                    for t in (fwd[:, :, :], wrow[:, :], spread[:, :], carry[:, :, :]):
                        dve.memset(t, 0.0)
                    dve.drain()

                def ap(t, b):
                    return t[:, bass.ds(b, 1), :].rearrange("q b e -> q (b e)")

                def scores_by_column(it, s):
                    dve.wait_ge(gathered[s], (it + 1) * (16 * B))
                    for k in (0, 1):
                        last = dve.tensor_copy(els[:, k, :].rearrange("p (j h) -> p j h", h=H), rows[:, s, :, score + k * H:score + (k + 1) * H])
                    last.then_inc(d2p, 1)

                el, er = g.bank[4][0:HP, 0:P], g.bank[4][0:HP, P:2 * P]

                def maxima(it, s):
                    b = it * 2 + s
                    dve.wait_ge(p2d, b * 4 + 1)
                    dve.tensor_tensor(own[:, :], er, ap(low_own, b), ALU.add)
                    dve.tensor_tensor_scan(fwd[0:HP, 0, :], ap(low, b), el, LOW, ALU.add, ALU.max)
                    dve.drain()
                    dve.tensor_tensor_scan(fwd[0:HP, 1, :], ap(low, b), own[:, :], LOW, ALU.add, ALU.max).then_inc(d2p, 1)
                    dve.tensor_tensor_scan(top[:, ::-1], ap(low_back, b), fwd[0:HP, 0, ::-1], LOW, ALU.add, ALU.max)

                def carried(it, s):
                    b = it * 2 + s
                    dve.wait_ge(p2d, b * 4 + 2)
                    same = g.same_low[0:1, bass.ds(b * B + c0, B)]
                    for k in (0, 1):
                        lasts = g.bank[6][0:1, k * HP:(k + 1) * HP].rearrange("o (j h) -> o j h", h=H)
                        for h in range(H):
                            dve.tensor_tensor_scan(state[:, k, 1:, h], same, lasts[:, :, h], state[:, k, 0:1, h], ALU.add, ALU.max)
                    dve.drain()
                    cont = g.cont_low[0:1, bass.ds(b * B + c0, B)].unsqueeze(2).broadcast_to([1, B, H])
                    for k in (0, 1):
                        last = dve.tensor_tensor(carry[:, k, 0:HP].rearrange("o (j h) -> o j h", h=H), state[:, k, 0:B, :], cont, ALU.add)
                    last.then_inc(d2p, 1)
                    dve.drain()
                    dve.tensor_copy(state[:, :, 0, :], state[:, :, B, :])

                def exponents(it, s):
                    b = it * 2 + s
                    dve.wait_ge(p2d, b * 4 + 3)
                    dve.tensor_copy(cin[:, :], g.bank[6][0:HP, 256:258])
                    dve.drain()
                    dve.scalar_tensor_tensor(out=own[:, :], in0=ap(low0, b), scalar=cin[:, 1:2], in1=fwd[0:HP, 1, :], op0=ALU.add, op1=ALU.max)
                    dve.scalar_tensor_tensor(out=top[:, :], in0=ap(low0, b), scalar=cin[:, 0:1], in1=top[:, :], op0=ALU.add, op1=ALU.max)
                    dve.drain()
                    dve.tensor_tensor(zz[:, 0, 0:P], el, own[:, :], ALU.add)
                    dve.tensor_tensor(zz[:, 0, P:P + 1], cin[:, 0:1], own[:, 0:1], ALU.add)
                    dve.tensor_tensor(zz[:, 1, 0:P], top[:, :], own[:, :], ALU.add)
                    dve.tensor_tensor(zz[:, 1, P:P + 1], top[:, 0:1], own[:, 0:1], ALU.add)
                    dve.drain()
                    dve.scalar_tensor_tensor(out=zl[:, :, :], in0=zz[:, :, :], scalar=0.2, in1=zz[:, :, :], op0=ALU.mult, op1=ALU.max)
                    dve.drain()
                    dve.tensor_tensor(diff[:, :], zl[:, 0, :], zl[:, 1, :], ALU.subtract).then_inc(d2a, 1)

                def carried_factors(it, s):
                    dve.wait_ge(exped, it * 2 + s + 1)
                    dve.tensor_scalar(spread[0:HP, :], g.select[kind][0:HP, 0:OUT], wrow[0:HP, P:P + 1], None, ALU.mult).then_inc(d2p, 1)

                def weights(it, s):
                    b = it * 2 + s
                    if soft:
                        dve.wait_ge(p2d, b * 4 + 4)
                        dve.tensor_copy(wcol[:, s, :], g.bank[6][:, 0:HP])
                        dve.tensor_copy(keep[0:OUT, s, :], g.bank[6][0:OUT, 128:128 + B])
                    else:
                        dve.tensor_copy(keep[:, s, :], g.keep[:, bass.ds(b * B + c0, B)])
                    dve.tensor_copy(rel[:, s, :], g.rel[:, bass.ds(b * B + c0, B)])
                    dve.drain()

                def payload(it, s):
                    w4 = wcol[:, s, :].rearrange("p (j h) -> p j h", h=H)
                    dve.tensor_tensor(pay[:, s, :, 0:HEADS * NE].rearrange("p j (h x) -> p j h x", h=H),
                                      rows[:, s, :, 0:HEADS * NE].rearrange("p j (h x) -> p j h x", h=H),
                                      w4.unsqueeze(3).broadcast_to([P, B, H, NE]), ALU.mult)
                    dve.tensor_copy(pay[:, s, :, HEADS * NE:OUT], w4).then_inc(ready, 1)

                steps = {}
                if soft:
                    if kind == "router":
                        steps[SCORES_AT] = scores_by_column
                    for k, step in enumerate((maxima, carried, exponents, carried_factors)):
                        steps[SCORES_AT + 2 + 2 * k] = step
                steps[B - 4] = weights
                if kind == "router":
                    steps[B - 3] = payload

                def first():
                    for j in sorted(steps):
                        steps[j](0, 0)

                starts = WindowStarts(dve, g)

                def fix(it, s, j):
                    c = (it * 2 + s) * B + j
                    at = starts.of(c + c0, j)
                    dve.wait_ge(moved, c + 5)
                    dve.wait_ge(fixed, c + 8)
                    a = acc[0:OUT, 0:blocks, bass.ds(at, 1)].rearrange("p k o -> p (k o)")
                    dve.scalar_tensor_tensor(out=a, in0=a, scalar=keep[0:OUT, s, j:j + 1], in1=first_col[0:OUT, j % 8, :],
                                             op0=ALU.mult, op1=ALU.add).then_inc(fixed, 1)

                def expert_out(three, u):
                    e = u % FT // FE
                    dve.wait_ge(h_used, three * (3 * FT) + u + 3)
                    dve.wait_ge(stored[e % 2], (three * 3 + u // FT) * (8 * NE) + (e // 2 + 1) * 16)
                    dve.tensor_tensor(mine[:, e % 2], g.bank[7][:, :].rearrange("p (t d) -> p t d", d=D),
                                      b2[:, e:e + 1, :].broadcast_to([P, 2, D]), ALU.add).then_inc(mine_ready, 1)

                def body(it, s, last, turn):
                    at_chunk = blocks_at(turn[1], turn[2]) if turn else {}
                    for j in range(B):
                        if not last and j in steps:
                            steps[j](*after(it, s))
                        u = at_chunk.get(j - 2, 0)
                        if u and u % FE == 0:
                            expert_out(turn[0], u - 1)
                        c = (it * 2 + s) * B + j
                        dve.wait_ge(summed, c + 2 * B - 3)
                        if kind == "gat":
                            dve.tensor_scalar(onehot[:, j % 4, :], g.iota[:, :], rel[:, s, j:j + 1], wcol[:, s, j:j + 1], ALU.is_equal, ALU.mult).then_inc(oh, 1)
                        else:
                            dve.tensor_scalar(onehot[:, j % 4, :], g.iota[:, :], rel[:, s, j:j + 1], None, ALU.is_equal).then_inc(oh, 1)
                        if j >= 3:
                            fix(it, s, j - 3)
                    for j in range(B - 3, B):
                        fix(it, s, j)
                    if turn and turn[1] == (1 if turn[2] else 3):
                        expert_out(turn[0], (1 if turn[2] else 3) * FT - 1)

                if work:
                    dve.wait_ge(w_in, 80)
                batches(dve, first, body)

            @block.tensor
            def _(pe):
                pe.nop().then_inc(summed, 2 * B)

                def scores_by_row(it, s):
                    pe.wait_ge(gathered[s], (it + 1) * (16 * B))
                    if kind == "router":
                        pe.wait_ge(d2p, (it * 2 + s) * PD + 1)
                    for k in (0, 1):
                        last = nc.tensor.transpose(g.bank[4][0:HP, k * P:(k + 1) * P],
                                                   els[:, k, :] if kind == "router" else rows[:, s, :, score + k], g.ident[:, :])
                    last.then_inc(p2d, 1)

                def lasts_in_row(it, s):
                    pe.wait_ge(d2p, (it * 2 + s) * PD + PD - 2)
                    for k in (0, 1):
                        last = nc.tensor.matmul(g.bank[6][0:1, k * HP:(k + 1) * HP], fwd[:, k, P - 1:P], g.ident[:, 0:HP], start=True, stop=True)
                    last.then_inc(p2d, 1)

                def carried_in_column(it, s):
                    pe.wait_ge(d2p, (it * 2 + s) * PD + PD - 1)
                    for k in (0, 1):
                        last = nc.tensor.matmul(g.bank[6][:, 256 + k:257 + k], carry[:, k, :], g.ones[0:1, 0:1], start=True, stop=True)
                    last.then_inc(p2d, 1)

                def weights_by_edge(it, s):
                    pe.wait_ge(d2p, (it * 2 + s) * PD + PD)
                    nc.tensor.transpose(g.bank[6][:, 0:P], wrow[:, 0:P], g.ident[:, :])
                    grouping = g.group if kind == "router" else g.ident
                    nc.tensor.matmul(g.bank[6][0:OUT, 128:128 + B], spread[:, :], grouping[:, 0:B], start=True, stop=True).then_inc(p2d, 1)

                steps = {}
                if soft:
                    steps[SCORES_AT + 1] = scores_by_row
                    steps[SCORES_AT + 3] = lasts_in_row
                    steps[SCORES_AT + 5] = carried_in_column
                    steps[SCORES_AT + 9] = weights_by_edge

                def first():
                    for j in sorted(steps):
                        steps[j](0, 0)

                def hidden_units(three, u):
                    f, p = u % FT, u // FT
                    if f == 0:
                        pe.wait_ge(xt_in[p], (three + 1) * 16)
                    pe.wait_ge(h_ready, three * (3 * FT) + u + 1)
                    for c in (0, 1):
                        last = nc.tensor.matmul(g.bank[5][:, 0:2 * P].rearrange("p (t n) -> p t n", n=P), w1[:, c, f * P:(f + 1) * P],
                                                xt[:, p, :, c, :], start=c == 0, stop=c == 1)
                    last.then_inc(h_made, 1)

                def expert_sum(three, u):
                    f = u % FT
                    pe.wait_ge(h_ready, three * (3 * FT) + u + 2)
                    if f % FE == 0:
                        pe.wait_ge(mine_ready, three * (3 * NE) + u // FE + 1)
                        nc.tensor.matmul(g.bank[7][:, :], zero[:, 0:P], zero[:, :], start=True, stop=False)
                    for t in (0, 1):
                        last = nc.tensor.matmul(g.bank[7][:, t * D:(t + 1) * D], hidden[:, f % 2, t * P:(t + 1) * P], w2[:, f, :],
                                                start=False, stop=f % FE == FE - 1 and t == 1)
                    last.then_inc(h_used, 1)

                def body(it, s, last_batch, turn):
                    b = it * 2 + s
                    at_chunk = blocks_at(turn[1], turn[2]) if turn else {}
                    if not soft:
                        pe.wait_ge(gathered[s], (it + 1) * (16 * B))
                    if kind == "router":
                        pe.wait_ge(ready, b + 1)
                    for j in range(B):
                        if not last_batch and j in steps:
                            steps[j](*after(it, s))
                        if j in at_chunk:
                            hidden_units(turn[0], at_chunk[j])
                        if at_chunk.get(j - 1, 0):
                            expert_sum(turn[0], at_chunk[j - 1] - 1)
                        c = b * B + j
                        pe.wait_ge(oh, c + 1)
                        pe.wait_ge(moved, c + 1)
                        out = g.bank[j % 4]
                        if kind == "router":
                            last = nc.tensor.matmul(out[0:OUT, 0:P], pay[:, s, j, :], onehot[:, j % 4, :], start=True, stop=True)
                        else:
                            for k in range(min(blocks, 2)):
                                last = nc.tensor.matmul(out[:, k * P:(k + 1) * P], rows[:, s, j, k * P:(k + 1) * P], onehot[:, j % 4, :], start=True, stop=True)
                            if blocks == 3:
                                last = nc.tensor.matmul(out[:, 2 * P:3 * P], g.ones[:, :], onehot[:, j % 4, :], start=True, stop=True)
                        last.then_inc(summed, 1)
                    if turn and turn[1] == (1 if turn[2] else 3):
                        expert_sum(turn[0], (1 if turn[2] else 3) * FT - 1)

                if work:
                    pe.nop().then_inc(mine_ready, 1)
                    pe.nop().then_inc(h_used, 2)
                    pe.nop().then_inc(h_made, 1)
                    pe.wait_ge(zeroed, 1)
                    pe.wait_ge(w_in, 80)
                batches(pe, first, body)

            @block.scalar
            def _(act):
                act.nop().then_inc(moved, 4)
                act.nop().then_inc(fixed, 8)
                if soft:
                    act.preload_act_table(ACT.Exp)

                def exps(it, s):
                    act.wait_ge(d2a, it * 2 + s + 1)
                    act.activation(wrow[0:HP, :], diff[:, :], ACT.Exp).then_inc(exped, 1)

                steps = {SCORES_AT + 7: exps} if soft else {}

                def first():
                    for j in sorted(steps):
                        steps[j](0, 0)

                starts = WindowStarts(act, g)

                def hidden_gelu(three, u):
                    k, f = three * (3 * FT) + u, u % FT
                    act.wait_ge(h_made, k + 2)
                    act.wait_ge(h_used, k + 1)
                    act.activation(hidden[:, f % 2, :], g.bank[5][:, 0:2 * P], ACT.Gelu, bias=b1[:, f:f + 1]).then_inc(h_ready, 1)

                if work:
                    act.nop().then_inc(h_ready, 1)
                    act.wait_ge(w_in, 80)

                def body(it, s, last, turn):
                    at_chunk = blocks_at(turn[1], turn[2]) if turn else {}
                    for j in range(B):
                        if not last and j in steps:
                            steps[j](*after(it, s))
                        if j - 1 in at_chunk:
                            hidden_gelu(turn[0], at_chunk[j - 1])
                        c = (it * 2 + s) * B + j
                        at = starts.of(c + c0, j)
                        act.wait_ge(summed, c + 2 * B + 1)
                        act.wait_ge(fixed, c + 1)
                        src = g.bank[j % 4][0:OUT, 0:blocks * P].rearrange("p (k n) -> p k n", k=blocks)
                        act.activation(first_col[0:OUT, j % 8, :], src[:, :, 0], ACT.Copy)
                        act.wait_ge(moved, c + 4)
                        act.activation(acc[0:OUT, 0:blocks, bass.ds(at + 1, P - 1)], src[:, :, 1:P], ACT.Copy).then_inc(moved, 1)

                batches(act, first, body)


def groups(eng, body):
    with eng.Fori(0, NG // 2) as it:
        for s in (0, 1):
            body(it, s, False)
    body(NG // 2, 0, True)


class Normaliser:

    def __init__(self, m):
        self.parts = m.sbuf("ln_parts", [P, G, 6])
        self.mv = m.sbuf("ln_mv", [P, G, 2])
        self.var = m.sbuf("ln_var", [P, G])
        self.root = m.sbuf("ln_root", [P, G])
        self.inv = m.sbuf("ln_inv", [P, G])
        self.tmp = m.sbuf("ln_tmp", [P, G])
        self.var_ready, self.root_ready = m.sem("var_ready"), m.sem("root_ready")

    def vector(self, dve, x, out, gi, done):
        for t in range(G):
            dve.bn_stats(self.parts[:, t, :], x[:, t, :])
        dve.drain()
        for t in range(G):
            dve.bn_aggr(self.mv[:, t, :], self.parts[:, t, :])
        dve.drain()
        dve.tensor_scalar(self.var[:, :], self.mv[:, :, 1], EPS, None, ALU.add).then_inc(self.var_ready, 1)
        dve.drain()
        dve.wait_ge(self.root_ready, gi + 1)
        newton(dve, self.var[:, :], self.root[:, :], self.inv[:, :], self.tmp[:, :])
        for t in range(G):
            last = dve.tensor_scalar(out[:, t, :], x[:, t, :], self.mv[:, t, 0:1], self.inv[:, t:t + 1], ALU.subtract, ALU.mult)
        last.then_inc(done, 1)

    def scalar(self, act, gi):
        act.wait_ge(self.var_ready, gi + 1)
        act.activation(self.root[:, :], self.var[:, :], ACT.Sqrt).then_inc(self.root_ready, 1)


def newton(dve, var, root, inv, tmp):
    dve.reciprocal(inv, root)
    dve.drain()
    dve.tensor_tensor(tmp, inv, inv, ALU.mult)
    dve.drain()
    dve.tensor_tensor(tmp, tmp, var, ALU.mult)
    dve.drain()
    dve.tensor_scalar(tmp, tmp, -0.5, 1.5, ALU.mult, ALU.add)
    dve.drain()
    dve.tensor_tensor(inv, inv, tmp, ALU.mult)
    dve.drain()


def turn(nc, g, x, turned):
    for i in range(2 * G):
        t, c = divmod(i, 2)
        last = nc.tensor.transpose(g.bank[i // 4][:, i % 4 * P:(i % 4 + 1) * P], x[:, t, c * P:(c + 1) * P], g.ident[:, :])
        if i % 4 == 3 or i == 2 * G - 1:
            last.then_inc(turned, 1)


def turned_copies(act, g, out, turned, before, done):
    flat = out.rearrange("p t c n -> p (t c n)")
    for q in range(4):
        w = min(512, 2 * G * P - q * 512)
        act.wait_ge(turned, before + q + 1)
        last = act.activation(flat[:, q * 512:q * 512 + w], g.bank[q][:, 0:w], ACT.Copy)
    last.then_inc(done, 1)


def project(nc, io, g, kind):
    from_acc = kind in ("gat1", "router")
    loads_x = kind != "gat1"
    H = HEADS if kind == "router" else 1
    M = {"gcn": HID, "gat0": D, "gat1": D, "router": HEADS * NE}[kind]
    OUT = M if kind == "gcn" else M + 2 * H
    table = io["table_" + {"gcn": "gcn", "router": "router"}.get(kind, "gat")]
    TW = table.shape[1]
    x_rows = {"gcn": io["x"], "gat0": io["res"], "router": io["res"]}.get(kind)
    layer = {"gat0": 0, "gat1": 1}.get(kind)
    with ExitStack() as stack:
        m = Memory(nc, stack, "project_" + kind)
        if loads_x:
            x = m.sbuf("x", [P, 2, G, D])
            xn = m.sbuf("xn", [P, G, D])
            norm = Normaliser(m)
        xt = m.sbuf("xt", [P, 2, G, 2, P])
        wt = m.sbuf("wt", [P, 2, OUT])
        trow = m.sbuf("trow", [P, 2, G, TW])
        w_in, w_done, x_in = m.sem("w_in"), m.sem("w_done"), [m.sem(f"x_in{i}") for i in (0, 1)]
        xn_ready, turned, xt_ready = m.sem("xn_ready"), m.sem("turned"), m.sem("xt_ready")
        made, taken, stored = m.sem("made"), m.sem("taken"), [m.sem(f"stored{i}") for i in (0, 1)]
        stores = 48 if kind == "router" else 16
        loads = 1
        if kind == "gcn":
            dn = m.sbuf("dn", [P, 2, G])
        else:
            att = m.sbuf("att", [P, 2, M])
            prod = m.sbuf("prod", [P, 2, M])
            loads = 3
        if from_acc:
            inv_den = m.sbuf("inv_den", [P, G * P])
            ot = m.sbuf("ot", [P, 2, G * P])
            bias = m.sbuf("bias", [P, 2])
            scaled, ot_ready, back, out_ready = m.sem("scaled"), m.sem("ot_ready"), m.sem("back"), m.sem("out_ready")
            loads = 5

        with nc.Block() as block:
            @block.sync
            def _(sp):
                w = {"gcn": io["W_conv"], "router": io["W_gat"]}.get(kind)
                w = io["W"][layer] if w is None else w
                sp.dma_start(wt[:, :, 0:M], w.rearrange("(c p) n -> p c n", p=P)).then_inc(w_in, 16)
                if kind != "gcn":
                    al, ar = (io["att_src"], io["att_dst"]) if kind == "router" else (io["attn_l"][layer], io["attn_r"][layer])
                    flat = (lambda a: a.rearrange("h x -> (h x)")) if kind == "router" else (lambda a: a)
                    sp.dma_start(att[:, 0, :], flat(al).partition_broadcast(P)).then_inc(w_in, 16)
                    sp.dma_start(att[:, 1, :], flat(ar).partition_broadcast(P)).then_inc(w_in, 16)
                if from_acc:
                    b = io["bias"][1 if kind == "router" else 0]
                    for c in (0, 1):
                        sp.dma_start(bias[:, c:c + 1], b[c * P:(c + 1) * P].rearrange("(p o) -> p o", o=1)).then_inc(w_in, 16)
                for i in (0, 1):
                    sp.nop().then_inc(stored[i], stores)

                def load(gi, s):
                    rows = x_rows.rearrange("(t p) d -> p t d", p=P)
                    sp.dma_start(x[:, s], rows[:, bass.ds(gi * G, G), :]).then_inc(x_in[s], 16)

                def body(it, s, last):
                    gi = it * 2 + s
                    if loads_x and not last:
                        sp.wait_ge(stored[1 - s], (it + s + 1) * stores)
                        load(gi + 1, 1 - s)
                    if kind == "router":
                        sp.wait_ge(out_ready, gi + 1)
                        rows = io["res2"].rearrange("(t p) d -> p t d", p=P)
                        sp.dma_start(rows[:, bass.ds(gi * G, G), :], x[:, s]).then_inc(stored[s], 16)
                        sp.wait_ge(xt_ready, gi + 2)
                        sp.dma_start(io["xt"][:, bass.ds(gi * (2 * G * P), 2 * G * P)], xt[:, s].rearrange("p t c n -> p (t c n)")).then_inc(stored[s], 16)
                    sp.wait_ge(taken, gi * G + G + 4)
                    rows = table.rearrange("(t p) w -> p t w", p=P)
                    sp.dma_start(rows[:, bass.ds(gi * G, G), :], trow[:, s]).then_inc(stored[s], 16)

                if loads_x:
                    load(0, 0)
                groups(sp, body)
                for i in (0, 1):
                    sp.wait_ge(stored[i], (NG // 2 + 1 + (1 - i)) * stores)

            @block.vector
            def _(dve):
                dve.memset(trow[:, :, :, :], 0.0)
                dve.wait_ge(w_in, 16 * loads)
                if kind in ("gat0", "gat1"):
                    for side in (0, 1):
                        for c in (0, 1):
                            dve.tensor_tensor_reduce(out=prod[:, c, :], in0=wt[:, c, 0:M], in1=att[:, side, :], scale=1.0, scalar=0.0,
                                                     op0=ALU.mult, op1=ALU.add, accum_out=wt[:, c, M + side:M + side + 1])
                            dve.drain()
                if kind == "router":
                    for side in (0, 1):
                        dve.tensor_tensor(prod[:, :, :], wt[:, :, 0:M], att[:, side:side + 1, :].broadcast_to([P, 2, M]), ALU.mult)
                        dve.drain()
                        dve.tensor_reduce(wt[:, :, M + side * H:M + (side + 1) * H], prod[:, :, :].rearrange("p c (h x) -> p c h x", x=NE), AX, ALU.add)
                        dve.drain()
                dve.drain()
                dve.nop().then_inc(w_done, 1)

                def body(it, s, last):
                    gi = it * 2 + s
                    dve.wait_ge(xt_ready, gi + 1)
                    if kind == "gcn":
                        dve.tensor_copy(dn[:, s, :], g.dinv[:, bass.ds(gi * G, G)])
                    if from_acc:
                        nodes = bass.ds(gi * (G * P), G * P)
                        dve.reciprocal(inv_den[:, :], g.acc[:, 2, nodes])
                        dve.drain()
                        for c in (0, 1):
                            ins = dve.tensor_tensor(ot[:, c, :], g.acc[:, c, nodes], inv_den[:, :], ALU.mult)
                        ins.then_inc(scaled, 1)
                    if loads_x:
                        dve.wait_ge(x_in[s], (it + 1) * 16)
                    if kind == "router":
                        for q in range(4):
                            w = min(2, G - 2 * q)
                            dve.wait_ge(back, gi * 4 + q + 1)
                            ins = dve.tensor_tensor(x[:, s, 2 * q:2 * q + w, :], x[:, s, 2 * q:2 * q + w, :],
                                                    g.bank[q][:, 0:w * D].rearrange("p (t d) -> p t d", d=D), ALU.add)
                        ins.then_inc(out_ready, 1)
                        dve.drain()
                    if loads_x:
                        norm.vector(dve, x[:, s], xn, gi, xn_ready)

                groups(dve, body)

            @block.tensor
            def _(pe):
                pe.wait_ge(w_done, 1)

                def body(it, s, last):
                    gi = it * 2 + s
                    if kind == "router":
                        pe.wait_ge(ot_ready, gi + 1)
                        for t in range(G):
                            for c in (0, 1):
                                ins = nc.tensor.transpose(g.bank[t // 2][:, t % 2 * D + c * P:t % 2 * D + (c + 1) * P], ot[:, c, t * P:(t + 1) * P], g.ident[:, :])
                            if t % 2 or t == G - 1:
                                ins.then_inc(back, 1)
                    if loads_x:
                        pe.wait_ge(xn_ready, gi + 1)
                        turn(nc, g, xn, turned)
                    pe.wait_ge(xt_ready, gi + 2)
                    for t in range(G):
                        pe.wait_ge(taken, gi * G + t + 2)
                        for c in (0, 1):
                            ins = nc.tensor.matmul(g.bank[4 + t % 4][:, 0:OUT], xt[:, s, t, c, :], wt[:, c, :], start=c == 0, stop=c == 1)
                        ins.then_inc(made, 1)

                groups(pe, body)

            @block.scalar
            def _(act):
                act.nop().then_inc(taken, 4)
                act.nop().then_inc(xt_ready, 1)
                act.wait_ge(w_done, 1)
                early = kind != "router"

                def body(it, s, last):
                    gi = it * 2 + s
                    if from_acc:
                        act.wait_ge(scaled, gi + 1)
                        for c in (0, 1):
                            if kind == "router":
                                ins = act.activation(ot[:, c, :], ot[:, c, :], ACT.Identity, bias=bias[:, c:c + 1])
                            else:
                                ins = act.activation(xt[:, s, :, c, :], ot[:, c, :].rearrange("p (t n) -> p t n", n=P), ACT.Relu, bias=bias[:, c:c + 1])
                        ins.then_inc(ot_ready if kind == "router" else xt_ready, 1)
                    if loads_x and not early:
                        norm.scalar(act, gi)
                    act.wait_ge(stored[s], (it + 1) * stores)
                    if loads_x:
                        turned_copies(act, g, xt[:, s], turned, gi * 4, xt_ready)
                    for t in range(G):
                        if loads_x and early and t == 3 and not last:
                            norm.scalar(act, gi + 1)
                        act.wait_ge(made, gi * G + t + 1)
                        act.activation(trow[:, s, t, 0:OUT], g.bank[4 + t % 4][:, 0:OUT], ACT.Copy,
                                       scale=dn[:, s, t:t + 1] if kind == "gcn" else 1.0).then_inc(taken, 1)

                if loads_x and early:
                    norm.scalar(act, 0)
                groups(act, body)


def switch_experts(nc, io, g):
    SUBS = ((0, 4), (4, G - 4))
    SUM, TURN, LOGIT, CHOICE, CHOSEN, FILLS = 0, 4, 8, 9, 11, 13
    with ExitStack() as stack:
        m = Memory(nc, stack, "switch")
        x = m.sbuf("x", [P, 2, G, D])
        xt = m.sbuf("xt", [P, 2, G, 2, P])
        w1 = m.sbuf("w1", [P, 2, FH])
        w2 = m.sbuf("w2", [P, FT, D])
        b1 = m.sbuf("b1", [P, FT])
        b2 = m.sbuf("b2", [EXPERTS, D])
        ot = m.sbuf("ot", [P, G * P])
        chosen = m.sbuf("chosen", [P, G, EXPERTS])
        wide = m.sbuf("wide", [P, G, P])
        gate = m.sbuf("gate", [P, 2, G * P])
        chosen_t = m.sbuf("chosen_t", [EXPERTS, 2, G * P])
        zero = m.sbuf("zero", [P, 4 * P], BF16)
        raw = m.sbuf("raw", [P, 4, 4 * P])
        hidden = m.sbuf("hidden", [P, 4, 4 * P])
        norm = Normaliser(m)
        w_in, x_in = m.sem("w_in"), [m.sem(f"x_in{i}") for i in (0, 1)]
        ot_ready, xn_ready, routed = m.sem("ot_ready"), m.sem("xn_ready"), m.sem("routed")
        filled, read = m.sem("front_filled"), m.sem("front_read")
        h_made, h_raw, h_ready, h_used = m.sem("h_made"), m.sem("h_raw"), m.sem("h_ready"), m.sem("h_used")
        x_ready, stored = m.sem("x_ready"), m.sem("stored")
        xn = m.sbuf("xn", [P, G, D])
        wlin = m.sbuf("wlin", [P, D])
        bconv = m.sbuf("bconv", [P, 1])
        bconv_wide = m.sbuf("bconv_wide", [P, P])
        blin = m.sbuf("blin", [P, D])
        rw = m.sbuf("rw", [EXPERTS, D])
        rwt = m.sbuf("rwt", [P, 2, EXPERTS])
        rb = m.sbuf("rb", [P, EXPERTS])
        dn = m.sbuf("dn", [P, G])
        logits = m.sbuf("logits", [P, G, EXPERTS])
        top = m.sbuf("top", [P, G, 8])
        topi = m.sbuf("topi", [P, G, 8], U32)
        best = m.sbuf("best", [P, G])
        own = m.sbuf("own", [P, FT])
        setup = m.sem("setup")

        with nc.Block() as block:
            @block.sync
            def _(sp):
                with nc.allow_non_contiguous_dma(reason="biases by partition"):
                    for c in (0, 1):
                        sp.dma_start(w1[:, c, :], io["s_W1"][c * P:(c + 1) * P, :]).then_inc(w_in, 16)
                    sp.dma_start(w2[:, :, :], io["s_W2"].rearrange("e h d -> (e h) d").rearrange("(f p) d -> p f d", p=P)).then_inc(w_in, 16)
                    sp.dma_start(b1[:, :], io["s_b1"]).then_inc(w_in, 16)
                    sp.dma_start(b2[:, :], io["s_b2"]).then_inc(w_in, 16)
                    sp.dma_start(wlin[:, :], io["W_lin"]).then_inc(w_in, 16)
                    sp.dma_start(bconv[:, :], io["b_conv"].rearrange("(p o) -> p o", o=1)).then_inc(w_in, 16)
                    sp.dma_start(blin[:, :], io["b_lin"].partition_broadcast(P)).then_inc(w_in, 16)
                    sp.dma_start(rw[:, :], io["router_w"]).then_inc(w_in, 16)
                    sp.dma_start(rb[:, :], io["router_b"].partition_broadcast(P)).then_inc(w_in, 16)
                sp.nop().then_inc(stored, 16)

                def load(gi, s):
                    rows = io["x"].rearrange("(t p) d -> p t d", p=P)
                    sp.dma_start(x[:, s], rows[:, bass.ds(gi * G, G), :]).then_inc(x_in[s], 16)

                def body(it, s, last):
                    gi = it * 2 + s
                    if not last:
                        sp.wait_ge(stored, (gi + 1) * 16)
                        load(gi + 1, 1 - s)
                    sp.wait_ge(x_ready, gi + 2)
                    rows = io["res"].rearrange("(t p) d -> p t d", p=P)
                    sp.dma_start(rows[:, bass.ds(gi * G, G), :], x[:, s]).then_inc(stored, 16)

                load(0, 0)
                groups(sp, body)
                sp.wait_ge(stored, (NG + 1) * 16)

            @block.vector
            def _(dve):
                dve.nop().then_inc(x_ready, 1)
                dve.nop().then_inc(h_ready, 4)
                dve.memset(zero[:, :], 0.0)
                dve.drain()
                dve.wait_ge(w_in, 16 * 10)
                dve.tensor_scalar(bconv_wide[:, :], g.ones[:, :], bconv[:, 0:1], None, ALU.mult).then_inc(setup, 1)
                dve.wait_ge(setup, 2)
                dve.tensor_tensor(blin[:, :], blin[:, :], g.bank[0][:, 0:D], ALU.add)
                for c in (0, 1):
                    dve.tensor_copy(rwt[:, c, :], g.bank[1][:, c * EXPERTS:(c + 1) * EXPERTS])
                dve.tensor_scalar(own[0:EH, :], g.iota[0:EH, 0:FT], 2.0, None, ALU.mult)
                dve.tensor_scalar(own[EH:P, :], g.iota[EH:P, 0:FT], 2.0, 1.0, ALU.mult, ALU.add)
                dve.drain()
                dve.nop().then_inc(setup, 1)

                def gcn_added(it, s):
                    gi = it * 2 + s
                    dve.tensor_copy(dn[:, :], g.dinv[:, bass.ds(gi * G, G)])
                    dve.wait_ge(x_in[s], (it + 1) * 16)
                    dve.tensor_tensor(x[:, s], x[:, s], blin[:, :].unsqueeze(1).broadcast_to([P, G, D]), ALU.add)
                    dve.drain()
                    for t in range(G):
                        q = SUM + t // 2
                        if t % 2 == 0:
                            dve.wait_ge(filled, gi * FILLS + q + 1)
                        ins = dve.scalar_tensor_tensor(out=x[:, s, t, :], in0=g.bank[6 + q % 2][:, t % 2 * D:(t % 2 + 1) * D], scalar=dn[:, t:t + 1],
                                                       in1=x[:, s, t, :], op0=ALU.mult, op1=ALU.add)
                        if t % 2 or t == G - 1:
                            ins.then_inc(read, 1)
                    dve.drain()
                    norm.vector(dve, x[:, s], xn, gi, xn_ready)

                def route(it, s):
                    gi = it * 2 + s
                    dve.wait_ge(filled, gi * FILLS + LOGIT + 1)
                    dve.tensor_tensor(logits[:, :, :], g.bank[6 + LOGIT % 2][:, 0:G * EXPERTS].rearrange("p (t e) -> p t e", e=EXPERTS),
                                      rb[:, :].unsqueeze(1).broadcast_to([P, G, EXPERTS]), ALU.add).then_inc(read, 1)
                    dve.drain()
                    for t in range(G):
                        dve.max(out=top[:, t, :], in_=logits[:, t, :])
                    dve.drain()
                    for t in range(G):
                        dve.max_index(out=topi[:, t, :], in_max=top[:, t, :], in_values=logits[:, t, :])
                    dve.drain()
                    dve.tensor_copy(best[:, :], topi[:, :, 0])
                    dve.drain()
                    dve.tensor_tensor(chosen[:, :, :], g.iota[:, 0:EXPERTS].unsqueeze(1).broadcast_to([P, G, EXPERTS]),
                                      best[:, :].unsqueeze(2).broadcast_to([P, G, EXPERTS]), ALU.is_equal)
                    dve.tensor_copy(wide[:, :, :], best[:, :].unsqueeze(2).broadcast_to([P, G, P])).then_inc(routed, 1)

                steps = {3: gcn_added, 8: route}

                def body(it, s, last):
                    gi = it * 2 + s
                    dve.wait_ge(read, (gi + 1) * FILLS + 1)
                    for f in range(FT):
                        if not last and f in steps:
                            steps[f](it if s == 0 else it + 1, 1 - s)
                        for h, (t0, n) in enumerate(SUBS):
                            k = 2 * f + h
                            dve.wait_ge(h_raw, gi * (2 * FT) + k + 5)
                            dve.wait_ge(h_used, gi * (2 * FT) + k + 1)
                            dve.scalar_tensor_tensor(out=hidden[:, k % 4, 0:n * P], in0=gate[:, s, t0 * P:(t0 + n) * P], scalar=own[:, f:f + 1],
                                                     in1=raw[:, k % 4, 0:n * P], op0=ALU.is_equal, op1=ALU.mult).then_inc(h_ready, 1)
                    for q in range(4):
                        w = min(2, G - 2 * q)
                        if q % 2 == 0:
                            dve.wait_ge(h_used, (gi + 1) * (2 * FT) + 3 + q // 2)
                        xs, ps = x[:, s, 2 * q:2 * q + w, :], g.bank[q][:, 0:w * D].rearrange("p (t d) -> p t d", d=D)
                        ins = dve.scalar_tensor_tensor(out=xs, in0=ps, scalar=0.0, in1=xs, op0=ALU.max, op1=ALU.add)
                    ins.then_inc(x_ready, 1)

                gcn_added(0, 0)
                route(0, 0)
                groups(dve, body)

            @block.tensor
            def _(pe):
                pe.nop().then_inc(h_used, 4)
                pe.nop().then_inc(read, 1)
                pe.wait_ge(w_in, 16 * 10)
                pe.wait_ge(setup, 1)
                nc.tensor.matmul(g.bank[0][:, 0:D], bconv_wide[:, :], wlin[:, :], start=True, stop=True)
                for c in (0, 1):
                    last = nc.tensor.transpose(g.bank[1][:, c * EXPERTS:(c + 1) * EXPERTS], rw[:, c * P:(c + 1) * P], g.ident[0:EXPERTS, 0:EXPERTS])
                last.then_inc(setup, 1)
                pe.wait_ge(setup, 3)

                def sums(it, s, q0):
                    gi = it * 2 + s
                    if q0 == 0:
                        pe.wait_ge(ot_ready, gi + 1)
                    for q in (q0, q0 + 1):
                        pe.wait_ge(read, gi * FILLS + (SUM + q if q else 1))
                        for t in range(2 * q, min(2 * q + 2, G)):
                            ins = nc.tensor.matmul(g.bank[6 + (SUM + q) % 2][:, t % 2 * D:(t % 2 + 1) * D], ot[:, t * P:(t + 1) * P], wlin[:, :], start=True, stop=True)
                        ins.then_inc(filled, 1)

                def turns(it, s, q0):
                    gi = it * 2 + s
                    if q0 == 0:
                        pe.wait_ge(xn_ready, gi + 1)
                    for q in (q0, q0 + 1):
                        pe.wait_ge(read, gi * FILLS + TURN + q)
                        for i in range(4 * q, min(4 * q + 4, 2 * G)):
                            t, c = divmod(i, 2)
                            ins = nc.tensor.transpose(g.bank[6 + (TURN + q) % 2][:, i % 4 * P:(i % 4 + 1) * P], xn[:, t, c * P:(c + 1) * P], g.ident[:, :])
                        ins.then_inc(filled, 1)

                def logit(it, s):
                    gi = it * 2 + s
                    pe.wait_ge(read, gi * FILLS + LOGIT + 1)
                    for t in range(G):
                        for c in (0, 1):
                            ins = nc.tensor.matmul(g.bank[6 + LOGIT % 2][:, t * EXPERTS:(t + 1) * EXPERTS], xt[:, s, t, c, :], rwt[:, c, :], start=c == 0, stop=c == 1)
                    ins.then_inc(filled, 1)

                def choices(it, s):
                    gi = it * 2 + s
                    pe.wait_ge(routed, gi + 1)
                    for q, (t0, n) in enumerate(SUBS):
                        pe.wait_ge(read, gi * FILLS + CHOICE + q)
                        for t in range(n):
                            ins = nc.tensor.transpose(g.bank[6 + (CHOICE + q) % 2][:, t * P:(t + 1) * P], wide[:, t0 + t, :], g.ident[:, :])
                        ins.then_inc(filled, 1)

                def chosen_turned(it, s):
                    gi = it * 2 + s
                    for q, (t0, n) in enumerate(SUBS):
                        pe.wait_ge(read, gi * FILLS + CHOSEN + q)
                        for t in range(n):
                            ins = nc.tensor.transpose(g.bank[6 + (CHOSEN + q) % 2][0:EXPERTS, t * P:(t + 1) * P], chosen[:, t0 + t, :], g.ident[:, :])
                        ins.then_inc(filled, 1)

                steps = {1: lambda it, s: sums(it, s, 0), 2: lambda it, s: sums(it, s, 2), 5: lambda it, s: turns(it, s, 0),
                         6: lambda it, s: turns(it, s, 2), 7: logit, 10: choices, 11: chosen_turned}

                def body(it, s, last):
                    gi = it * 2 + s
                    pe.wait_ge(read, (gi + 1) * FILLS + 1)
                    pe.wait_ge(x_ready, gi + 1)
                    for q in range(4):
                        nc.tensor.matmul(g.bank[q][:, :], zero[:, 0:P], zero[:, :], start=True, stop=False)
                    for t in range(G):
                        nc.tensor.matmul(g.bank[t // 2][:, t % 2 * D:(t % 2 + 1) * D], chosen_t[:, s, t * P:(t + 1) * P], b2[:, :], start=False, stop=False)

                    def up(f):
                        for h, (t0, n) in enumerate(SUBS):
                            k = 2 * f + h
                            pe.wait_ge(h_raw, gi * (2 * FT) + k + 3)
                            for c in (0, 1):
                                ins = nc.tensor.matmul(g.bank[4 + k % 2][:, 0:n * P].rearrange("p (t n) -> p t n", n=P), w1[:, c, f * P:(f + 1) * P],
                                                       xt[:, s, t0:t0 + n, c, :], start=c == 0, stop=c == 1)
                            ins.then_inc(h_made, 1)

                    def down(f):
                        for h, (t0, n) in enumerate(SUBS):
                            k = 2 * f + h
                            pe.wait_ge(h_ready, gi * (2 * FT) + k + 5)
                            for t in range(n):
                                ins = nc.tensor.matmul(g.bank[(t0 + t) // 2][:, (t0 + t) % 2 * D:((t0 + t) % 2 + 1) * D], hidden[:, k % 4, t * P:(t + 1) * P],
                                                       w2[:, f, :], start=False, stop=f == FT - 1 and ((t0 + t) % 2 == 1 or t0 + t == G - 1))
                            ins.then_inc(h_used, 1)

                    up(0)
                    for f in range(FT):
                        if not last and f in steps:
                            steps[f](it if s == 0 else it + 1, 1 - s)
                        if f + 1 < FT:
                            up(f + 1)
                        down(f)

                for f in sorted(steps):
                    steps[f](0, 0)
                groups(pe, body)

            @block.scalar
            def _(act):
                act.nop().then_inc(h_raw, 4)
                act.wait_ge(w_in, 16 * 10)

                def sums_of(it, s):
                    act.activation(ot[:, :], g.acc[:, 0, bass.ds((it * 2 + s) * (G * P), G * P)], ACT.Copy).then_inc(ot_ready, 1)

                def root(it, s):
                    norm.scalar(act, it * 2 + s)

                def rows_turned(it, s, q0):
                    flat = xt[:, s].rearrange("p t c n -> p (t c n)")
                    for q in (q0, q0 + 1):
                        w = min(512, 2 * G * P - q * 512)
                        act.wait_ge(filled, (it * 2 + s) * FILLS + TURN + q + 1)
                        ins = act.activation(flat[:, q * 512:q * 512 + w], g.bank[6 + (TURN + q) % 2][:, 0:w], ACT.Copy)
                        ins.then_inc(read, 1)

                def all_turned(it, s):
                    rows_turned(it, s, 2)

                def spread(it, s):
                    for q, (t0, n) in enumerate(SUBS):
                        act.wait_ge(filled, (it * 2 + s) * FILLS + CHOICE + q + 1)
                        act.activation(gate[:, s, t0 * P:(t0 + n) * P], g.bank[6 + (CHOICE + q) % 2][:, 0:n * P], ACT.Copy).then_inc(read, 1)

                def chosen_copied(it, s):
                    for q, (t0, n) in enumerate(SUBS):
                        act.wait_ge(filled, (it * 2 + s) * FILLS + CHOSEN + q + 1)
                        act.activation(chosen_t[:, s, t0 * P:(t0 + n) * P], g.bank[6 + (CHOSEN + q) % 2][0:EXPERTS, 0:n * P], ACT.Copy).then_inc(read, 1)

                steps = {0: sums_of, 3: root, 6: lambda it, s: rows_turned(it, s, 0), 7: all_turned, 11: spread, 12: chosen_copied}

                def body(it, s, last):
                    gi = it * 2 + s
                    for f in range(FT):
                        if not last and f in steps:
                            steps[f](it if s == 0 else it + 1, 1 - s)
                        for h, (t0, n) in enumerate(SUBS):
                            k = 2 * f + h
                            act.wait_ge(h_made, gi * (2 * FT) + k + 1)
                            act.wait_ge(h_ready, gi * (2 * FT) + k + 1)
                            act.activation(raw[:, k % 4, 0:n * P], g.bank[4 + k % 2][:, 0:n * P], ACT.Relu, bias=b1[:, f:f + 1]).then_inc(h_raw, 1)

                for f in sorted(steps):
                    steps[f](0, 0)
                groups(act, body)


def mix_experts(nc, io, g):
    RW = HEADS * NE
    SUBS = ((0, 4), (4, G - 4))
    with ExitStack() as stack:
        m = Memory(nc, stack, "mix")
        x = m.sbuf("x", [P, 2, G, D])
        outs = m.sbuf("outs", [P, 2, NE, G, D])
        ot = m.sbuf("ot", [P, G * P])
        norm = Normaliser(m)
        den = m.sbuf("den", [P, G, HEADS])
        agg = m.sbuf("agg", [P, G, RW])
        aggn = m.sbuf("aggn", [P, G, RW])
        rows3 = m.sbuf("rows3", [P, 3, RW])
        scores = m.sbuf("scores", [P, 2, G, 8])
        top = m.sbuf("top", [P, 2, G, 8])
        topi = m.sbuf("topi", [P, 2, G, 8], U32)
        best = m.sbuf("best", [P, 2, G])
        hot = m.sbuf("hot", [P, 2, G, NE])
        gap, rise = m.sbuf("gap", [P, G]), m.sbuf("rise", [P, G])
        share = m.sbuf("share", [P, 2, G])
        gate = m.sbuf("gate", [P, G, NE])
        w_in, x_in = m.sem("w_in"), [m.sem(f"x_in{i}") for i in (0, 1)]
        ot_ready, sums, normed = m.sem("ot_ready"), m.sem("sums"), m.sem("normed")
        gap_ready, gap_exped = m.sem("gap_ready"), m.sem("gap_exped")
        x_ready, stored = m.sem("x_ready"), m.sem("stored")
        with nc.Block() as block:
            @block.sync
            def _(sp):
                for i, k in enumerate(("b_gat", "ln_gamma", "ln_beta")):
                    sp.dma_start(rows3[:, i, :], io[k].partition_broadcast(P)).then_inc(w_in, 16)
                x_rows = io["res2"].rearrange("(t p) d -> p t d", p=P)
                out_rows = io["out"].rearrange("(t p) d -> p t d", p=P)

                def load(gi, s):
                    tiles = bass.ds(gi * G, G)
                    sp.dma_start(x[:, s], x_rows[:, tiles, :]).then_inc(x_in[s], 16)
                    for e in range(NE):
                        sp.dma_start(outs[:, s, e], io["expert_out"][e].rearrange("(t p) d -> p t d", p=P)[:, tiles, :]).then_inc(x_in[s], 16)

                def body(it, s, last):
                    gi = it * 2 + s
                    if not last:
                        sp.wait_ge(stored, (gi + 1) * 16)
                        load(gi + 1, 1 - s)
                    sp.wait_ge(x_ready, gi + 1)
                    sp.dma_start(out_rows[:, bass.ds(gi * G, G), :], x[:, s]).then_inc(stored, 16)

                sp.nop().then_inc(stored, 16)
                load(0, 0)
                groups(sp, body)
                sp.wait_ge(stored, (NG + 1) * 16)

            @block.vector
            def _(dve):
                dve.memset(scores[:, :, :, :], LOW)
                dve.drain()
                dve.wait_ge(w_in, 48)

                def body(it, s, last):
                    gi = it * 2 + s
                    dve.wait_ge(sums, gi + 1)
                    for q, (t0, n) in enumerate(SUBS):
                        v = g.bank[q][:, 0:n * P].rearrange("p (t k) -> p t k", k=P)
                        dve.tensor_scalar(den[:, t0:t0 + n, :], v[:, :, RW:RW + HEADS], 1e-16, None, ALU.add)
                    dve.drain()
                    dve.reciprocal(den[:, :, :], den[:, :, :])
                    dve.drain()
                    for q, (t0, n) in enumerate(SUBS):
                        for t in range(n):
                            v = g.bank[q][:, t * P:t * P + RW].rearrange("p (h x) -> p h x", x=NE)
                            dve.tensor_tensor(agg[:, t0 + t, :].rearrange("p (h x) -> p h x", x=NE), v,
                                              den[:, t0 + t, :].unsqueeze(2).broadcast_to([P, HEADS, NE]), ALU.mult)
                    dve.drain()
                    r3 = [rows3[:, i:i + 1, :].broadcast_to([P, G, RW]) for i in range(3)]
                    dve.tensor_tensor(agg[:, :, :], agg[:, :, :], r3[0], ALU.add)
                    dve.drain()
                    norm.vector(dve, agg, aggn, gi, normed)
                    dve.drain()
                    dve.tensor_tensor(aggn[:, :, :], aggn[:, :, :], r3[1], ALU.mult)
                    dve.drain()
                    dve.tensor_tensor(aggn[:, :, :], aggn[:, :, :], r3[2], ALU.add)
                    dve.drain()
                    dve.tensor_reduce(scores[:, 0, :, 0:NE], aggn[:, :, :].rearrange("p t (h x) -> p t x h", x=NE), AX, ALU.add)
                    dve.drain()
                    dve.tensor_scalar(scores[:, 0, :, 0:NE], scores[:, 0, :, 0:NE], 1.0 / HEADS, None, ALU.mult)
                    dve.drain()
                    for k in (0, 1):
                        for t in range(G):
                            dve.max(out=top[:, k, t, :], in_=scores[:, k, t, :])
                        dve.drain()
                        for t in range(G):
                            dve.max_index(out=topi[:, k, t, :], in_max=top[:, k, t, :], in_values=scores[:, k, t, :])
                        dve.drain()
                        dve.tensor_copy(best[:, k, :], topi[:, k, :, 0])
                        dve.drain()
                        dve.tensor_tensor(hot[:, k, :, :], g.iota[:, 0:NE].unsqueeze(1).broadcast_to([P, G, NE]),
                                          best[:, k, :].unsqueeze(2).broadcast_to([P, G, NE]), ALU.is_equal)
                        dve.drain()
                        if k == 0:
                            dve.scalar_tensor_tensor(out=scores[:, 1, :, 0:NE], in0=hot[:, 0, :, :], scalar=LOW / 2, in1=scores[:, 0, :, 0:NE], op0=ALU.mult, op1=ALU.add)
                            dve.drain()
                    dve.tensor_tensor(gap[:, :], top[:, 1, :, 0], top[:, 0, :, 0], ALU.subtract).then_inc(gap_ready, 1)
                    dve.wait_ge(gap_exped, gi + 1)
                    dve.tensor_scalar(share[:, 0, :], rise[:, :], 1.0, None, ALU.add)
                    dve.drain()
                    dve.reciprocal(share[:, 0, :], share[:, 0, :])
                    dve.drain()
                    dve.tensor_tensor(share[:, 1, :], share[:, 0, :], rise[:, :], ALU.mult)
                    dve.drain()
                    for k in (0, 1):
                        dve.tensor_tensor(hot[:, k, :, :], hot[:, k, :, :], share[:, k, :].unsqueeze(2).broadcast_to([P, G, NE]), ALU.mult)
                    dve.drain()
                    dve.tensor_tensor(gate[:, :, :], hot[:, 0, :, :], hot[:, 1, :, :], ALU.add)
                    dve.drain()
                    dve.wait_ge(x_in[s], (it + 1) * (16 * (NE + 1)))
                    for e in range(NE):
                        for t in range(G):
                            last_sum = dve.scalar_tensor_tensor(out=x[:, s, t, :], in0=outs[:, s, e, t, :], scalar=gate[:, t, e:e + 1],
                                                                in1=x[:, s, t, :], op0=ALU.mult, op1=ALU.add)
                        if e < NE - 1:
                            dve.drain()
                    last_sum.then_inc(x_ready, 1)

                groups(dve, body)

            @block.tensor
            def _(pe):
                def body(it, s, last):
                    pe.wait_ge(ot_ready, it * 2 + s + 1)
                    for t in range(G):
                        turned = nc.tensor.transpose(g.bank[t // 4][:, t % 4 * P:(t % 4 + 1) * P], ot[:, t * P:(t + 1) * P], g.ident[:, :])
                    turned.then_inc(sums, 1)

                groups(pe, body)

            @block.scalar
            def _(act):
                def body(it, s, last):
                    gi = it * 2 + s
                    act.activation(ot[:, :], g.acc[:, 0, bass.ds(gi * (G * P), G * P)], ACT.Copy).then_inc(ot_ready, 1)
                    norm.scalar(act, gi)
                    act.wait_ge(gap_ready, gi + 1)
                    act.activation(rise[:, :], gap[:, :], ACT.Exp).then_inc(gap_exped, 1)

                groups(act, body)


def make_globals(nc, m, g):
    g.passes = g.lows = g.carried = 0
    g.bank = [m.stack.enter_context(nc.psum_tensor(f"bank{i}", [P, 512], F32)) for i in range(8)]
    g.ident = m.sbuf("ident", [P, P])
    g.ones = m.sbuf("ones", [P, P])
    g.carrier = m.sbuf("carrier", [1, 33])
    g.iota = m.sbuf("iota", [P, P])
    g.group = m.sbuf("group", [P, B])
    g.select_router = m.sbuf("select_router", [P, HEADS * NE + HEADS])
    g.select = {"gat": g.ones, "router": g.select_router}
    g.dinv = m.sbuf("dinv", [P, NT])
    g.src = m.sbuf("src_of", [P, CH], I16)
    g.rel = m.sbuf("rel", [P, CH], BF16)
    g.keep = m.sbuf("keep", [P, C1])
    g.base = m.sbuf("base", [1, CH], I16)
    g.cont_low = m.sbuf("cont_low", [1, CH], BF16)
    g.same_low = m.sbuf("same_low", [1, CH], BF16)
    g.low = g.low_back = g.low0 = g.low_own = None


def zero_sums(nc, g, blocks):
    with nc.Block() as block:
        @block.vector
        def _(dve):
            dve.memset(g.acc[:, 0:(blocks + 1) // 2, :], 0.0)

        @block.gpsimd
        def _(pool):
            if blocks == 3:
                pool.memset(g.acc[:, 2, :], 0.0)


def gnn_ffn(nc, *args):
    io = dict(zip(NAMES + ("out",), args))
    for name, shape, dt in (("keys", (1 << SORT_BITS,), I32), ("table_gcn", (NPAD, HID), F32),
                            ("table_gat", (NPAD, D + 4), F32), ("table_router", (NPAD, HEADS * NE + 2 * HEADS), F32),
                            ("res", (NPAD, D), F32), ("res2", (NPAD, D), F32), ("xt", (P, NT * 2 * P), F32), ("expert_out", (NE, NPAD, D), F32)):
        io[name] = nc.dram_tensor(name, shape, dt, kind="Internal").ap()

    class Shared:
        pass

    g = Shared()
    with ExitStack() as stack:
        m = Memory(nc, stack, "g")
        make_globals(nc, m, g)
        sort_edges(nc, io, g)
        index_edges(nc, io, g)
        with ExitStack() as gcn:
            g.acc = Memory(nc, gcn, "gcn_sums").sbuf("acc", [P, 1, WIN])
            zero_sums(nc, g, 1)
            project(nc, io, g, "gcn")
            gather_pass(nc, io, g, "gcn", io["table_gcn"], 0, C1)
            switch_experts(nc, io, g)
        g.acc = m.sbuf("acc", [P, 3, WIN])
        zero_sums(nc, g, 3)
        with ExitStack() as low:
            ml = Memory(nc, low, "gat_low")
            for layer in (0, 1):
                project(nc, io, g, f"gat{layer}")
                if layer == 1:
                    gather_pass(nc, io, g, "gat", io["table_gat"], 0, C1)
                    continue
                g.low, g.low_back = ml.sbuf("low", [B, C1 // B, P], BF16), ml.sbuf("low_back", [B, C1 // B, P], BF16)
                g.low0, g.low_own = ml.sbuf("low0", [B, C1 // B, P], BF16), ml.sbuf("low_own", [B, C1 // B, P], BF16)
                running_lows(nc, io, g, 0, C1, 1)
                gather_pass(nc, io, g, "gat", io["table_gat"], 0, C1)
        project(nc, io, g, "router")
        with ExitStack() as low:
            ml = Memory(nc, low, "router_low")
            g.low, g.low_back = ml.sbuf("low", [B * HEADS, C2 // B, P], BF16), ml.sbuf("low_back", [B * HEADS, C2 // B, P], BF16)
            g.low0, g.low_own = ml.sbuf("low0", [B * HEADS, C2 // B, P], BF16), ml.sbuf("low_own", [B * HEADS, C2 // B, P], BF16)
            running_lows(nc, io, g, C1, C2, HEADS)
            gather_pass(nc, io, g, "router", io["table_router"], C1, C2)
        mix_experts(nc, io, g)


_INS = ("x", "src", "dst", "L0_gnn_W_conv", "L0_gnn_b_conv", "L0_gnn_W_lin", "L0_gnn_b_lin", "L0_ffn_router_w",
        "L0_ffn_router_b", "L0_ffn_W1", "L0_ffn_b1", "L0_ffn_W2", "L0_ffn_b2", "L1_gnn_W", "L1_gnn_attn_l",
        "L1_gnn_attn_r", "L1_gnn_bias", "L1_ffn_W_gat", "L1_ffn_att_src", "L1_ffn_att_dst", "L1_ffn_b_gat",
        "L1_ffn_ln_gamma", "L1_ffn_ln_beta", "L1_ffn_W1", "L1_ffn_b1", "L1_ffn_W2", "L1_ffn_b2", "L1_ffn_edge_index")
NAMES = ("x", "src", "dst", "W_conv", "b_conv", "W_lin", "b_lin", "router_w", "router_b", "s_W1", "s_b1", "s_W2", "s_b2",
         "W", "attn_l", "attn_r", "bias", "W_gat", "att_src", "att_dst", "b_gat", "ln_gamma", "ln_beta",
         "t_W1", "t_b1", "t_W2", "t_b2", "edges")


def kernel(**inputs):
    import numpy as _np
    import concourse.bacc as _bacc
    from concourse import mybir as _mybir
    from concourse.bass_utils import run_bass_kernel_spmd as _run

    nc = _bacc.Bacc("TRN2", target_bir_lowering=False, num_devices=1)
    arrays, args = {}, []
    for name in _INS:
        a = _np.ascontiguousarray(inputs[name])
        if name == "x":
            a = _np.concatenate([a, _np.zeros((NPAD - a.shape[0], a.shape[1]), a.dtype)])
        elif name.endswith("ffn_W1"):
            a = _np.ascontiguousarray(a.transpose(1, 0, 2).reshape(D, -1))
        elif name.endswith("ffn_b1"):
            a = _np.ascontiguousarray(a.reshape(-1, P).T)
        arrays[f"in_{name}_dram"] = a
        args.append(nc.dram_tensor(f"in_{name}_dram", a.shape, _mybir.dt.from_np(a.dtype), kind="ExternalInput").ap())
    args.append(nc.dram_tensor("out_0_dram", (NPAD, D), F32, kind="ExternalOutput").ap())
    gnn_ffn(nc, *args)
    r = _run(nc, [arrays], core_ids=[0])
    return r.results[0]["out_0_dram"][:N_NODES]
```
